# Optimizing a Trainium2 kernel written in Bass

```python
import numpy as np
import jax
import jax.numpy as jnp

def _softmax(x, axis=-1):
    return jax.nn.softmax(x, axis=axis)

def _gelu(x):
    return jax.nn.gelu(x, approximate=True)

def _silu(x):
    return jax.nn.silu(x)

def _sigmoid(x):
    return jax.nn.sigmoid(x)

def _layernorm(x, axis=-1, eps=1e-05):
    m = jnp.mean(x, axis=axis, keepdims=True)
    v = jnp.var(x, axis=axis, keepdims=True)
    return (x - m) / jnp.sqrt(v + eps)

def _scatter_add(tgt, idx, src, axis=0):
    return tgt.at[idx].add(src)

def _segment_sum(src, seg, n):
    return jax.ops.segment_sum(src, seg, n)
kernel_name = 'mk_decoder_preln_d1_seqx_r2_804d99'

def setup_inputs(seed: int=0):
    np.random.seed(seed)
    _w = jnp.asarray

    def _rec_inputs():
        import jax
        import jax.numpy as jnp
        _rk = jax.random.key(seed)
        x = 7.22e-05 + 1 * jax.random.normal(jax.random.fold_in(_rk, 1), (4, 1024, 512), jnp.float32)
        _lenS = 1024 - jax.random.randint(jax.random.fold_in(_rk, 7), (4,), 0, max(1, 1024 // 4) + 1, jnp.int32)
        _lenS2 = 2048 - jax.random.randint(jax.random.fold_in(_rk, 8), (4,), 0, max(1, 2048 // 4) + 1, jnp.int32)
        _ctx_1024P = jax.random.normal(jax.random.fold_in(_rk, 11), (4, 16, 512), jnp.float32)
        _ctx_1024c = jax.random.dirichlet(jax.random.fold_in(_rk, 511), 0.3 * jnp.ones((16,), jnp.float32), (4, 2048))
        _ctx_1024t = jnp.einsum('bsk,bkd->bsd', _ctx_1024c, _ctx_1024P)
        _ctx_1024t = _ctx_1024t * jax.lax.rsqrt(jnp.mean(jnp.square(_ctx_1024t)) + 1e-12) * 0.953939
        ctx_1024 = 4.13588e-05 + 0.999923 * (_ctx_1024t + 0.3 * jax.random.normal(jax.random.fold_in(_rk, 611), (4, 2048, 512), jnp.float32))
        return (x, ctx_1024)
    x, ctx_1024 = _rec_inputs()

    def _L0_attn_setup():
        import jax, jax.numpy as jnp
        import numpy as np
        D_MODEL = 512
        NUM_HEADS = 16
        DK = D_MODEL // NUM_HEADS
        key = jax.random.key(seed)
        kx, kq, kk, kv, ko = jax.random.split(key, 5)
        B, S = (4, 1024)
        bound = float(np.sqrt(6.0 / (D_MODEL + D_MODEL)))
        uni = lambda k: jax.random.uniform(k, (D_MODEL, D_MODEL), jnp.float32, -bound, bound)
        return {'x': jax.random.normal(kx, (B, S, D_MODEL), jnp.float32), 'q_heads': uni(kq), 'k_heads': uni(kk), 'v_heads': uni(kv), 'output_proj': uni(ko)}
    _L0_attn_all = _L0_attn_setup()
    _L0_attn_in = {k: v for k, v in _L0_attn_all.items() if k in ('q_heads', 'k_heads', 'v_heads', 'output_proj')}
    del _L0_attn_all

    def _L0_xattn_setup():
        import jax, jax.numpy as jnp
        import numpy as np
        EMBED = 512
        HEADS = 16
        HEAD_DIM = EMBED // HEADS
        key = jax.random.key(seed)
        ks = jax.random.split(key, 7)
        B, Sd, Se = (4, 1024, 1024)
        dec = jax.random.normal(ks[0], (B, Sd, EMBED), dtype=jnp.float32)
        enc = jax.random.normal(ks[1], (B, Se, EMBED), dtype=jnp.float32)
        scale = 1.0 / np.sqrt(EMBED)
        W_q = jax.random.normal(ks[2], (EMBED, EMBED), dtype=jnp.float32) * scale
        W_k = jax.random.normal(ks[3], (EMBED, EMBED), dtype=jnp.float32) * scale
        W_v = jax.random.normal(ks[4], (EMBED, EMBED), dtype=jnp.float32) * scale
        W_o = jax.random.normal(ks[5], (EMBED, EMBED), dtype=jnp.float32) * scale
        b_o = jax.random.normal(ks[6], (EMBED,), dtype=jnp.float32) * 0.01
        return {'decoder_input': dec, 'encoder_output': enc, 'W_q': W_q, 'W_k': W_k, 'W_v': W_v, 'W_o': W_o, 'b_o': b_o}
    _L0_xattn_all = _L0_xattn_setup()
    _L0_xattn_in = {k: v for k, v in _L0_xattn_all.items() if k in ('W_q', 'W_k', 'W_v', 'W_o', 'b_o')}
    del _L0_xattn_all

    def _L0_ffn_setup():
        import jax, jax.numpy as jnp
        import numpy as np
        LN_EPS = 1e-05

        def _layernorm(x, g, b):
            m = jnp.mean(x, axis=-1, keepdims=True)
            v = jnp.mean(jnp.square(x - m), axis=-1, keepdims=True)
            return (x - m) * jax.lax.rsqrt(v + LN_EPS) * g + b
        K_TOP = 2
        key = jax.random.key(seed)
        ks = jax.random.split(key, 4)
        B, N, D, E = (8, 1024, 512, 4)
        s = 0.02
        return {'x': jax.random.normal(ks[0], (B, N, D), dtype=jnp.float32), 'gate_W': jax.random.normal(ks[1], (D, E), dtype=jnp.float32) * s, 'gate_b': jnp.zeros((E,), jnp.float32), 'W1': jax.random.normal(ks[2], (E, D, D), dtype=jnp.float32) * s, 'b1': jnp.zeros((E, D), jnp.float32), 'g1': jnp.ones((E, D), jnp.float32), 'be1': jnp.zeros((E, D), jnp.float32), 'W2': jax.random.normal(ks[3], (E, D, D), dtype=jnp.float32) * s, 'b2': jnp.zeros((E, D), jnp.float32), 'g2': jnp.ones((E, D), jnp.float32), 'be2': jnp.zeros((E, D), jnp.float32)}
    _L0_ffn_all = _L0_ffn_setup()
    _L0_ffn_in = {k: v for k, v in _L0_ffn_all.items() if k in ('gate_W', 'gate_b', 'W1', 'b1', 'g1', 'be1', 'W2', 'b2', 'g2', 'be2')}
    del _L0_ffn_all
    return {'x': x, 'ctx_1024': ctx_1024, 'L0_attn_q_heads': _L0_attn_in['q_heads'], 'L0_attn_k_heads': _L0_attn_in['k_heads'], 'L0_attn_v_heads': _L0_attn_in['v_heads'], 'L0_attn_output_proj': _L0_attn_in['output_proj'], 'L0_xattn_W_q': _L0_xattn_in['W_q'], 'L0_xattn_W_k': _L0_xattn_in['W_k'], 'L0_xattn_W_v': _L0_xattn_in['W_v'], 'L0_xattn_W_o': _L0_xattn_in['W_o'], 'L0_xattn_b_o': _L0_xattn_in['b_o'], 'L0_ffn_gate_W': _L0_ffn_in['gate_W'], 'L0_ffn_gate_b': _L0_ffn_in['gate_b'], 'L0_ffn_W1': _L0_ffn_in['W1'], 'L0_ffn_b1': _L0_ffn_in['b1'], 'L0_ffn_g1': _L0_ffn_in['g1'], 'L0_ffn_be1': _L0_ffn_in['be1'], 'L0_ffn_W2': _L0_ffn_in['W2'], 'L0_ffn_b2': _L0_ffn_in['b2'], 'L0_ffn_g2': _L0_ffn_in['g2'], 'L0_ffn_be2': _L0_ffn_in['be2']}

def reference(x, ctx_1024, L0_attn_q_heads, L0_attn_k_heads, L0_attn_v_heads, L0_attn_output_proj, L0_xattn_W_q, L0_xattn_W_k, L0_xattn_W_v, L0_xattn_W_o, L0_xattn_b_o, L0_ffn_gate_W, L0_ffn_gate_b, L0_ffn_W1, L0_ffn_b1, L0_ffn_g1, L0_ffn_be1, L0_ffn_W2, L0_ffn_b2, L0_ffn_g2, L0_ffn_be2):
    import jax
    import jax.numpy as jnp

    def _L0_attn_ref(x, q_heads, k_heads, v_heads, output_proj):
        import jax, jax.numpy as jnp
        import numpy as np
        D_MODEL = 512
        NUM_HEADS = 16
        DK = D_MODEL // NUM_HEADS
        B, S, _ = x.shape

        def proj(W):
            return (x @ W.T).reshape(B, S, NUM_HEADS, DK).transpose(0, 2, 1, 3)
        q, k, v = (proj(q_heads), proj(k_heads), proj(v_heads))
        scale = 1.0 / jnp.sqrt(jnp.asarray(DK, x.dtype))
        scores = jnp.einsum('bhqd,bhkd->bhqk', q, k) * scale
        causal = jnp.triu(jnp.ones((S, S), bool), k=1)
        scores = jnp.where(causal, jnp.asarray(-jnp.inf, scores.dtype), scores)
        attn = jax.nn.softmax(scores, axis=-1)
        out = jnp.einsum('bhqk,bhkd->bhqd', attn, v)
        out = out.transpose(0, 2, 1, 3).reshape(B, S, D_MODEL)
        return out @ output_proj.T

    def _L0_xattn_ref(decoder_input, encoder_output, W_q, W_k, W_v, W_o, b_o):
        import jax, jax.numpy as jnp
        import numpy as np
        EMBED = 512
        HEADS = 16
        HEAD_DIM = EMBED // HEADS
        B, Sd, E = decoder_input.shape
        Se = encoder_output.shape[1]
        Q = (decoder_input @ W_q).reshape(B, Sd, HEADS, HEAD_DIM)
        K = (encoder_output @ W_k).reshape(B, Se, HEADS, HEAD_DIM)
        V = (encoder_output @ W_v).reshape(B, Se, HEADS, HEAD_DIM)
        scores = jnp.einsum('bqhd,bkhd->bhqk', Q, K) / jnp.sqrt(jnp.float32(HEAD_DIM))
        attn = jax.nn.softmax(scores, axis=-1)
        out = jnp.einsum('bhqk,bkhd->bqhd', attn, V).reshape(B, Sd, E)
        return out @ W_o + b_o

    def _L0_ffn_ref(x, gate_W, gate_b, W1, b1, g1, be1, W2, b2, g2, be2):
        import jax, jax.numpy as jnp
        import numpy as np
        LN_EPS = 1e-05

        def _layernorm(x, g, b):
            m = jnp.mean(x, axis=-1, keepdims=True)
            v = jnp.mean(jnp.square(x - m), axis=-1, keepdims=True)
            return (x - m) * jax.lax.rsqrt(v + LN_EPS) * g + b
        K_TOP = 2
        B, N, D = x.shape
        BN = B * N
        xf = x.reshape(BN, D)
        gate_scores = xf @ gate_W + gate_b
        topk_scores, topk_idx = jax.lax.top_k(gate_scores, K_TOP)
        weights = jax.nn.softmax(topk_scores, axis=-1)

        def expert(w1, bb1, gg1, bbe1, w2, bb2, gg2, bbe2):
            h = jax.nn.relu(_layernorm(xf @ w1 + bb1, gg1, bbe1))
            return _layernorm(h @ w2 + bb2, gg2, bbe2)
        all_out = jax.vmap(expert)(W1, b1, g1, be1, W2, b2, g2, be2)
        exp_out = all_out[topk_idx, jnp.arange(BN)[:, None]]
        out = jnp.sum(weights[..., None] * exp_out, axis=1)
        return (out + xf).reshape(B, N, D)
    x = x + _L0_attn_ref(_layernorm(x, axis=-1), L0_attn_q_heads, L0_attn_k_heads, L0_attn_v_heads, L0_attn_output_proj)
    x = x + _L0_xattn_ref(_layernorm(x, axis=-1), ctx_1024, L0_xattn_W_q, L0_xattn_W_k, L0_xattn_W_v, L0_xattn_W_o, L0_xattn_b_o)
    x = x + _L0_ffn_ref(_layernorm(x, axis=-1), L0_ffn_gate_W, L0_ffn_gate_b, L0_ffn_W1, L0_ffn_b1, L0_ffn_g1, L0_ffn_be1, L0_ffn_W2, L0_ffn_b2, L0_ffn_g2, L0_ffn_be2)
    return x

_drawn_inputs = setup_inputs


def setup_inputs(seed=0):
    import zlib

    import numpy as np

    out = dict(_drawn_inputs(seed))
    spreads = {'L0_ffn_gate_b': (0.0, 0.1),
     'L0_ffn_b1': (0.0, 0.1),
     'L0_ffn_g1': (1.0, 0.2),
     'L0_ffn_be1': (0.0, 0.1),
     'L0_ffn_b2': (0.0, 0.1),
     'L0_ffn_g2': (1.0, 0.2),
     'L0_ffn_be2': (0.0, 0.1)}
    factors = {}
    for name, (base, spread) in spreads.items():
        noise = np.random.default_rng([zlib.crc32(name.encode()), seed]).standard_normal(out[name].shape)
        drawn = base * np.exp(spread * noise) if base else spread * noise
        out[name] = jnp.asarray(drawn.astype(out[name].dtype))
    for name, factor in factors.items():
        out[name] = (out[name] * factor).astype(out[name].dtype)
    return out
```

```python
import numpy as np
import concourse.bass as bass
import concourse.mybir as mybir
from contextlib import ExitStack

F32, F32R = mybir.dt.float32, mybir.dt.float32r
ACT = mybir.ActivationFunctionType
ALU = mybir.AluOpType
AX = mybir.AxisListType

P = 128
BATCH, SEQ, CTX = 4, 1024, 2048
D, HEADS, DK = 512, 16, 32
KT = D // P
HG = HEADS // 4
EXPERTS = 4
CH = 512
TPC = CH // P
EPS = 1e-5
MASKED = -3.0e38


class Signal:

    def __init__(self, nc, ctx, name, per, credit=0, step=1):
        self.sem = nc.alloc_semaphore(name)
        self.per, self.credit, self.step = per, credit, step

    def give_credit(self, eng):
        eng.sem_inc(self.sem, self.credit * self.step)

    def at(self, it, n):
        return it * (self.per * self.step) + (n + self.credit) * self.step


def build_constants(nc, ident, mask, neg_half):
    with ExitStack() as ctx:
        made = nc.alloc_semaphore("constants_made")
        block = ctx.enter_context(nc.Block())

        @block.gpsimd
        def _(pool):
            pool.memset(ident[:, :], 0.0).then_inc(made, 1)
            pool.memset(mask[:, :], 0.0).then_inc(made, 1)
            pool.memset(neg_half[:, :], -0.5).then_inc(made, 1)
            pool.wait_ge(made, 3)
            pool.affine_select(out=ident[:, :], in_=ident[:, :], compare_op=ALU.not_equal, fill=1.0,
                               base=0, pattern=[[-1, P]], channel_multiplier=1).then_inc(made, 1)
            pool.affine_select(out=mask[:, :], in_=mask[:, :], compare_op=ALU.is_ge, fill=MASKED,
                               base=0, pattern=[[-1, P]], channel_multiplier=1).then_inc(made, 1)
            pool.wait_ge(made, 5)


def load_weights(nc, name, weights, hi, lo, ident):
    with ExitStack() as ctx:
        raw = ctx.enter_context(nc.sbuf_tensor(f"{name}_raw", [P, 2, KT, D], F32))
        turned = ctx.enter_context(nc.psum_tensor(f"{name}_turned", [P, KT, D], F32))
        loaded = [nc.alloc_semaphore(f"{name}_loaded{u}") for u in range(2)]
        turned_ready = nc.alloc_semaphore(f"{name}_turned")
        hi_ready = nc.alloc_semaphore(f"{name}_hi")
        lo_ready = nc.alloc_semaphore(f"{name}_lo")
        block = ctx.enter_context(nc.Block())

        @block.sync
        def _(sp):
            for n, (w, _) in enumerate(weights):
                if n >= 2:
                    sp.wait_ge(lo_ready, n - 1)
                sp.dma_start(raw[:, n % 2], w.rearrange("(k p) n -> p k n", p=P)).then_inc(loaded[n % 2], 16)

        @block.tensor
        def _(pe):
            done = 0
            for n, (_, transposed) in enumerate(weights):
                if not transposed:
                    continue
                pe.wait_ge(loaded[n % 2], 16 * (n // 2 + 1))
                if n:
                    pe.wait_ge(lo_ready, n)
                for k in range(KT):
                    for m in range(KT):
                        mm = nc.tensor.transpose(turned[:, k, m * P:(m + 1) * P],
                                                 raw[:, n % 2, m, k * P:(k + 1) * P], ident[:, :])
                done += 1
                mm.then_inc(turned_ready, 1)

        def source(eng, n, seen):
            if weights[n][1]:
                eng.wait_ge(turned_ready, seen + 1)
                return turned[:, :, :], seen + 1
            eng.wait_ge(loaded[n % 2], 16 * (n // 2 + 1))
            return raw[:, n % 2], seen

        @block.scalar
        def _(act):
            seen = 0
            for n in range(len(weights)):
                src, seen = source(act, n, seen)
                nc.scalar.activation(hi[:, n], src, ACT.Copy).then_inc(hi_ready, 1)

        @block.vector
        def _(dve):
            seen = 0
            for n in range(len(weights)):
                src, seen = source(dve, n, seen)
                dve.wait_ge(hi_ready, n + 1)
                nc.vector.tensor_tensor(lo[:, n], src, hi[:, n].bitcast(F32),
                                        ALU.subtract).then_inc(lo_ready, 1)


def project(nc, name, src, chunks, norm, weights, outs, ident, neg_half):
    NOUT = 4 * len(weights)
    with ExitStack() as ctx:
        sb = lambda n, shape, dt=F32: ctx.enter_context(nc.sbuf_tensor(f"{name}_{n}", shape, dt))
        sig = lambda n, per, credit=0, step=1: Signal(nc, ctx, f"{name}_{n}", per, credit, step)
        w_hi = sb("w_hi", [P, len(weights), KT, D], F32R)
        w_lo = sb("w_lo", [P, len(weights), KT, D], F32R)
        load_weights(nc, f"{name}_w", weights, w_hi, w_lo, ident)
        x_in = sb("x_in", [P, 2, TPC, D])
        x_n = sb("x_n", [P, 2, TPC, D]) if norm else x_in
        stats = sb("stats", [P, TPC, 6])
        mean_var = sb("mean_var", [P, TPC, 2])
        var_eps = sb("var_eps", [P, TPC])
        rstd = sb("rstd", [P, TPC])
        xt_hi = sb("xt_hi", [P, 2, KT, CH], F32R)
        xt_lo = sb("xt_lo", [P, 2, KT, CH], F32R)
        out_hi = sb("out_hi", [P, 4, D], F32R)
        out_lo = sb("out_lo", [P, 4, D], F32R)
        out_n = sb("out_n", [P, 4, D])
        turned = [ctx.enter_context(nc.psum_tensor(f"{name}_turned{n}", [P, KT, P], F32)) for n in range(2)]
        acc = [ctx.enter_context(nc.psum_tensor(f"{name}_acc{n}", [P, D], F32)) for n in range(4)]

        loaded = [sig(f"loaded{u}", chunks // 2, step=16) for u in range(2)]
        step = sig("dve_step", 3 * chunks)
        rooted = sig("rooted", chunks)
        waited = sig("waited", 1)
        normed = sig("normed", chunks, 2)
        turned_ready = sig("turned_ready", TPC * chunks, 8)
        hi_ready = sig("xt_hi_ready", TPC * chunks)
        lo_ready = sig("xt_lo_ready", TPC * chunks, 2)
        acc_ready = sig("acc_ready", NOUT * chunks, 2 * NOUT)
        NSPLIT = 4 * sum(o[0] == "T" for o in outs)
        out_hi_ready = sig("out_hi_ready", NSPLIT * chunks)
        out_lo_ready = sig("out_lo_ready", NOUT * chunks, 4)
        dmas = lambda n: 2 if n < NSPLIT else 1
        stores = [sum(dmas(n) for n in range(s, NOUT, 4)) for s in range(4)]
        stored = [sig(f"stored{s}", stores[s] * chunks, 4, step=16) for s in range(4)]
        block = ctx.enter_context(nc.Block())
        src_v = src.rearrange("(c t p) d -> c p t d", p=P, t=TPC)

        def stores_before(s, u, n):
            return u * stores[s] + sum(dmas(m) for m in range(s, n, 4))

        def load(sp, it, u):
            if norm:
                sp.wait_ge(normed.sem, normed.at(it, u - 1))
            else:
                sp.wait_ge(turned_ready.sem, turned_ready.at(it, TPC * (u - 1)))
            sp.dma_start(x_in[:, u % 2], src_v[it * chunks + u]).then_inc(loaded[u % 2].sem, 16)

        @block.sync
        def _(sp):
            for s in range(4):
                stored[s].give_credit(sp)
            with sp.Fori(0, BATCH) as it:
                for u in range(chunks):
                    load(sp, it, u)
                    for n in range(NOUT):
                        kind, g, s = outs[n // 4][0], n % 4, n % 4
                        tok = slice(u * CH, (u + 1) * CH)
                        if kind == "T":
                            sp.wait_ge(out_lo_ready.sem, out_lo_ready.at(it, u * NOUT + n + 1))
                            sp.dma_start(outs[n // 4][1][it * HG + g, :, tok], out_hi[:, s].bitcast(F32)).then_inc(stored[s].sem, 16)
                            sp.dma_start(outs[n // 4][2][it * HG + g, :, tok], out_lo[:, s].bitcast(F32)).then_inc(stored[s].sem, 16)
                        else:
                            sp.wait_ge(out_lo_ready.sem, out_lo_ready.at(it, u * NOUT + n + 1))
                            t0 = u * CH + g * P
                            rows = outs[n // 4][1].rearrange("(b h) t d -> b t h d", h=HG)[it, t0:t0 + P]
                            sp.dma_start(rows, out_n[:, s].rearrange("p (h d) -> p h d", h=HG)).then_inc(stored[s].sem, 16)
            for s in range(4):
                sp.wait_ge(stored[s].sem, stored[s].at(BATCH, 0))

        @block.gpsimd
        def _(pool):
            if not norm:
                return
            with pool.Fori(0, BATCH) as it:
                for u in range(chunks):
                    pool.wait_ge(step.sem, step.at(it, 3 * u + 3))
                    pool.wait_ge(normed.sem, normed.at(it, u))
                    nc.gpsimd.tensor_tensor(rstd[:, :], var_eps[:, :], neg_half[:, :], ALU.pow).then_inc(rooted.sem, 1)

        @block.vector
        def _(dve):
            normed.give_credit(dve)
            lo_ready.give_credit(dve)
            out_lo_ready.give_credit(dve)
            with dve.Fori(0, BATCH) as it:
                for u in range(chunks):
                    if norm:
                        dve.wait_ge(loaded[u % 2].sem, loaded[u % 2].at(it, u // 2 + 1))
                        for t in range(TPC):
                            last = nc.vector.bn_stats(stats[:, t, :], x_in[:, u % 2, t, :])
                        last.then_inc(step.sem, 1)
                        dve.wait_ge(step.sem, step.at(it, 3 * u + 1))
                        dve.sem_inc(waited.sem, 1)
                        for t in range(TPC):
                            last = nc.vector.bn_aggr(mean_var[:, t, :], stats[:, t, :])
                        last.then_inc(step.sem, 1)
                        dve.wait_ge(step.sem, step.at(it, 3 * u + 2))
                        nc.vector.tensor_scalar(var_eps[:, :], mean_var[:, :, 1], EPS, None,
                                                ALU.add).then_inc(step.sem, 1)
                        dve.wait_ge(rooted.sem, rooted.at(it, u + 1))
                        dve.wait_ge(turned_ready.sem, turned_ready.at(it, TPC * (u - 1)))
                        for t in range(TPC):
                            last = nc.vector.tensor_scalar(x_n[:, u % 2, t, :], x_in[:, u % 2, t, :],
                                                           mean_var[:, t, 0:1], rstd[:, t:t + 1],
                                                           ALU.subtract, ALU.mult)
                        last.then_inc(normed.sem, 1)
                    for t in range(TPC):
                        dve.wait_ge(hi_ready.sem, hi_ready.at(it, TPC * u + t + 1))
                        nc.vector.tensor_tensor(xt_lo[:, u % 2, :, t * P:(t + 1) * P], turned[t % 2][:, :, :],
                                                xt_hi[:, u % 2, :, t * P:(t + 1) * P].bitcast(F32),
                                                ALU.subtract).then_inc(lo_ready.sem, 1)
                    for n in range(NOUT):
                        s = n % 4
                        o = outs[n // 4]
                        if o[0] == "T":
                            dve.wait_ge(out_hi_ready.sem, out_hi_ready.at(it, u * NSPLIT + n + 1))
                            dve.wait_ge(stored[s].sem, stored[s].at(it, stores_before(s, u, n)))
                            nc.vector.scalar_tensor_tensor(out_lo[:, s], acc[s][:, :], o[3], out_hi[:, s].bitcast(F32),
                                                           ALU.mult, ALU.subtract).then_inc(out_lo_ready.sem, 1)
                        else:
                            dve.wait_ge(acc_ready.sem, acc_ready.at(it, u * NOUT + n + 1))
                            dve.wait_ge(stored[s].sem, stored[s].at(it, stores_before(s, u, n)))
                            nc.vector.tensor_copy(out_n[:, s], acc[s][:, :]).then_inc(out_lo_ready.sem, 1)

        @block.scalar
        def _(act):
            with act.Fori(0, BATCH) as it:
                for u in range(chunks):
                    for t in range(TPC):
                        act.wait_ge(turned_ready.sem, turned_ready.at(it, TPC * u + t + 1))
                        if t == 0:
                            act.wait_ge(acc_ready.sem, acc_ready.at(it, (u - 1) * NOUT))
                        nc.scalar.activation(xt_hi[:, u % 2, :, t * P:(t + 1) * P], turned[t % 2][:, :, :],
                                             ACT.Copy).then_inc(hi_ready.sem, 1)
                    for n in range(NOUT):
                        s = n % 4
                        o = outs[n // 4]
                        if o[0] == "T":
                            act.wait_ge(acc_ready.sem, acc_ready.at(it, u * NOUT + n + 1))
                            act.wait_ge(stored[s].sem, stored[s].at(it, stores_before(s, u, n)))
                            nc.scalar.activation(out_hi[:, s], acc[s][:, :], ACT.Copy,
                                                 scale=o[3]).then_inc(out_hi_ready.sem, 1)

        @block.tensor
        def _(pe):
            turned_ready.give_credit(pe)
            acc_ready.give_credit(pe)
            with pe.Fori(0, BATCH) as it:
                for u in range(chunks):
                    if norm:
                        pe.wait_ge(normed.sem, normed.at(it, u + 1))
                    else:
                        pe.wait_ge(loaded[u % 2].sem, loaded[u % 2].at(it, u // 2 + 1))
                    for t in range(TPC):
                        pe.wait_ge(lo_ready.sem, lo_ready.at(it, TPC * u + t - 1))
                        for k in range(KT):
                            mm = nc.tensor.transpose(turned[t % 2][:, k, :], x_n[:, u % 2, t, k * P:(k + 1) * P],
                                                     ident[:, :])
                        mm.then_inc(turned_ready.sem, 1)
                    pe.wait_ge(lo_ready.sem, lo_ready.at(it, TPC * (u + 1)))
                    for n in range(NOUT):
                        w, g, s = n // 4, n % 4, n % 4
                        pe.wait_ge(out_lo_ready.sem, out_lo_ready.at(it, u * NOUT + n - 3))
                        cols = slice(g * P, (g + 1) * P)
                        i = 0
                        for a, b in ((0, 0), (0, 1), (1, 0)):
                            for k in range(KT):
                                x_part = (xt_hi, xt_lo)[a][:, u % 2, k, :]
                                w_part = (w_hi, w_lo)[b][:, w, k, :]
                                if outs[w][0] == "T":
                                    mm = nc.tensor.matmul(acc[s][:, :], w_part[:, cols], x_part,
                                                          start=i == 0, stop=i == 11)
                                else:
                                    mm = nc.tensor.matmul(acc[s][:, :], x_part[:, cols], w_part,
                                                          start=i == 0, stop=i == 11)
                                i += 1
                        mm.then_inc(acc_ready.sem, 1)


def attend(nc, name, q_parts, k_parts, v, out_t, keys, causal, ident, mask):
    HALVES = keys // 1024
    QC = SEQ // 256
    steps = [(w, qc, half) for w in range(2) for qc in range(QC) for half in range(HALVES)]
    G = len(steps)
    NCH = 2 * QC
    SETS = keys // P
    with ExitStack() as ctx:
        sb = lambda n, shape, dt=F32: ctx.enter_context(nc.sbuf_tensor(f"{name}_{n}", shape, dt))
        sig = lambda n, per, credit=0, step=1: Signal(nc, ctx, f"{name}_{n}", per, credit, step)
        q_st = sb("q_stack", [P, 2, 4, SEQ], F32R)
        k_st = sb("k_stack", [P, 2, 4, keys], F32R)
        v_sb = sb("v", [P, 2, SETS, P])
        probs = sb("probs", [P, 2, 8, 1024])
        probs_t = sb("probs_t", [P, 2, 4, 256])
        neg_max = sb("neg_max", [P, 2, HALVES, 8])
        sums = sb("sums", [P, 2, HALVES, 8])
        shift = sb("shift", [P, 2, 8])
        grow = sb("grow", [P, 2, 8])
        total = sb("total", [P, 2, 8])
        weight = sb("weight", [P, 2, HALVES, 8])
        w_sb = sb("w_sb", [P, HALVES * 256])
        part = sb("part", [P, 2, HALVES, 256])
        mixed = sb("mixed", [P, 2, 256]) if HALVES == 2 else part[:, :, 0, :]
        scores = [ctx.enter_context(nc.psum_tensor(f"{name}_scores{n}", [P, 1024], F32)) for n in range(2)]
        turned = [ctx.enter_context(nc.psum_tensor(f"{name}_turned{n}", [P, 2, 256], F32)) for n in range(2)]
        o_ps = ctx.enter_context(nc.psum_tensor(f"{name}_out", [P, 2, 256], F32))
        w_ps = ctx.enter_context(nc.psum_tensor(f"{name}_weights", [P, 2, 256], F32))

        def key_tiles(s):
            return 2 * steps[s][1] + 2 if causal else 8

        def tiles_before(s):
            return sum(key_tiles(m) for m in range(s))
        NT = tiles_before(G)

        loaded = [sig(f"loaded{w}", 8 + SETS // 8, step=16) for w in range(2)]
        scored = sig("scored", 8 * G)
        masked = sig("masked", 8 * G)
        maxed = sig("maxed", 8 * G)
        exped = sig("exped", 8 * G, 2)
        turned_r = [sig(f"turned_ready{a}", NT) for a in range(2)]
        copied = [sig(f"copied{a}", NT, 1) for a in range(2)]
        pv_done = sig("pv_done", NT, 16)
        prep = sig("weights_prep", 5 * NCH)
        grown = sig("grown", NCH)
        waited = sig("waited", 1)
        totals = sig("totals", NCH)
        weighed = sig("weighed", NCH, 1)
        spread = sig("spread", NCH, 2)
        spread_sb = sig("spread_sb", NCH, 1)
        scaled = sig("scaled", NCH, 2)
        mixed_r = sig("mixed_ready", NCH, 2)
        stored = [sig(f"stored{c}", NCH // 2, 1, step=16) for c in range(2)]
        block = ctx.enter_context(nc.Block())
        PASSES = BATCH * HG // 2

        def load_heads(sp, bh, w):
            for r in range(4):
                rows = slice(32 * r, 32 * r + 32)
                sp.dma_start(q_st[rows, w].bitcast(F32), q_parts[r // 2][bh].rearrange("(h p) t -> p h t", p=DK)).then_inc(loaded[w].sem, 16)
                sp.dma_start(k_st[rows, w].bitcast(F32), k_parts[r % 2][bh].rearrange("(h p) t -> p h t", p=DK)).then_inc(loaded[w].sem, 16)
            for k in range(0, SETS, 8):
                sp.dma_start(v_sb[:, w, k:k + 8], v[bh, k * P:(k + 8) * P].rearrange("(k p) d -> p k d", p=P)).then_inc(loaded[w].sem, 16)

        @block.sync
        def _(sp):
            for c in range(2):
                stored[c].give_credit(sp)
            load_heads(sp, 0, 0)

            def store(it, w):
                ready = mixed_r if HALVES == 2 else scaled
                for qc in range(QC):
                    c = w * QC + qc
                    sp.wait_ge(ready.sem, ready.at(it, c + 1))
                    sp.dma_start(out_t[it * 2 + w, :, qc * 256:(qc + 1) * 256], mixed[:, c % 2]).then_inc(stored[c % 2].sem, 16)

            def one_pass(it, more):
                sp.wait_ge(pv_done.sem, pv_done.at(it, 0))
                load_heads(sp, it * 2 + 1, 1)
                store(it, 0)
                if more:
                    sp.wait_ge(pv_done.sem, pv_done.at(it, tiles_before(G // 2)))
                    load_heads(sp, it * 2 + 2, 0)
                store(it, 1)
            with sp.Fori(0, PASSES - 1) as it:
                one_pass(it, True)
            one_pass(PASSES - 1, False)
            for c in range(2):
                sp.wait_ge(stored[c].sem, stored[c].at(PASSES, 0))

        @block.gpsimd
        def _(pool):
            if HALVES == 1:
                return
            mixed_r.give_credit(pool)
            with pool.Fori(0, PASSES) as it:
                def weights(c):
                    cp = c % 2
                    pool.wait_ge(exped.sem, exped.at(it, 16 * (c + 1)))
                    for a in range(2):
                        nc.gpsimd.tensor_tensor(shift[:, a, :], neg_max[:, cp, a, :], neg_max[:, cp, 1 - a, :],
                                                ALU.subtract).then_inc(prep.sem, 1)
                    pool.wait_ge(prep.sem, prep.at(it, 5 * c + 2))
                    pool.sem_inc(waited.sem, 1)
                    nc.gpsimd.tensor_scalar(shift[:, :, :], shift[:, :, :], 80.0, -200.0, ALU.min,
                                            ALU.max).then_inc(prep.sem, 1)
                    pool.wait_ge(grown.sem, grown.at(it, c + 1))
                    pool.wait_ge(weighed.sem, weighed.at(it, c))
                    for a in range(2):
                        nc.gpsimd.tensor_tensor(total[:, a, :], grow[:, a, :], sums[:, cp, 1 - a, :],
                                                ALU.mult).then_inc(prep.sem, 1)
                    pool.wait_ge(prep.sem, prep.at(it, 5 * c + 5))
                    nc.gpsimd.tensor_tensor(total[:, :, :], total[:, :, :], sums[:, cp, :, :],
                                            ALU.add).then_inc(totals.sem, 1)

                def finish(c):
                    cp = c % 2
                    pool.wait_ge(scaled.sem, scaled.at(it, c + 1))
                    pool.wait_ge(stored[cp].sem, stored[cp].at(it, c // 2))
                    nc.gpsimd.tensor_tensor(mixed[:, cp], part[:, cp, 0, :], part[:, cp, 1, :],
                                            ALU.add).then_inc(mixed_r.sem, 1)
                for c in range(NCH + 1):
                    if c < NCH:
                        weights(c)
                    if c > 0:
                        finish(c - 1)

        @block.tensor
        def _(pe):
            pv_done.give_credit(pe)
            spread.give_credit(pe)
            with pe.Fori(0, PASSES) as it:
                def score(s, j):
                    w, qc, half = steps[s]
                    h, t = j % 4, j // 4
                    n = 8 * s + j
                    if s % (G // 2) == 0 and j == 0:
                        pe.wait_ge(loaded[w].sem, loaded[w].at(it, loaded[w].per))
                    pe.wait_ge(exped.sem, exped.at(it, n - 1))
                    width = (2 * qc + t + 1) * P if causal else 1024
                    q0 = qc * 256 + t * P
                    for k0 in range(0, width, 512):
                        kn = min(512, width - k0)
                        mm = nc.tensor.matmul(scores[n % 2][:, k0:k0 + kn], q_st[:, w, h, q0:q0 + P],
                                              k_st[:, w, h, half * 1024 + k0:half * 1024 + k0 + kn],
                                              start=True, stop=True)
                    mm.then_inc(scored.sem, 1)

                def turn(s, k):
                    n = tiles_before(s) + k
                    if k == 0:
                        pe.wait_ge(exped.sem, exped.at(it, 8 * (s + 1)))
                    late = causal and k == 2 * steps[s][1] + 1
                    for a in range(2):
                        pe.wait_ge(copied[a].sem, copied[a].at(it, n))
                        for h in (2 * a, 2 * a + 1):
                            for t in range(1 if late else 0, 2):
                                mm = nc.tensor.transpose(turned[a][:, h % 2, t * P:(t + 1) * P],
                                                         probs[:, s % 2, 4 * t + h, k * P:(k + 1) * P], ident[:, :])
                        mm.then_inc(turned_r[a].sem, 1)

                def attend_tile(s, k):
                    w, qc, half = steps[s]
                    n = tiles_before(s) + k
                    o_half = half if HALVES == 2 else s % 2
                    if k == 0:
                        c = s // HALVES
                        pe.wait_ge(scaled.sem, scaled.at(it, c if HALVES == 2 else c - 1))
                    for a in range(2):
                        pe.wait_ge(copied[a].sem, copied[a].at(it, n + 1))
                    q0 = P if causal and k == 2 * qc + 1 else 0
                    last = k == key_tiles(s) - 1
                    for h in range(4):
                        mm = nc.tensor.matmul(o_ps[32 * h:32 * h + 32, o_half, q0:], v_sb[:, w, 8 * half + k, 32 * h:32 * h + 32],
                                              probs_t[:, n % 2, h, q0:], start=k == 0, stop=last, skip_group_check=True)
                    mm.then_inc(pv_done.sem, 1)

                def spread_weights(c):
                    pe.wait_ge(weighed.sem, weighed.at(it, c + 1))
                    pe.wait_ge(spread_sb.sem, spread_sb.at(it, c))
                    for a in range(HALVES):
                        for t in range(2):
                            for h in range(4):
                                wt = weight[:, c % 2, a, 4 * t + h:4 * t + h + 1].to_broadcast([P, DK])
                                mm = nc.tensor.matmul(w_ps[32 * h:32 * h + 32, a, t * P:(t + 1) * P], wt, ident[:, :],
                                                      start=True, stop=True, skip_group_check=True)
                    mm.then_inc(spread.sem, 1)

                for s in range(G + 1):
                    for j in range(8):
                        if s < G:
                            score(s, j)
                        if s > 0 and j < key_tiles(s - 1):
                            turn(s - 1, j)
                            if j > 0:
                                attend_tile(s - 1, j - 1)
                    if s > 0:
                        attend_tile(s - 1, key_tiles(s - 1) - 1)
                        if s % HALVES == 0:
                            spread_weights(s // HALVES - 1)

        def copy_turned(eng, copy, it, s, k, a):
            n = tiles_before(s) + k
            eng.wait_ge(turned_r[a].sem, turned_r[a].at(it, n + 1))
            eng.wait_ge(pv_done.sem, pv_done.at(it, n - 1))
            q0 = P if causal and k == 2 * steps[s][1] + 1 else 0
            copy(probs_t[:, n % 2, 2 * a:2 * a + 2, q0:], turned[a][:, :, q0:]).then_inc(copied[a].sem, 1)

        @block.scalar
        def _(act):
            exped.give_credit(act)
            copied[0].give_credit(act)
            spread_sb.give_credit(act)
            with act.Fori(0, PASSES) as it:
                def exp_piece(s, j):
                    w, qc, half = steps[s]
                    n, c = 8 * s + j, s // HALVES
                    width = (2 * qc + j // 4 + 1) * P if causal else 1024
                    act.wait_ge(maxed.sem, maxed.at(it, n + 1))
                    if j == 0:
                        act.wait_ge(pv_done.sem, pv_done.at(it, tiles_before(max(s - 1, 0))))
                    nc.scalar.activation(probs[:, s % 2, j, 0:width], scores[n % 2][:, 0:width], ACT.Exp,
                                         bias=neg_max[:, c % 2, half, j:j + 1],
                                         accum_out=sums[:, c % 2, half, j:j + 1]).then_inc(exped.sem, 1)

                for s in range(G + 1):
                    for j in range(8):
                        if s < G:
                            exp_piece(s, j)
                        if s > 0 and j < key_tiles(s - 1):
                            copy_turned(act, lambda o, i: nc.scalar.activation(o, i, ACT.Copy), it, s - 1, j, 0)
                        if HALVES == 2 and j == 1 and s > 0 and s % 2 == 0:
                            c = s // 2 - 1
                            act.wait_ge(prep.sem, prep.at(it, 5 * c + 3))
                            nc.scalar.activation(grow[:, :, :], shift[:, :, :], ACT.Exp).then_inc(grown.sem, 1)
                    if s > 0 and s % HALVES == 0:
                        c = s // HALVES - 1
                        act.wait_ge(spread.sem, spread.at(it, c + 1))
                        act.wait_ge(scaled.sem, scaled.at(it, c))
                        nc.scalar.activation(w_sb[:, :], w_ps[:, 0:HALVES, :], ACT.Copy).then_inc(spread_sb.sem, 1)

        @block.vector
        def _(dve):
            copied[1].give_credit(dve)
            scaled.give_credit(dve)
            weighed.give_credit(dve)
            with dve.Fori(0, PASSES) as it:
                def max_piece(s, j):
                    w, qc, half = steps[s]
                    n, c = 8 * s + j, s // HALVES
                    width = (2 * qc + j // 4 + 1) * P if causal else 1024
                    sc = scores[n % 2]
                    dve.wait_ge(scored.sem, scored.at(it, n + 1))
                    if causal:
                        nc.vector.tensor_tensor(sc[:, width - P:width], sc[:, width - P:width], mask[:, :],
                                                ALU.add).then_inc(masked.sem, 1)
                        dve.wait_ge(masked.sem, masked.at(it, n + 1))
                    if j == 0 and half == 0:
                        dve.wait_ge(spread.sem, spread.at(it, c - 1))
                    nc.vector.tensor_reduce(neg_max[:, c % 2, half, j:j + 1], sc[:, 0:width], AX.X, ALU.max,
                                            negate=True).then_inc(maxed.sem, 1)

                for s in range(G + 1):
                    for j in range(8):
                        if s < G:
                            max_piece(s, j)
                        if s > 0 and j < key_tiles(s - 1):
                            copy_turned(dve, lambda o, i: nc.vector.tensor_copy(o, i), it, s - 1, j, 1)
                        if j == (5 if HALVES == 2 else 1) and s > 0 and s % HALVES == 0:
                            c = s // HALVES - 1
                            if HALVES == 2:
                                dve.wait_ge(totals.sem, totals.at(it, c + 1))
                                nc.vector.reciprocal(weight[:, c % 2, :, :], total[:, :, :]).then_inc(weighed.sem, 1)
                            else:
                                dve.wait_ge(exped.sem, exped.at(it, 8 * (c + 1)))
                                nc.vector.reciprocal(weight[:, c % 2, :, :], sums[:, c % 2, :, :]).then_inc(weighed.sem, 1)
                    if s > 0 and s % HALVES == 0:
                        c = s // HALVES - 1
                        dve.wait_ge(spread_sb.sem, spread_sb.at(it, c + 1))
                        dve.wait_ge(pv_done.sem, pv_done.at(it, tiles_before(s)))
                        if HALVES == 2:
                            dve.wait_ge(mixed_r.sem, mixed_r.at(it, c - 1))
                            src = o_ps[:, :, :]
                        else:
                            dve.wait_ge(stored[c % 2].sem, stored[c % 2].at(it, c // 2))
                            src = o_ps[:, (s - 1) % 2:(s - 1) % 2 + 1, :]
                        nc.vector.tensor_tensor(part[:, c % 2, :, :], src,
                                                w_sb[:, :].rearrange("p (a q) -> p a q", a=HALVES),
                                                ALU.mult).then_inc(scaled.sem, 1)


def project_out(nc, name, attn_t, weight, bias, residual, out, ident):
    with ExitStack() as ctx:
        sb = lambda n, shape, dt=F32: ctx.enter_context(nc.sbuf_tensor(f"{name}_{n}", shape, dt))
        sig = lambda n, per, credit=0, step=1: Signal(nc, ctx, f"{name}_{n}", per, credit, step)
        w_hi = sb("w_hi", [P, 1, KT, D], F32R)
        w_lo = sb("w_lo", [P, 1, KT, D], F32R)
        load_weights(nc, f"{name}_w", [weight], w_hi, w_lo, ident)
        a_in = sb("a_in", [P, 2, KT, CH])
        a_hi = sb("a_hi", [P, 2, KT, CH], F32R)
        a_lo = sb("a_lo", [P, 2, KT, CH], F32R)
        res = sb("res", [P, 2, TPC, D])
        row = sb("row", [P, D])
        y = sb("y", [P, 2, TPC, D])
        acc = [ctx.enter_context(nc.psum_tensor(f"{name}_acc{n}", [P, D], F32)) for n in range(4)]
        loaded = [sig(f"loaded{u}", 2, step=16) for u in range(2)]
        row_loaded = sig("row_loaded", 0)
        biased = sig("biased", 2)
        waited = sig("waited", 1)
        hi_ready = sig("a_hi_ready", 2)
        lo_ready = sig("a_lo_ready", 2, 2)
        acc_ready = sig("acc_ready", 8, 16)
        added = sig("added", 8, 16)
        stored = [sig(f"stored{u}", 1, 1, step=16) for u in range(2)]
        block = ctx.enter_context(nc.Block())
        res_v = residual.rearrange("(c t p) d -> c p t d", p=P, t=TPC)
        out_v = out.rearrange("(c t p) d -> c p t d", p=P, t=TPC)

        @block.sync
        def _(sp):
            for u in range(2):
                stored[u].give_credit(sp)
            if bias is not None:
                sp.dma_start(row[:, :], bias.rearrange("(o d) -> o d", o=1).to_broadcast([P, D])).then_inc(row_loaded.sem, 16)
            with sp.Fori(0, BATCH) as it:
                for u in range(2):
                    sp.wait_ge(lo_ready.sem, lo_ready.at(it, u - 1))
                    sp.sem_inc(waited.sem, 1)
                    sp.wait_ge(added.sem, added.at(it, 4 * (u - 1)))
                    sp.dma_start(a_in[:, u], attn_t.rearrange("(b g) p t -> b p g t", g=HG)[it, :, :, u * CH:(u + 1) * CH]).then_inc(loaded[u].sem, 16)
                    sp.dma_start(res[:, u], res_v[it * 2 + u]).then_inc(loaded[u].sem, 16)
                for u in range(2):
                    sp.wait_ge(added.sem, added.at(it, 4 * (u + 1)))
                    sp.dma_start(out_v[it * 2 + u], y[:, u]).then_inc(stored[u].sem, 16)
            for u in range(2):
                sp.wait_ge(stored[u].sem, stored[u].at(BATCH, 0))

        @block.scalar
        def _(act):
            with act.Fori(0, BATCH) as it:
                for u in range(2):
                    act.wait_ge(loaded[u].sem, loaded[u].at(it, 2))
                    act.wait_ge(acc_ready.sem, acc_ready.at(it, 4 * (u - 1)))
                    nc.scalar.activation(a_hi[:, u], a_in[:, u], ACT.Copy).then_inc(hi_ready.sem, 1)

        @block.vector
        def _(dve):
            lo_ready.give_credit(dve)
            added.give_credit(dve)
            if bias is not None:
                dve.wait_ge(row_loaded.sem, 16)
            with dve.Fori(0, BATCH) as it:
                for u in range(2):
                    dve.wait_ge(hi_ready.sem, hi_ready.at(it, u + 1))
                    nc.vector.tensor_tensor(a_lo[:, u], a_in[:, u], a_hi[:, u].bitcast(F32),
                                            ALU.subtract).then_inc(lo_ready.sem, 1)
                    if bias is not None:
                        for t in range(TPC):
                            last = nc.vector.tensor_tensor(res[:, u, t], res[:, u, t], row[:, :], ALU.add)
                        last.then_inc(biased.sem, 1)
                        dve.wait_ge(biased.sem, biased.at(it, u + 1))
                    dve.wait_ge(stored[u].sem, stored[u].at(it, 0))
                    for t in range(TPC):
                        dve.wait_ge(acc_ready.sem, acc_ready.at(it, 4 * u + t + 1))
                        nc.vector.tensor_tensor(y[:, u, t], acc[t][:, :], res[:, u, t], ALU.add).then_inc(added.sem, 1)

        @block.tensor
        def _(pe):
            acc_ready.give_credit(pe)
            with pe.Fori(0, BATCH) as it:
                for u in range(2):
                    pe.wait_ge(lo_ready.sem, lo_ready.at(it, u + 1))
                    for t in range(TPC):
                        pe.wait_ge(added.sem, added.at(it, 4 * (u - 1) + t + 1))
                        i = 0
                        for a, w in ((a_hi, w_hi), (a_hi, w_lo), (a_lo, w_hi)):
                            for k in range(KT):
                                mm = nc.tensor.matmul(acc[t][:, :], a[:, u, k, t * P:(t + 1) * P], w[:, 0, k, :],
                                                      start=i == 0, stop=i == 11)
                                i += 1
                        mm.then_inc(acc_ready.sem, 1)


def route(nc, name, src, gate_w, gate_b, y_hi, y_lo, base, gates, ident, neg_half):
    with ExitStack() as ctx:
        sb = lambda n, shape, dt=F32: ctx.enter_context(nc.sbuf_tensor(f"{name}_{n}", shape, dt))
        sig = lambda n, per, credit=0, step=1: Signal(nc, ctx, f"{name}_{n}", per, credit, step)
        gw = sb("gw", [P, KT, EXPERTS])
        gw_hi = sb("gw_hi", [P, KT, EXPERTS], F32R)
        gw_lo = sb("gw_lo", [P, KT, EXPERTS], F32R)
        gb = sb("gb", [EXPERTS, 1])
        earlier = sb("earlier", [P, TPC, EXPERTS, EXPERTS])
        x_in = sb("x_in", [P, 2, TPC, D])
        x_n = sb("x_n", [P, 2, TPC, D])
        stats = sb("stats", [P, TPC, 6])
        mean_var = sb("mean_var", [P, TPC, 2])
        var_eps = sb("var_eps", [P, TPC])
        rstd = sb("rstd", [P, TPC])
        xt_hi = sb("xt_hi", [P, 2, KT, CH], F32R)
        xt_lo = sb("xt_lo", [P, 2, KT, CH], F32R)
        g_rows = sb("g_rows", [EXPERTS, CH])
        g = sb("g", [P, TPC, EXPERTS])
        above = sb("above", [P, TPC, EXPERTS, EXPERTS])
        ties = sb("ties", [P, TPC, EXPERTS, EXPERTS])
        rank = sb("rank", [P, TPC, EXPERTS])
        top = sb("top", [P, TPC])
        e_g = sb("e_g", [P, TPC, EXPERTS])
        turned = [ctx.enter_context(nc.psum_tensor(f"{name}_turned{n}", [P, KT, P], F32)) for n in range(2)]
        g_ps = ctx.enter_context(nc.psum_tensor(f"{name}_g_ps", [P, CH], F32))
        gt_ps = ctx.enter_context(nc.psum_tensor(f"{name}_gt_ps", [P, TPC, P], F32))
        small = nc.alloc_semaphore(f"{name}_small")
        earlier_made = nc.alloc_semaphore(f"{name}_earlier_made")
        gw_hi_ready = nc.alloc_semaphore(f"{name}_gw_hi_ready")
        gw_lo_ready = nc.alloc_semaphore(f"{name}_gw_lo_ready")
        loaded = [sig(f"loaded{u}", 1, step=16) for u in range(2)]
        step = sig("dve_step", 2 * 12)
        rooted = sig("rooted", 2)
        waited = sig("waited", 1)
        normed = sig("normed", 2, 1)
        based = sig("based", 2, 2)
        turned_ready = sig("turned_ready", 2 * TPC, 8)
        hi_ready = sig("hi_ready", 2 * TPC)
        lo_ready = sig("lo_ready", 2 * TPC, 2)
        scored = sig("scored", 2, 2)
        rows = sig("rows", 2, 1)
        g_turned = sig("g_turned", 2)
        g_read = sig("g_read", 2, 1)
        less_max = sig("less_max", 2)
        exped = sig("exped", 2)
        stored = [sig(f"stored{u}", 2, 2, step=16) for u in range(2)]
        block = ctx.enter_context(nc.Block())
        src_v = src.rearrange("(c t p) d -> c p t d", p=P, t=TPC)

        @block.sync
        def _(sp):
            sp.dma_start(gw[:, :, :], gate_w.rearrange("(k p) e -> p k e", p=P)).then_inc(small, 16)
            sp.dma_start(gb[:, :], gate_b.rearrange("(e o) -> e o", o=1)).then_inc(small, 16)
            for u in range(2):
                stored[u].give_credit(sp)
            with sp.Fori(0, BATCH) as it:
                for u in range(2):
                    sp.wait_ge(based.sem, based.at(it, u - 1))
                    sp.dma_start(x_in[:, u], src_v[it * 2 + u]).then_inc(loaded[u].sem, 16)
                for u in range(2):
                    sp.wait_ge(lo_ready.sem, lo_ready.at(it, TPC * (u + 1)))
                    for part, dst in ((xt_hi, y_hi), (xt_lo, y_lo)):
                        sp.dma_start(dst.rearrange("k p (c t) -> c p k t", t=CH)[it * 2 + u], part[:, u].bitcast(F32)).then_inc(stored[u].sem, 16)
            for u in range(2):
                sp.wait_ge(stored[u].sem, stored[u].at(BATCH, 0))

        @block.gpsimd
        def _(pool):
            based.give_credit(pool)
            pool.memset(earlier[:, :, :, :], 1.0).then_inc(earlier_made, 1)
            pool.wait_ge(earlier_made, 1)
            pool.affine_select(out=earlier[:, :, :, :], in_=earlier[:, :, :, :], compare_op=ALU.is_gt, fill=0.0, base=0,
                               pattern=[[0, TPC], [1, EXPERTS], [-1, EXPERTS]], channel_multiplier=0).then_inc(earlier_made, 1)
            with pool.Fori(0, BATCH) as it:
                for u in range(2):
                    pool.wait_ge(step.sem, step.at(it, 12 * u + 3))
                    pool.wait_ge(normed.sem, normed.at(it, u))
                    nc.gpsimd.tensor_tensor(rstd[:, :], var_eps[:, :], neg_half[:, :], ALU.pow).then_inc(rooted.sem, 1)
                    pool.wait_ge(normed.sem, normed.at(it, u + 1))
                    nc.gpsimd.tensor_tensor(base[:, bass.ds(it * (2 * TPC) + TPC * u, TPC), :], x_in[:, u], x_n[:, u],
                                            ALU.add).then_inc(based.sem, 1)
            pool.wait_ge(based.sem, based.at(BATCH, 0))

        @block.scalar
        def _(act):
            act.wait_ge(small, 32)
            nc.scalar.activation(gw_hi[:, :, :], gw[:, :, :], ACT.Copy).then_inc(gw_hi_ready, 1)
            rows.give_credit(act)
            with act.Fori(0, BATCH) as it:
                for u in range(2):
                    for t in range(TPC):
                        act.wait_ge(turned_ready.sem, turned_ready.at(it, TPC * u + t + 1))
                        if t == 0:
                            act.wait_ge(scored.sem, scored.at(it, u - 1))
                            act.wait_ge(stored[u].sem, stored[u].at(it, 0))
                        nc.scalar.activation(xt_hi[:, u, :, t * P:(t + 1) * P], turned[t % 2][:, :, :],
                                             ACT.Copy).then_inc(hi_ready.sem, 1)
                    act.wait_ge(scored.sem, scored.at(it, u + 1))
                    act.wait_ge(g_read.sem, g_read.at(it, u))
                    nc.scalar.activation(g_rows[:, :], g_ps[0:EXPERTS, :], ACT.Identity,
                                         bias=gb[:, 0:1]).then_inc(rows.sem, 1)
                    act.wait_ge(less_max.sem, less_max.at(it, u + 1))
                    nc.scalar.activation(e_g[:, :, :], e_g[:, :, :], ACT.Exp).then_inc(exped.sem, 1)

        @block.vector
        def _(dve):
            normed.give_credit(dve)
            dve.wait_ge(small, 32)
            dve.wait_ge(gw_hi_ready, 1)
            dve.wait_ge(earlier_made, 2)
            nc.vector.tensor_tensor(gw_lo[:, :, :], gw[:, :, :], gw_hi[:, :, :].bitcast(F32), ALU.subtract).then_inc(gw_lo_ready, 1)
            lo_ready.give_credit(dve)
            g_read.give_credit(dve)
            with dve.Fori(0, BATCH) as it:
                for u in range(2):
                    n = [12 * u]

                    def link(ins):
                        n[0] += 1
                        ins.then_inc(step.sem, 1)
                        dve.wait_ge(step.sem, step.at(it, n[0]))

                    dve.wait_ge(loaded[u].sem, loaded[u].at(it, 1))
                    for t in range(TPC):
                        last = nc.vector.bn_stats(stats[:, t, :], x_in[:, u, t, :])
                    n[0] += 1
                    last.then_inc(step.sem, 1)
                    dve.wait_ge(step.sem, step.at(it, n[0]))
                    dve.sem_inc(waited.sem, 1)
                    for t in range(TPC):
                        last = nc.vector.bn_aggr(mean_var[:, t, :], stats[:, t, :])
                    link(last)
                    link(nc.vector.tensor_scalar(var_eps[:, :], mean_var[:, :, 1], EPS, None, ALU.add))
                    dve.wait_ge(rooted.sem, rooted.at(it, u + 1))
                    dve.wait_ge(turned_ready.sem, turned_ready.at(it, TPC * (u - 1)))
                    dve.wait_ge(based.sem, based.at(it, u - 1))
                    for t in range(TPC):
                        last = nc.vector.tensor_scalar(x_n[:, u, t, :], x_in[:, u, t, :], mean_var[:, t, 0:1],
                                                       rstd[:, t:t + 1], ALU.subtract, ALU.mult)
                    last.then_inc(normed.sem, 1)
                    for t in range(TPC):
                        dve.wait_ge(hi_ready.sem, hi_ready.at(it, TPC * u + t + 1))
                        nc.vector.tensor_tensor(xt_lo[:, u, :, t * P:(t + 1) * P], turned[t % 2][:, :, :],
                                                xt_hi[:, u, :, t * P:(t + 1) * P].bitcast(F32),
                                                ALU.subtract).then_inc(lo_ready.sem, 1)
                    dve.wait_ge(g_turned.sem, g_turned.at(it, u + 1))
                    nc.vector.tensor_copy(g[:, :, :], gt_ps[:, :, 0:EXPERTS]).then_inc(g_read.sem, 1)
                    dve.wait_ge(g_read.sem, g_read.at(it, u + 1))
                    four = [P, TPC, EXPERTS, EXPERTS]
                    other = g[:, :, :].unsqueeze(2).to_broadcast(four)
                    own = g[:, :, :].unsqueeze(3).to_broadcast(four)
                    nc.vector.tensor_tensor(above[:, :, :, :], other, own, ALU.is_gt)
                    nc.vector.tensor_reduce(top[:, :], g[:, :, :], AX.X, ALU.max)
                    link(nc.vector.tensor_tensor(ties[:, :, :, :], other, own, ALU.is_equal))
                    nc.vector.tensor_tensor(e_g[:, :, :], g[:, :, :], top[:, :].unsqueeze(2).to_broadcast([P, TPC, EXPERTS]),
                                            ALU.subtract).then_inc(less_max.sem, 1)
                    link(nc.vector.tensor_tensor(ties[:, :, :, :], ties[:, :, :, :], earlier[:, :, :, :], ALU.mult))
                    link(nc.vector.tensor_tensor(above[:, :, :, :], above[:, :, :, :], ties[:, :, :, :], ALU.add))
                    link(nc.vector.tensor_reduce(rank[:, :, :], above[:, :, :, :], AX.X, ALU.add))
                    link(nc.vector.tensor_scalar(rank[:, :, :], rank[:, :, :], 2.0, None, ALU.is_lt))
                    dve.wait_ge(exped.sem, exped.at(it, u + 1))
                    link(nc.vector.tensor_tensor(rank[:, :, :], rank[:, :, :], e_g[:, :, :], ALU.mult))
                    link(nc.vector.tensor_reduce(top[:, :], rank[:, :, :], AX.X, ALU.add))
                    link(nc.vector.reciprocal(top[:, :], top[:, :]))
                    link(nc.vector.tensor_tensor(gates[:, bass.ds(it * (2 * TPC) + TPC * u, TPC), :], rank[:, :, :],
                                                 top[:, :].unsqueeze(2).to_broadcast([P, TPC, EXPERTS]), ALU.mult))
                    assert n[0] == 12 * (u + 1)

        @block.tensor
        def _(pe):
            pe.wait_ge(gw_lo_ready, 1)
            turned_ready.give_credit(pe)
            scored.give_credit(pe)
            with pe.Fori(0, BATCH) as it:
                for u in range(2):
                    pe.wait_ge(normed.sem, normed.at(it, u + 1))
                    for t in range(TPC):
                        pe.wait_ge(lo_ready.sem, lo_ready.at(it, TPC * u + t - 1))
                        for k in range(KT):
                            mm = nc.tensor.transpose(turned[t % 2][:, k, :], x_n[:, u, t, k * P:(k + 1) * P], ident[:, :])
                        mm.then_inc(turned_ready.sem, 1)
                    pe.wait_ge(lo_ready.sem, lo_ready.at(it, TPC * (u + 1)))
                    pe.wait_ge(rows.sem, rows.at(it, u))
                    i = 0
                    for x_part, w_part in ((xt_hi, gw_hi), (xt_hi, gw_lo), (xt_lo, gw_hi)):
                        for k in range(KT):
                            mm = nc.tensor.matmul(g_ps[0:EXPERTS, :], w_part[:, k, :], x_part[:, u, k, :],
                                                  start=i == 0, stop=i == 11)
                            i += 1
                    mm.then_inc(scored.sem, 1)
                    pe.wait_ge(gw_lo_ready, 1)
                    pe.wait_ge(rows.sem, rows.at(it, u + 1))
                    pe.wait_ge(g_read.sem, g_read.at(it, u))
                    for t in range(TPC):
                        mm = nc.tensor.transpose(gt_ps[:, t, 0:EXPERTS], g_rows[:, t * P:(t + 1) * P], ident[0:EXPERTS, 0:EXPERTS])
                    mm.then_inc(g_turned.sem, 1)


def split_experts(nc, w1, w2, w_hi, w_lo):
    with ExitStack() as ctx:
        raw = ctx.enter_context(nc.sbuf_tensor("split_raw", [P, 2, KT, D], F32))
        hi = ctx.enter_context(nc.sbuf_tensor("split_hi", [P, 2, KT, D], F32R))
        lo = ctx.enter_context(nc.sbuf_tensor("split_lo", [P, 2, KT, D], F32R))
        loaded = [nc.alloc_semaphore(f"split_loaded{u}") for u in range(2)]
        stored = [nc.alloc_semaphore(f"split_stored{u}") for u in range(2)]
        hi_ready = nc.alloc_semaphore("split_hi_ready")
        lo_ready = nc.alloc_semaphore("split_lo_ready")
        block = ctx.enter_context(nc.Block())
        mats = [(w, e) for e in range(EXPERTS) for w in range(2)]

        @block.sync
        def _(sp):
            for n, (w, e) in enumerate(mats):
                if n >= 2:
                    sp.wait_ge(lo_ready, n - 1)
                sp.dma_start(raw[:, n % 2], (w1, w2)[w][e].rearrange("(k p) n -> p k n", p=P)).then_inc(loaded[n % 2], 16)

        @block.gpsimd
        def _(pool):
            for n, (w, e) in enumerate(mats):
                pool.wait_ge(lo_ready, n + 1)
                for part, dst in ((hi, w_hi), (lo, w_lo)):
                    pool.dma_start(dst[e, w].rearrange("(k p) n -> p k n", p=P), part[:, n % 2].bitcast(F32)).then_inc(stored[n % 2], 16)
            for u in range(2):
                pool.wait_ge(stored[u], 16 * len(mats))

        @block.scalar
        def _(act):
            for n in range(len(mats)):
                act.wait_ge(loaded[n % 2], 16 * (n // 2 + 1))
                if n >= 2:
                    act.wait_ge(stored[n % 2], 32 * (n // 2))
                nc.scalar.activation(hi[:, n % 2], raw[:, n % 2], ACT.Copy).then_inc(hi_ready, 1)

        @block.vector
        def _(dve):
            for n in range(len(mats)):
                dve.wait_ge(hi_ready, n + 1)
                nc.vector.tensor_tensor(lo[:, n % 2], raw[:, n % 2], hi[:, n % 2].bitcast(F32), ALU.subtract).then_inc(lo_ready, 1)


def experts(nc, w_hi_d, w_lo_d, vectors, y_hi, y_lo, base, gates, out, ident):
    TOK, TT = 256, 2
    CHUNKS = BATCH * SEQ // TOK
    b1, g1, be1, b2, g2, be2 = vectors
    name = "experts"
    with ExitStack() as ctx:
        sb = lambda n, shape, dt=F32: ctx.enter_context(nc.sbuf_tensor(f"{name}_{n}", shape, dt))
        sig = lambda n, per, credit=0, step=1: Signal(nc, ctx, f"{name}_{n}", per, credit, step)
        w_hi = sb("w_hi", [P, 2, 2, KT, D], F32R)
        w_lo = sb("w_lo", [P, 2, 2, KT, D], F32R)
        rows = sb("rows", [P, 2, 4, D])
        cols = sb("cols", [P, 2, EXPERTS, KT])
        yt_hi = sb("yt_hi", [P, 2, KT, TOK], F32R)
        yt_lo = sb("yt_lo", [P, 2, KT, TOK], F32R)
        t1 = sb("t1", [P, TT, D])
        u1 = sb("u1", [P, TT, D])
        relu = sb("relu", [P, KT, TOK])
        ht_hi = sb("ht_hi", [P, KT, TOK], F32R)
        ht_lo = sb("ht_lo", [P, KT, TOK], F32R)
        t2 = sb("t2", [P, TT, D])
        u2 = sb("u2", [P, TT, D])
        v2 = sb("v2", [P, TT, D])
        stats = sb("stats", [P, 2, TT, 6])
        mean_var = sb("mean_var", [P, 2, TT, 2])
        rstd = sb("rstd", [P, 2, TT])
        neg_mean = sb("neg_mean", [P, 2, TT])
        root = sb("root", [P, 2, TT])
        eps = sb("eps", [P, 1])
        acc1 = [ctx.enter_context(nc.psum_tensor(f"{name}_acc1_{n}", [P, D], F32)) for n in range(TT)]
        acc2 = [ctx.enter_context(nc.psum_tensor(f"{name}_acc2_{n}", [P, D], F32)) for n in range(TT)]
        turned = [ctx.enter_context(nc.psum_tensor(f"{name}_turned{n}", [P, 2, TOK], F32)) for n in range(2)]

        weights_in = [nc.alloc_semaphore(f"{name}_weights_in{w}") for w in range(2)]
        cols_in = nc.alloc_semaphore(f"{name}_cols_in")
        y_in = [Signal(nc, ctx, f"{name}_y_in{u}", 2, 0, 16) for u in range(2)]
        m1 = sig("m1_done", TT, 2 * TT)
        b1_added = sig("b1_added", TT, TT)
        norm1 = sig("norm1_step", 4)
        u1_ready = sig("u1_ready", TT)
        turned_ready = sig("turned_ready", 2, 2)
        relu_ready = sig("relu_ready", 1)
        relu_banks = sig("relu_banks", 2, 2)
        hi_ready = sig("hi_ready", 1)
        lo_ready = sig("lo_ready", 1, 1)
        m2 = sig("m2_done", TT, 2 * TT)
        b2_added = sig("b2_added", TT, TT)
        norm2 = sig("norm2_step", 4)
        rooted = [sig(f"rooted{n}", 1) for n in range(2)]
        waited = sig("waited", 1)
        u2_ready = sig("u2_ready", TT, TT)
        g2_done = sig("g2_done", TT, TT)
        v2_ready = sig("v2_ready", TT)
        added = sig("added", TT, TT)
        stored = nc.alloc_semaphore(f"{name}_stored")
        block = ctx.enter_context(nc.Block())

        def chunks(eng, first, step, last_step):
            with eng.Fori(0, CHUNKS // 2 - 1) as i:
                for u in range(2):
                    step(i * 2 + (first + u), i * 2 + u, u, i + first // 2, True)
            i = CHUNKS // 2 - 1
            for u in range(2):
                step(first + 2 * i + u, 2 * i + u, u, i + first // 2, u == 0)

        @block.sync
        def _(sp):
            for n, vec in enumerate((g1, be1)):
                sp.dma_start(cols[:, n], vec.rearrange("e (k p) -> p e k", p=P),
                             allow_slow_non_contiguous=True).then_inc(cols_in, 16)

            def load_expert(e):
                w = e % 2
                if e >= 2:
                    sp.wait_ge(added.sem, added.at((e - 1) * CHUNKS, 0))
                for part, dst in ((w_hi_d, w_hi), (w_lo_d, w_lo)):
                    for m in range(2):
                        sp.dma_start(dst[:, w, m].bitcast(F32), part[e, m].rearrange("(k p) n -> p k n", p=P)).then_inc(weights_in[w], 16)
                for n, vec in enumerate((b1, b2, g2, be2)):
                    sp.dma_start(rows[:, w, n, :], vec[e:e + 1, :].to_broadcast([P, D])).then_inc(weights_in[w], 16)

            load_expert(0)
            for e in range(EXPERTS):
                if e == 0:
                    load_expert(1)

                def load_y(lin, c, u, pair, more):
                    sp.wait_ge(m1.sem, m1.at(lin, -TT))
                    for part, dst in ((y_hi, yt_hi), (y_lo, yt_lo)):
                        sp.dma_start(dst[:, u].bitcast(F32), part.rearrange("k p (c t) -> c p k t", t=TOK)[c]).then_inc(y_in[u].sem, 16)
                    if e == EXPERTS - 1:
                        return
                chunks(sp, e * CHUNKS, load_y, None)
                if 1 <= e < EXPERTS - 1:
                    load_expert(e + 1)

        @block.gpsimd
        def _(pool):
            g2_done.give_credit(pool)
            out_v = out.rearrange("(c t p) d -> c p t d", p=P, t=TT)
            for e in range(EXPERTS):
                w = e % 2

                def scale_shift(lin, c, u, pair, more):
                    for t in range(TT):
                        pool.wait_ge(u2_ready.sem, u2_ready.at(lin, t + 1))
                        pool.wait_ge(added.sem, added.at(lin, t + 1 - TT))
                        nc.gpsimd.tensor_tensor(v2[:, t], u2[:, t], rows[:, w, 2], ALU.mult).then_inc(g2_done.sem, 1)
                        pool.wait_ge(g2_done.sem, g2_done.at(lin, t + 1))
                        nc.gpsimd.tensor_tensor(v2[:, t], v2[:, t], rows[:, w, 3], ALU.add).then_inc(v2_ready.sem, 1)
                chunks(pool, e * CHUNKS, scale_shift, None)

        @block.tensor
        def _(pe):
            m1.give_credit(pe)
            m2.give_credit(pe)
            turned_ready.give_credit(pe)

            def product(acc, left_hi, left_lo, w, m, t):
                i = 0
                for left, right in ((left_hi, w_hi), (left_hi, w_lo), (left_lo, w_hi)):
                    for k in range(KT):
                        mm = nc.tensor.matmul(acc[:, :], left[:, k, t * P:(t + 1) * P], right[:, w, m, k, :],
                                              start=i == 0, stop=i == 11)
                        i += 1
                return mm

            for e in range(EXPERTS):
                w = e % 2
                pe.wait_ge(weights_in[w], 16 * 8 * (e // 2 + 1))

                def first_products(lin, u, pair):
                    pe.wait_ge(y_in[u].sem, y_in[u].at(pair, 2))
                    for t in range(TT):
                        pe.wait_ge(b1_added.sem, b1_added.at(lin, t + 1 - TT))
                        product(acc1[t], yt_hi[:, u], yt_lo[:, u], w, 0, t).then_inc(m1.sem, 1)

                def step(lin, c, u, pair, more):
                    for a in range(2):
                        pe.wait_ge(u1_ready.sem, u1_ready.at(lin, TT))
                        pe.wait_ge(relu_banks.sem, relu_banks.at(lin, a - 1))
                        for k in (2 * a, 2 * a + 1):
                            for t in range(TT):
                                mm = nc.tensor.transpose(turned[a][:, k % 2, t * P:(t + 1) * P],
                                                         u1[:, t, k * P:(k + 1) * P], ident[:, :])
                        mm.then_inc(turned_ready.sem, 1)
                    if more:
                        first_products(lin + 1, 1 - u, pair + (1 if u == 1 else 0))
                    pe.wait_ge(lo_ready.sem, lo_ready.at(lin, 1))
                    for t in range(TT):
                        pe.wait_ge(b2_added.sem, b2_added.at(lin, t + 1 - TT))
                        product(acc2[t], ht_hi, ht_lo, w, 1, t).then_inc(m2.sem, 1)

                first_products(e * CHUNKS, 0, e * CHUNKS // 2)
                chunks(pe, e * CHUNKS, step, None)

        @block.scalar
        def _(act):
            act.wait_ge(cols_in, 33)
            relu_banks.give_credit(act)
            u2_ready.give_credit(act)
            for e in range(EXPERTS):
                def normalise(lin, n, src, dst, norm, ready):
                    act.wait_ge(norm.sem, norm.at(lin, 2))
                    nc.scalar.activation(root[:, n, :], mean_var[:, n, :, 1], ACT.Sqrt, bias=eps[:, 0:1]).then_inc(rooted[n].sem, 1)
                    act.wait_ge(norm.sem, norm.at(lin, 4))
                    for t in range(TT):
                        nc.scalar.activation(dst[:, t], src[:, t], ACT.Identity, scale=rstd[:, n, t:t + 1],
                                             bias=neg_mean[:, n, t:t + 1]).then_inc(ready.sem, 1)

                def norm_first(lin):
                    act.wait_ge(turned_ready.sem, turned_ready.at(lin, 0))
                    normalise(lin, 0, t1, u1, norm1, u1_ready)

                def step(lin, c, u, pair, more):
                    act.wait_ge(lo_ready.sem, lo_ready.at(lin, 0))
                    for k in range(KT):
                        if k % 2 == 0:
                            act.wait_ge(turned_ready.sem, turned_ready.at(lin, k // 2 + 1))
                        ins = nc.scalar.activation(relu[:, k, :], turned[k // 2][:, k % 2, :], ACT.Relu,
                                                   scale=cols[:, 0, e, k:k + 1], bias=cols[:, 1, e, k:k + 1])
                        if k % 2:
                            ins.then_inc(relu_banks.sem, 1)
                    act.wait_ge(relu_banks.sem, relu_banks.at(lin, 2))
                    act.wait_ge(m2.sem, m2.at(lin, 0))
                    nc.scalar.activation(ht_hi[:, :, :], relu[:, :, :], ACT.Copy).then_inc(hi_ready.sem, 1)
                    if more:
                        norm_first(lin + 1)
                    act.wait_ge(g2_done.sem, g2_done.at(lin, 0))
                    normalise(lin, 1, t2, u2, norm2, u2_ready)

                norm_first(e * CHUNKS)
                chunks(act, e * CHUNKS, step, None)

        @block.vector
        def _(dve):
            nc.vector.memset(eps[:, :], EPS).then_inc(cols_in, 1)
            b1_added.give_credit(dve)
            b2_added.give_credit(dve)
            lo_ready.give_credit(dve)
            added.give_credit(dve)
            for e in range(EXPERTS):
                w = e % 2
                dve.wait_ge(weights_in[w], 16 * 8 * (e // 2 + 1))

                def statistics(lin, n, acc, row, t_sb, done, added_row, norm, ready):
                    for t in range(TT):
                        dve.wait_ge(done.sem, done.at(lin, t + 1))
                        nc.vector.tensor_tensor(t_sb[:, t], acc[t][:, :], rows[:, w, row], ALU.add).then_inc(added_row.sem, 1)
                    for t in range(TT):
                        dve.wait_ge(added_row.sem, added_row.at(lin, t + 1))
                        last = nc.vector.bn_stats(stats[:, n, t, :], t_sb[:, t])
                    last.then_inc(norm.sem, 1)
                    dve.wait_ge(norm.sem, norm.at(lin, 1))
                    dve.sem_inc(waited.sem, 1)
                    for t in range(TT):
                        last = nc.vector.bn_aggr(mean_var[:, n, t, :], stats[:, n, t, :])
                    last.then_inc(norm.sem, 1)
                    dve.wait_ge(norm.sem, norm.at(lin, 2))
                    dve.wait_ge(rooted[n].sem, rooted[n].at(lin, 1))
                    nc.vector.reciprocal(rstd[:, n, :], root[:, n, :]).then_inc(norm.sem, 1)
                    dve.wait_ge(norm.sem, norm.at(lin, 3))
                    nc.vector.scalar_tensor_tensor(neg_mean[:, n, :], mean_var[:, n, :, 0], -1.0, rstd[:, n, :],
                                                   ALU.mult, ALU.mult).then_inc(norm.sem, 1)

                def stats_first(lin):
                    dve.wait_ge(u1_ready.sem, u1_ready.at(lin, 0))
                    statistics(lin, 0, acc1, 0, t1, m1, b1_added, norm1, u1_ready)

                def step(lin, c, u, pair, more):
                    dve.wait_ge(hi_ready.sem, hi_ready.at(lin, 1))
                    nc.vector.tensor_tensor(ht_lo[:, :, :], relu[:, :, :], ht_hi[:, :, :].bitcast(F32),
                                            ALU.subtract).then_inc(lo_ready.sem, 1)
                    if more:
                        stats_first(lin + 1)
                    dve.wait_ge(u2_ready.sem, u2_ready.at(lin, 0))
                    statistics(lin, 1, acc2, 1, t2, m2, b2_added, norm2, u2_ready)
                    for t in range(TT):
                        dve.wait_ge(v2_ready.sem, v2_ready.at(lin, t + 1))
                        tile = base[:, bass.ds(c * TT + t, 1), :].rearrange("p o d -> p (o d)")
                        gate = gates[:, bass.ds(c * TT + t, 1), e:e + 1].rearrange("p o d -> p (o d)")
                        nc.vector.scalar_tensor_tensor(tile, v2[:, t], gate, tile, ALU.mult, ALU.add).then_inc(added.sem, 1)

                stats_first(e * CHUNKS)
                chunks(dve, e * CHUNKS, step, None)


def store_out(nc, base, out):
    with ExitStack() as ctx:
        stored = nc.alloc_semaphore("out_stored")
        block = ctx.enter_context(nc.Block())

        @block.sync
        def _(sp):
            v = out.rearrange("(n p) d -> p n d", p=P)
            for n in range(8):
                sp.dma_start(v[:, 4 * n:4 * n + 4], base[:, 4 * n:4 * n + 4]).then_inc(stored, 16)
            sp.wait_ge(stored, 128)


def in_phase(nc, phase, *args):
    with nc.cleanup_on_exit():
        phase(nc, *args)


def build_decoder(nc, a, out):
    tokens = BATCH * SEQ
    dram = lambda n, shape, dt=F32: nc.dram_tensor(n, shape, dt).ap()
    x = a["x"].rearrange("b s d -> (b s) d")
    ctx_in = a["ctx_1024"].rearrange("b s d -> (b s) d")
    out_rows = out.rearrange("b s d -> (b s) d")
    BG = BATCH * HG
    scale = DK ** -0.5
    with ExitStack() as ctx:
        ident = ctx.enter_context(nc.sbuf_tensor("ident", [P, P], F32))
        mask = ctx.enter_context(nc.sbuf_tensor("mask", [P, P], F32))
        neg_half = ctx.enter_context(nc.sbuf_tensor("neg_half", [P, TPC], F32))
        in_phase(nc, build_constants, ident, mask, neg_half)

        q1 = [dram(f"q1_{n}", (BG, P, SEQ)) for n in ("hi", "lo")]
        k1 = [dram(f"k1_{n}", (BG, P, SEQ)) for n in ("hi", "lo")]
        v1 = dram("v1", (BG, SEQ, P), F32)
        attn1 = dram("attn1", (BG, P, SEQ), F32)
        x1 = dram("x1", (tokens, D), F32)
        q2 = [dram(f"q2_{n}", (BG, P, SEQ)) for n in ("hi", "lo")]
        k2 = [dram(f"k2_{n}", (BG, P, CTX)) for n in ("hi", "lo")]
        v2 = dram("v2", (BG, CTX, P), F32)
        attn2 = dram("attn2", (BG, P, SEQ), F32)
        x2 = dram("x2", (tokens, D), F32)
        y = [dram(f"y_{n}", (KT, P, tokens)) for n in ("hi", "lo")]
        we = [dram(f"we_{n}", (EXPERTS, 2, D, D)) for n in ("hi", "lo")]

        in_phase(nc, project, "qkv1", x, 2, True,
                [(a["L0_attn_q_heads"], True), (a["L0_attn_k_heads"], True), (a["L0_attn_v_heads"], True)],
                [("T", q1[0], q1[1], scale), ("T", k1[0], k1[1], 1.0), ("N", v1)], ident, neg_half)
        in_phase(nc, attend, "self", q1, k1, v1, attn1, SEQ, True, ident, mask)
        in_phase(nc, project_out, "out1", attn1, (a["L0_attn_output_proj"], True), None, x, x1, ident)
        in_phase(nc, project, "q2", x1, 2, True, [(a["L0_xattn_W_q"], False)], [("T", q2[0], q2[1], scale)], ident, neg_half)
        in_phase(nc, project, "kv2", ctx_in, 4, False, [(a["L0_xattn_W_k"], False), (a["L0_xattn_W_v"], False)],
                [("T", k2[0], k2[1], 1.0), ("N", v2)], ident, neg_half)
        in_phase(nc, attend, "cross", q2, k2, v2, attn2, CTX, False, ident, mask)
        in_phase(nc, project_out, "out2", attn2, (a["L0_xattn_W_o"], False), a["L0_xattn_b_o"], x1, x2, ident)
        base = ctx.enter_context(nc.sbuf_tensor("base", [P, tokens // P, D], F32))
        gates = ctx.enter_context(nc.sbuf_tensor("gates", [P, tokens // P, EXPERTS], F32))
        in_phase(nc, route, "route", x2, a["L0_ffn_gate_W"], a["L0_ffn_gate_b"], y[0], y[1], base, gates, ident, neg_half)
        in_phase(nc, split_experts, a["L0_ffn_W1"], a["L0_ffn_W2"], we[0], we[1])
        in_phase(nc, experts, we[0], we[1], [a["L0_ffn_" + n] for n in ("b1", "g1", "be1", "b2", "g2", "be2")],
                y[0], y[1], base, gates, out_rows, ident)
        in_phase(nc, store_out, base, out_rows)


_INS = ["x", "ctx_1024", "L0_attn_q_heads", "L0_attn_k_heads", "L0_attn_v_heads", "L0_attn_output_proj",
        "L0_xattn_W_q", "L0_xattn_W_k", "L0_xattn_W_v", "L0_xattn_W_o", "L0_xattn_b_o",
        "L0_ffn_gate_W", "L0_ffn_gate_b", "L0_ffn_W1", "L0_ffn_b1", "L0_ffn_g1", "L0_ffn_be1",
        "L0_ffn_W2", "L0_ffn_b2", "L0_ffn_g2", "L0_ffn_be2"]


def kernel(**inputs):
    import concourse.bacc as bacc
    from concourse.bass_utils import run_bass_kernel_spmd

    nc = bacc.Bacc("TRN2", target_bir_lowering=False, num_devices=1)
    arrays, args = {}, {}
    for name in _INS:
        arr = np.ascontiguousarray(inputs[name])
        arrays[f"in_{name}"] = arr
        args[name] = nc.dram_tensor(f"in_{name}", arr.shape, mybir.dt.from_np(arr.dtype), kind="ExternalInput").ap()
    out = nc.dram_tensor("out", (BATCH, SEQ, D), F32, kind="ExternalOutput").ap()
    build_decoder(nc, args, out)
    return run_bass_kernel_spmd(nc, [arrays], core_ids=[0]).results[0]["out"]
```

```python
import numpy as np
import concourse.bass as bass
import concourse.mybir as mybir
from contextlib import ExitStack

F32, F32R, BF16 = mybir.dt.float32, mybir.dt.float32r, mybir.dt.bfloat16
ACT = mybir.ActivationFunctionType
ALU = mybir.AluOpType
AX = mybir.AxisListType

P = 128
BATCH, SEQ, CTX = 4, 1024, 2048
D, HEADS, DK = 512, 16, 32
KT = D // P
HG = HEADS // 4
EXPERTS = 4
CH = 512
TPC = CH // P
EPS = 1e-5
MASKED = -2.0 ** 127


class Signal:

    def __init__(self, nc, ctx, name, per, credit=0, step=1):
        self.sem = nc.alloc_semaphore(name)
        self.per, self.credit, self.step = per, credit, step

    def give_credit(self, eng):
        eng.sem_inc(self.sem, self.credit * self.step)

    def at(self, it, n):
        return it * (self.per * self.step) + (n + self.credit) * self.step


def build_constants(nc, ident, ident_b, mask, neg_half):
    with ExitStack() as ctx:
        made = nc.alloc_semaphore("constants_made")
        block = ctx.enter_context(nc.Block())

        @block.gpsimd
        def _(pool):
            pool.memset(ident[:, :], 0.0).then_inc(made, 1)
            pool.memset(mask[:, :], 0.0).then_inc(made, 1)
            pool.memset(neg_half[:, :], -0.5).then_inc(made, 1)
            pool.memset(ident_b[:, :], 0.0).then_inc(made, 1)
            pool.wait_ge(made, 4)
            pool.affine_select(out=ident_b[:, :], in_=ident_b[:, :], compare_op=ALU.not_equal, fill=1.0,
                               base=0, pattern=[[-1, P]], channel_multiplier=1).then_inc(made, 1)
            pool.affine_select(out=ident[:, :], in_=ident[:, :], compare_op=ALU.not_equal, fill=1.0,
                               base=0, pattern=[[-1, P]], channel_multiplier=1).then_inc(made, 1)
            pool.affine_select(out=mask[:, :], in_=mask[:, :], compare_op=ALU.is_ge, fill=MASKED,
                               base=0, pattern=[[-1, P]], channel_multiplier=1).then_inc(made, 1)
            pool.wait_ge(made, 7)


def load_weights(nc, name, weights, hi, lo, ident):
    with ExitStack() as ctx:
        raw = ctx.enter_context(nc.sbuf_tensor(f"{name}_raw", [P, 2, KT, D], F32))
        turned = ctx.enter_context(nc.psum_tensor(f"{name}_turned", [P, KT, D], F32))
        loaded = [nc.alloc_semaphore(f"{name}_loaded{u}") for u in range(2)]
        turned_ready = nc.alloc_semaphore(f"{name}_turned")
        hi_ready = nc.alloc_semaphore(f"{name}_hi")
        lo_ready = nc.alloc_semaphore(f"{name}_lo")
        block = ctx.enter_context(nc.Block())

        @block.sync
        def _(sp):
            for n, (w, _) in enumerate(weights):
                if n >= 2:
                    sp.wait_ge(lo_ready, n - 1)
                sp.dma_start(raw[:, n % 2], w.rearrange("(k p) n -> p k n", p=P)).then_inc(loaded[n % 2], 16)

        @block.tensor
        def _(pe):
            done = 0
            for n, (_, transposed) in enumerate(weights):
                if not transposed:
                    continue
                pe.wait_ge(loaded[n % 2], 16 * (n // 2 + 1))
                if n:
                    pe.wait_ge(lo_ready, n)
                for k in range(KT):
                    for m in range(KT):
                        mm = nc.tensor.transpose(turned[:, k, m * P:(m + 1) * P],
                                                 raw[:, n % 2, m, k * P:(k + 1) * P], ident[:, :])
                done += 1
                mm.then_inc(turned_ready, 1)

        def source(eng, n, seen):
            if weights[n][1]:
                eng.wait_ge(turned_ready, seen + 1)
                return turned[:, :, :], seen + 1
            eng.wait_ge(loaded[n % 2], 16 * (n // 2 + 1))
            return raw[:, n % 2], seen

        @block.scalar
        def _(act):
            seen = 0
            for n in range(len(weights)):
                src, seen = source(act, n, seen)
                nc.scalar.activation(hi[:, n], src, ACT.Copy).then_inc(hi_ready, 1)

        @block.vector
        def _(dve):
            seen = 0
            for n in range(len(weights)):
                src, seen = source(dve, n, seen)
                dve.wait_ge(hi_ready, n + 1)
                nc.vector.tensor_tensor(lo[:, n], src, hi[:, n].bitcast(F32),
                                        ALU.subtract).then_inc(lo_ready, 1)


def project(nc, name, src, chunks, norm, weights, outs, ident, neg_half):
    NOUT = 4 * len(weights)
    with ExitStack() as ctx:
        sb = lambda n, shape, dt=F32: ctx.enter_context(nc.sbuf_tensor(f"{name}_{n}", shape, dt))
        sig = lambda n, per, credit=0, step=1: Signal(nc, ctx, f"{name}_{n}", per, credit, step)
        w_hi = sb("w_hi", [P, len(weights), KT, D], F32R)
        w_lo = sb("w_lo", [P, len(weights), KT, D], F32R)
        load_weights(nc, f"{name}_w", weights, w_hi, w_lo, ident)
        x_in = sb("x_in", [P, 2, TPC, D])
        x_n = sb("x_n", [P, 2, TPC, D]) if norm else x_in
        stats = sb("stats", [P, TPC, 6])
        mean_var = sb("mean_var", [P, TPC, 2])
        var_eps = sb("var_eps", [P, TPC])
        rstd = sb("rstd", [P, TPC])
        xt_hi = sb("xt_hi", [P, 2, KT, CH], F32R)
        xt_lo = sb("xt_lo", [P, 2, KT, CH], F32R)
        out_hi = sb("out_hi", [P, 4, D], F32R)
        out_lo = sb("out_lo", [P, 4, D], F32R)
        out_n = sb("out_n", [P, 4, D])
        turned = [ctx.enter_context(nc.psum_tensor(f"{name}_turned{n}", [P, KT, P], F32)) for n in range(2)]
        acc = [ctx.enter_context(nc.psum_tensor(f"{name}_acc{n}", [P, D], F32)) for n in range(4)]

        loaded = [sig(f"loaded{u}", chunks // 2, step=16) for u in range(2)]
        step = sig("dve_step", 3 * chunks)
        rooted = sig("rooted", chunks)
        waited = sig("waited", 1)
        normed = sig("normed", chunks, 2)
        turned_ready = sig("turned_ready", TPC * chunks, 8)
        hi_ready = sig("xt_hi_ready", TPC * chunks)
        lo_ready = sig("xt_lo_ready", TPC * chunks, 2)
        acc_ready = sig("acc_ready", NOUT * chunks, 2 * NOUT)
        NSPLIT = 4 * sum(o[0] == "T" for o in outs)
        out_hi_ready = sig("out_hi_ready", NSPLIT * chunks)
        out_lo_ready = sig("out_lo_ready", NOUT * chunks, 4)
        dmas = lambda n: 2 if n < NSPLIT else 1
        stores = [sum(dmas(n) for n in range(s, NOUT, 4)) for s in range(4)]
        stored = [sig(f"stored{s}", stores[s] * chunks, 4, step=16) for s in range(4)]
        block = ctx.enter_context(nc.Block())
        src_v = src.rearrange("(c t p) d -> c p t d", p=P, t=TPC)
        TURN = {t * NOUT // TPC: t for t in range(TPC)}

        def passes(eng, chunk):
            with eng.Fori(0, BATCH - 1) as it:
                for u in range(chunks):
                    chunk(it, u, True)
            for u in range(chunks):
                chunk(BATCH - 1, u, False)

        def stores_before(s, u, n):
            return u * stores[s] + sum(dmas(m) for m in range(s, n, 4))

        @block.sync
        def _(sp):
            def load(it, u):
                if norm:
                    sp.wait_ge(normed.sem, normed.at(it, u - 1))
                else:
                    sp.wait_ge(turned_ready.sem, turned_ready.at(it, TPC * (u - 1)))
                sp.dma_start(x_in[:, u % 2], src_v[it * chunks + u]).then_inc(loaded[u % 2].sem, 16)

            def chunk(it, u, more):
                for n in range(NOUT):
                    kind, g, s = outs[n // 4][0], n % 4, n % 4
                    if n == 1 and (more or u + 2 < chunks):
                        load(it, u + 2)
                    sp.wait_ge(out_lo_ready.sem, out_lo_ready.at(it, u * NOUT + n + 1))
                    if kind == "T":
                        tok = slice(u * CH, (u + 1) * CH)
                        sp.dma_start(outs[n // 4][1][it * HG + g, :, tok], out_hi[:, s].bitcast(F32)).then_inc(stored[s].sem, 16)
                        sp.dma_start(outs[n // 4][2][it * HG + g, :, tok], out_lo[:, s].bitcast(F32)).then_inc(stored[s].sem, 16)
                    else:
                        t0 = u * CH + g * P
                        rows = outs[n // 4][1].rearrange("(b h) t d -> b t h d", h=HG)[it, t0:t0 + P]
                        sp.dma_start(rows, out_n[:, s].rearrange("p (h d) -> p h d", h=HG)).then_inc(stored[s].sem, 16)

            for s in range(4):
                stored[s].give_credit(sp)
            load(0, 0)
            load(0, 1)
            passes(sp, chunk)
            for s in range(4):
                sp.wait_ge(stored[s].sem, stored[s].at(BATCH, 0))

        @block.gpsimd
        def _(pool):
            if not norm:
                return

            def root(it, u):
                pool.wait_ge(step.sem, step.at(it, 3 * u + 3))
                pool.wait_ge(normed.sem, normed.at(it, u))
                nc.gpsimd.tensor_tensor(rstd[:, :], var_eps[:, :], neg_half[:, :], ALU.pow).then_inc(rooted.sem, 1)

            root(0, 0)
            root(0, 1)
            passes(pool, lambda it, u, more: root(it, u + 2) if more or u + 2 < chunks else None)

        @block.vector
        def _(dve):
            normed.give_credit(dve)
            lo_ready.give_credit(dve)
            out_lo_ready.give_credit(dve)

            def variance(it, u):
                dve.wait_ge(loaded[u % 2].sem, loaded[u % 2].at(it, u // 2 + 1))
                for t in range(TPC):
                    last = nc.vector.bn_stats(stats[:, t, :], x_in[:, u % 2, t, :])
                last.then_inc(step.sem, 1)
                dve.wait_ge(step.sem, step.at(it, 3 * u + 1))
                dve.sem_inc(waited.sem, 1)
                for t in range(TPC):
                    last = nc.vector.bn_aggr(mean_var[:, t, :], stats[:, t, :])
                last.then_inc(step.sem, 1)
                dve.wait_ge(step.sem, step.at(it, 3 * u + 2))
                nc.vector.tensor_scalar(var_eps[:, :], mean_var[:, :, 1], EPS, None, ALU.add).then_inc(step.sem, 1)

            def normalise(it, u):
                dve.wait_ge(rooted.sem, rooted.at(it, u + 1))
                dve.wait_ge(turned_ready.sem, turned_ready.at(it, TPC * (u - 1)))
                for t in range(TPC):
                    last = nc.vector.tensor_scalar(x_n[:, u % 2, t, :], x_in[:, u % 2, t, :],
                                                   mean_var[:, t, 0:1], rstd[:, t:t + 1],
                                                   ALU.subtract, ALU.mult)
                last.then_inc(normed.sem, 1)

            def split_lo(it, u, t):
                dve.wait_ge(hi_ready.sem, hi_ready.at(it, TPC * u + t + 1))
                nc.vector.tensor_tensor(xt_lo[:, u % 2, :, t * P:(t + 1) * P], turned[t % 2][:, :, :],
                                        xt_hi[:, u % 2, :, t * P:(t + 1) * P].bitcast(F32),
                                        ALU.subtract).then_inc(lo_ready.sem, 1)

            def take_out(it, u, n):
                s = n % 4
                o = outs[n // 4]
                if o[0] == "T":
                    dve.wait_ge(out_hi_ready.sem, out_hi_ready.at(it, u * NSPLIT + n + 1))
                    dve.wait_ge(stored[s].sem, stored[s].at(it, stores_before(s, u, n)))
                    nc.vector.scalar_tensor_tensor(out_lo[:, s], acc[s][:, :], o[3], out_hi[:, s].bitcast(F32),
                                                   ALU.mult, ALU.subtract).then_inc(out_lo_ready.sem, 1)
                else:
                    dve.wait_ge(acc_ready.sem, acc_ready.at(it, u * NOUT + n + 1))
                    dve.wait_ge(stored[s].sem, stored[s].at(it, stores_before(s, u, n)))
                    nc.vector.tensor_copy(out_n[:, s], acc[s][:, :]).then_inc(out_lo_ready.sem, 1)

            def chunk(it, u, more):
                for n in range(NOUT):
                    if n in TURN and (more or u + 1 < chunks):
                        split_lo(it, u + 1, TURN[n])
                    take_out(it, u, n)
                    if norm and (more or u + 2 < chunks):
                        if n == 0:
                            variance(it, u + 2)
                        if n == NOUT - 1:
                            normalise(it, u + 2)

            if norm:
                variance(0, 0)
                normalise(0, 0)
            for t in range(TPC):
                split_lo(0, 0, t)
            if norm:
                variance(0, 1)
                normalise(0, 1)
            passes(dve, chunk)

        @block.scalar
        def _(act):
            def split_hi(it, u, t):
                act.wait_ge(turned_ready.sem, turned_ready.at(it, TPC * u + t + 1))
                if t == 0:
                    act.wait_ge(acc_ready.sem, acc_ready.at(it, (u - 1) * NOUT))
                nc.scalar.activation(xt_hi[:, u % 2, :, t * P:(t + 1) * P], turned[t % 2][:, :, :],
                                     ACT.Copy).then_inc(hi_ready.sem, 1)

            def chunk(it, u, more):
                for n in range(NOUT):
                    if n in TURN and (more or u + 1 < chunks):
                        split_hi(it, u + 1, TURN[n])
                    s = n % 4
                    o = outs[n // 4]
                    if o[0] == "T":
                        act.wait_ge(acc_ready.sem, acc_ready.at(it, u * NOUT + n + 1))
                        act.wait_ge(stored[s].sem, stored[s].at(it, stores_before(s, u, n)))
                        nc.scalar.activation(out_hi[:, s], acc[s][:, :], ACT.Copy,
                                             scale=o[3]).then_inc(out_hi_ready.sem, 1)

            for t in range(TPC):
                split_hi(0, 0, t)
            passes(act, chunk)

        @block.tensor
        def _(pe):
            turned_ready.give_credit(pe)
            acc_ready.give_credit(pe)

            def turn(it, u, t):
                if t == 0 and norm:
                    pe.wait_ge(normed.sem, normed.at(it, u + 1))
                elif t == 0:
                    pe.wait_ge(loaded[u % 2].sem, loaded[u % 2].at(it, u // 2 + 1))
                pe.wait_ge(lo_ready.sem, lo_ready.at(it, TPC * u + t - 1))
                for k in range(KT):
                    mm = nc.tensor.transpose(turned[t % 2][:, k, :], x_n[:, u % 2, t, k * P:(k + 1) * P], ident[:, :])
                mm.then_inc(turned_ready.sem, 1)

            def chunk(it, u, more):
                pe.wait_ge(lo_ready.sem, lo_ready.at(it, TPC * (u + 1)))
                for n in range(NOUT):
                    w, g, s = n // 4, n % 4, n % 4
                    if n in TURN and (more or u + 1 < chunks):
                        turn(it, u + 1, TURN[n])
                    pe.wait_ge(out_lo_ready.sem, out_lo_ready.at(it, u * NOUT + n - 3))
                    cols = slice(g * P, (g + 1) * P)
                    i = 0
                    for a, b in ((0, 0), (0, 1), (1, 0)):
                        for k in range(KT):
                            x_part = (xt_hi, xt_lo)[a][:, u % 2, k, :]
                            w_part = (w_hi, w_lo)[b][:, w, k, :]
                            if outs[w][0] == "T":
                                mm = nc.tensor.matmul(acc[s][:, :], w_part[:, cols], x_part,
                                                      start=i == 0, stop=i == 11)
                            else:
                                mm = nc.tensor.matmul(acc[s][:, :], x_part[:, cols], w_part,
                                                      start=i == 0, stop=i == 11)
                            i += 1
                    mm.then_inc(acc_ready.sem, 1)

            for t in range(TPC):
                turn(0, 0, t)
            passes(pe, chunk)


def attend(nc, name, q_parts, k_parts, v, out_t, keys, causal, ident, ident_b, mask):
    HALVES = keys // 1024
    QC = SEQ // 256
    steps = [(w, qc, half) for w in range(2) for qc in range(QC) for half in range(HALVES)]
    G = len(steps)
    NCH = 2 * QC
    SETS = keys // P
    PASSES = BATCH * HG // 2
    GROW, WEIGH, SPREAD, SPREAD_COPY = (1, 3, 4, 5) if HALVES == 2 else (0, 1, 2, 3)
    with ExitStack() as ctx:
        sb = lambda n, shape, dt=F32: ctx.enter_context(nc.sbuf_tensor(f"{name}_{n}", shape, dt))
        sig = lambda n, per, credit=0, step=1: Signal(nc, ctx, f"{name}_{n}", per, credit, step)
        q_st = sb("q_stack", [P, 2, 4, SEQ], F32R)
        k_st = sb("k_stack", [P, 2, 4, keys], F32R)
        v_sb = sb("v", [P, 2, SETS, P])
        probs = sb("probs", [P, 2, 8, 1024])
        probs_t = sb("probs_t", [P, 2, 4, 256])
        neg_max = sb("neg_max", [P, 2, HALVES, 8])
        sums = sb("sums", [P, 2, HALVES, 8])
        shift = sb("shift", [P, 2, 8])
        grow = sb("grow", [P, 2, 8])
        total = sb("total", [P, 2, 8])
        weight = sb("weight", [P, 2, HALVES, 8])
        w_sb = sb("w_sb", [P, HALVES * 256])
        part = sb("part", [P, 2, HALVES, 256])
        mixed = sb("mixed", [P, 2, 256]) if HALVES == 2 else part[:, :, 0, :]
        scores = [ctx.enter_context(nc.psum_tensor(f"{name}_scores{n}", [P, 1024], F32)) for n in range(2)]
        turned = [ctx.enter_context(nc.psum_tensor(f"{name}_turned{n}", [P, 2, 256], F32)) for n in range(2)]
        out_ps = [ctx.enter_context(nc.psum_tensor(f"{name}_out{n}", [P, 2, 256], F32)) for n in range(2)]

        def tiles(s):
            return 2 * steps[s % G][1] + 2 if causal else 8

        def tiles_before(s):
            return sum(tiles(m) for m in range(s))
        NT = tiles_before(G)

        def width(n):
            _, qc, _ = steps[n // 8 % G]
            return (2 * qc + n % 8 // 4 + 1) * P if causal else 1024

        def first_query(s, k):
            return P if causal and k == tiles(s) - 1 else 0

        loaded = [sig(f"loaded{w}", 8 + SETS // 8, step=16) for w in range(2)]
        scored = sig("scored", 8 * G)
        maxed = sig("maxed", 8 * G)
        exped = sig("exped", 8 * G, 2)
        turned_r = [sig(f"turned_ready{a}", NT, a) for a in range(2)]
        copied = [sig(f"copied{a}", NT, 1) for a in range(2)]
        pv_done = sig("pv_done", NT, 16)
        prep = sig("weights_prep", 5 * NCH)
        grown = sig("grown", NCH)
        waited = sig("waited", 1)
        totals = sig("totals", NCH)
        weighed = sig("weighed", NCH, 1)
        spread = sig("spread", NCH, 2)
        spread_sb = sig("spread_sb", NCH, 1)
        scaled = sig("scaled", NCH, 2)
        mixed_r = sig("mixed_ready", NCH, 2)
        stored = [sig(f"stored{c}", NCH // 2, 1, step=16) for c in range(2)]
        block = ctx.enter_context(nc.Block())

        def load_heads(sp, bh, w):
            for r in range(4):
                rows = slice(32 * r, 32 * r + 32)
                sp.dma_start(q_st[rows, w].bitcast(F32), q_parts[r // 2][bh].rearrange("(h p) t -> p h t", p=DK)).then_inc(loaded[w].sem, 16)
                sp.dma_start(k_st[rows, w].bitcast(F32), k_parts[r % 2][bh].rearrange("(h p) t -> p h t", p=DK)).then_inc(loaded[w].sem, 16)
            for k in range(0, SETS, 8):
                sp.dma_start(v_sb[:, w, k:k + 8], v[bh, k * P:(k + 8) * P].rearrange("(k p) d -> p k d", p=P)).then_inc(loaded[w].sem, 16)

        @block.sync
        def _(sp):
            for c in range(2):
                stored[c].give_credit(sp)
            load_heads(sp, 0, 0)

            def store(it, w):
                ready = mixed_r if HALVES == 2 else scaled
                for qc in range(QC):
                    c = w * QC + qc
                    sp.wait_ge(ready.sem, ready.at(it, c + 1))
                    sp.dma_start(out_t[it * 2 + w, :, qc * 256:(qc + 1) * 256], mixed[:, c % 2]).then_inc(stored[c % 2].sem, 16)

            def one_pass(it, more):
                sp.wait_ge(pv_done.sem, pv_done.at(it, 0))
                load_heads(sp, it * 2 + 1, 1)
                store(it, 0)
                if more:
                    sp.wait_ge(pv_done.sem, pv_done.at(it, tiles_before(G // 2)))
                    load_heads(sp, it * 2 + 2, 0)
                store(it, 1)
            with sp.Fori(0, PASSES - 1) as it:
                one_pass(it, True)
            one_pass(PASSES - 1, False)
            for c in range(2):
                sp.wait_ge(stored[c].sem, stored[c].at(PASSES, 0))

        @block.gpsimd
        def _(pool):
            if HALVES == 1:
                return
            mixed_r.give_credit(pool)
            with pool.Fori(0, PASSES) as it:
                def weights(c):
                    cp = c % 2
                    pool.wait_ge(exped.sem, exped.at(it, 16 * (c + 1)))
                    for a in range(2):
                        nc.gpsimd.tensor_tensor(shift[:, a, :], neg_max[:, cp, a, :], neg_max[:, cp, 1 - a, :],
                                                ALU.subtract).then_inc(prep.sem, 1)
                    pool.wait_ge(prep.sem, prep.at(it, 5 * c + 2))
                    pool.sem_inc(waited.sem, 1)
                    nc.gpsimd.tensor_scalar(shift[:, :, :], shift[:, :, :], 80.0, -200.0, ALU.min,
                                            ALU.max).then_inc(prep.sem, 1)
                    pool.wait_ge(grown.sem, grown.at(it, c + 1))
                    pool.wait_ge(weighed.sem, weighed.at(it, c))
                    for a in range(2):
                        nc.gpsimd.tensor_tensor(total[:, a, :], grow[:, a, :], sums[:, cp, 1 - a, :],
                                                ALU.mult).then_inc(prep.sem, 1)
                    pool.wait_ge(prep.sem, prep.at(it, 5 * c + 5))
                    nc.gpsimd.tensor_tensor(total[:, :, :], total[:, :, :], sums[:, cp, :, :],
                                            ALU.add).then_inc(totals.sem, 1)

                def finish(c):
                    cp = c % 2
                    pool.wait_ge(scaled.sem, scaled.at(it, c + 1))
                    pool.wait_ge(stored[cp].sem, stored[cp].at(it, c // 2))
                    nc.gpsimd.tensor_tensor(mixed[:, cp], part[:, cp, 0, :], part[:, cp, 1, :],
                                            ALU.add).then_inc(mixed_r.sem, 1)
                for c in range(NCH):
                    weights(c)
                    finish(c)

        def chunk_ends(s):
            return s // HALVES if s % HALVES == HALVES - 1 else None

        @block.tensor
        def _(pe):
            pv_done.give_credit(pe)
            spread.give_credit(pe)
            turned_r[1].give_credit(pe)

            def score(it, n):
                w, qc, half = steps[n // 8 % G]
                h, t = n % 4, n % 8 // 4
                if n % (4 * G) == 0:
                    pe.wait_ge(loaded[w].sem, loaded[w].at(it, (n // (8 * G) + 1) * loaded[w].per))
                pe.wait_ge(exped.sem, exped.at(it, n - 1))
                q0 = qc * 256 + t * P
                for k0 in range(0, width(n), 512):
                    kn = min(512, width(n) - k0)
                    mm = nc.tensor.matmul(scores[n % 2][:, k0:k0 + kn], q_st[:, w, h, q0:q0 + P],
                                          k_st[:, w, h, half * 1024 + k0:half * 1024 + k0 + kn],
                                          start=True, stop=not (causal and k0 + kn == width(n)))
                if causal:
                    mm = nc.tensor.matmul(scores[n % 2][:, width(n) - P:width(n)], ident_b[:, :], mask[:, :],
                                          start=False, stop=True)
                mm.then_inc(scored.sem, 1)

            def turn(it, s, k):
                n = tiles_before(s) + k
                if k == 0:
                    pe.wait_ge(exped.sem, exped.at(it, 8 * (s + 1)))
                for a in range(2):
                    pe.wait_ge(copied[a].sem, copied[a].at(it, n))
                    for h in (2 * a, 2 * a + 1):
                        for t in range(first_query(s, k) // P, 2):
                            mm = nc.tensor.transpose(turned[a][:, h % 2, t * P:(t + 1) * P],
                                                     probs[:, s % 2, 4 * t + h, k * P:(k + 1) * P], ident[:, :])
                    mm.then_inc(turned_r[a].sem, 1)

            def attend_tile(it, s, k):
                w, qc, half = steps[s]
                n = tiles_before(s) + k
                c = s // HALVES
                if k == 0 and half == 0:
                    pe.wait_ge(spread_sb.sem, spread_sb.at(it, c))
                    pe.wait_ge(scaled.sem, scaled.at(it, c - 1))
                for a in range(2):
                    pe.wait_ge(copied[a].sem, copied[a].at(it, n + 1))
                q0 = first_query(s, k)
                for h in range(4):
                    mm = nc.tensor.matmul(out_ps[c % 2][32 * h:32 * h + 32, half, q0:],
                                          v_sb[:, w, 8 * half + k, 32 * h:32 * h + 32],
                                          probs_t[:, n % 2, h, q0:], start=k == 0, stop=k == tiles(s) - 1,
                                          skip_group_check=True)
                mm.then_inc(pv_done.sem, 1)

            def spread_weights(it, c):
                pe.wait_ge(weighed.sem, weighed.at(it, c + 1))
                pe.wait_ge(scaled.sem, scaled.at(it, c))
                for a in range(HALVES):
                    for t in range(2):
                        for h in range(4):
                            wt = weight[:, c % 2, a, 4 * t + h:4 * t + h + 1].to_broadcast([P, DK])
                            mm = nc.tensor.matmul(out_ps[(c + 1) % 2][32 * h:32 * h + 32, a, t * P:(t + 1) * P], wt,
                                                  ident[:, :], start=True, stop=True, skip_group_check=True)
                mm.then_inc(spread.sem, 1)

            def one_pass(it, more):
                for s in range(G):
                    for j in range(8):
                        n = 8 * (s + 1) + j + 1
                        if n < 8 * G or more:
                            score(it, n)
                        if j < tiles(s):
                            turn(it, s, j)
                        if j == 0 and s > 0 and tiles(s - 1) == 8:
                            attend_tile(it, s - 1, 7)
                        if 0 < j <= tiles(s):
                            attend_tile(it, s, j - 1)
                        if j == SPREAD and chunk_ends(s) is not None:
                            spread_weights(it, chunk_ends(s))
                attend_tile(it, G - 1, tiles(G - 1) - 1)

            for n in range(9):
                score(0, n)
            with pe.Fori(0, PASSES - 1) as it:
                one_pass(it, True)
            one_pass(PASSES - 1, False)

        def copy_turned(eng, copy, it, s, k, a):
            n = tiles_before(s) + k
            eng.wait_ge(turned_r[a].sem, turned_r[a].at(it, n + 1))
            eng.wait_ge(pv_done.sem, pv_done.at(it, n - 1))
            q0 = first_query(s, k)
            copy(probs_t[:, n % 2, 2 * a:2 * a + 2, q0:], turned[a][:, :, q0:]).then_inc(copied[a].sem, 1)

        @block.scalar
        def _(act):
            exped.give_credit(act)
            copied[0].give_credit(act)
            spread_sb.give_credit(act)

            def exp_piece(it, n):
                s, j = n // 8, n % 8
                half, c = s % HALVES, s // HALVES
                act.wait_ge(maxed.sem, maxed.at(it, n + 1))
                if j == 0 and s > 0:
                    act.wait_ge(turned_r[1].sem, turned_r[1].at(it, tiles_before(s - 1)))
                nc.scalar.activation(probs[:, s % 2, j, 0:width(n)], scores[n % 2][:, 0:width(n)], ACT.Exp,
                                     bias=neg_max[:, c % 2, half, j:j + 1],
                                     accum_out=sums[:, c % 2, half, j:j + 1]).then_inc(exped.sem, 1)

            def one_pass(it, more):
                for s in range(G):
                    for j in range(8):
                        n = 8 * (s + 1) + j
                        if n < 8 * G or more:
                            exp_piece(it, n)
                        if j < tiles(s):
                            copy_turned(act, lambda o, i: nc.scalar.activation(o, i, ACT.Copy), it, s, j, 0)
                        c = chunk_ends(s)
                        if c is None:
                            continue
                        if HALVES == 2 and j == GROW:
                            act.wait_ge(prep.sem, prep.at(it, 5 * c + 3))
                            nc.scalar.activation(grow[:, :, :], shift[:, :, :], ACT.Exp).then_inc(grown.sem, 1)
                        if j == SPREAD_COPY:
                            act.wait_ge(spread.sem, spread.at(it, c + 1))
                            act.wait_ge(scaled.sem, scaled.at(it, c))
                            nc.scalar.activation(w_sb[:, :], out_ps[(c + 1) % 2][:, 0:HALVES, :],
                                                 ACT.Copy).then_inc(spread_sb.sem, 1)

            for n in range(8):
                exp_piece(0, n)
            with act.Fori(0, PASSES - 1) as it:
                one_pass(it, True)
            one_pass(PASSES - 1, False)

        @block.vector
        def _(dve):
            copied[1].give_credit(dve)
            scaled.give_credit(dve)
            weighed.give_credit(dve)

            def max_piece(it, n):
                s, j = n // 8, n % 8
                half, c = s % HALVES, s // HALVES
                sc = scores[n % 2]
                dve.wait_ge(scored.sem, scored.at(it, n + 1))
                if j == 0 and half == 0:
                    dve.wait_ge(spread.sem, spread.at(it, c - 1))
                nc.vector.tensor_reduce(neg_max[:, c % 2, half, j:j + 1], sc[:, 0:width(n)], AX.X, ALU.max,
                                        negate=True).then_inc(maxed.sem, 1)

            def scale_chunk(it, c):
                dve.wait_ge(spread_sb.sem, spread_sb.at(it, c + 1))
                dve.wait_ge(pv_done.sem, pv_done.at(it, tiles_before((c + 1) * HALVES)))
                if HALVES == 2:
                    dve.wait_ge(mixed_r.sem, mixed_r.at(it, c - 1))
                else:
                    dve.wait_ge(stored[c % 2].sem, stored[c % 2].at(it, c // 2))
                nc.vector.tensor_tensor(part[:, c % 2, :, :], out_ps[c % 2][:, 0:HALVES, :],
                                        w_sb[:, :].rearrange("p (a q) -> p a q", a=HALVES),
                                        ALU.mult).then_inc(scaled.sem, 1)

            def one_pass(it, more):
                for s in range(G):
                    for j in range(8):
                        n = 8 * (s + 1) + j + 1
                        if n < 8 * G or more:
                            max_piece(it, n)
                        if j < tiles(s):
                            copy_turned(dve, lambda o, i: nc.vector.tensor_copy(o, i), it, s, j, 1)
                        if j == 1 and s > 0 and chunk_ends(s - 1) is not None:
                            scale_chunk(it, chunk_ends(s - 1))
                        if j == WEIGH and chunk_ends(s) is not None:
                            c = chunk_ends(s)
                            if HALVES == 2:
                                dve.wait_ge(totals.sem, totals.at(it, c + 1))
                                nc.vector.reciprocal(weight[:, c % 2, :, :], total[:, :, :]).then_inc(weighed.sem, 1)
                            else:
                                dve.wait_ge(exped.sem, exped.at(it, 8 * (c + 1)))
                                nc.vector.reciprocal(weight[:, c % 2, :, :], sums[:, c % 2, :, :]).then_inc(weighed.sem, 1)
                scale_chunk(it, NCH - 1)

            for n in range(9):
                max_piece(0, n)
            with dve.Fori(0, PASSES - 1) as it:
                one_pass(it, True)
            one_pass(PASSES - 1, False)


def project_out(nc, name, attn_t, weight, bias, residual, out, ident):
    with ExitStack() as ctx:
        sb = lambda n, shape, dt=F32: ctx.enter_context(nc.sbuf_tensor(f"{name}_{n}", shape, dt))
        sig = lambda n, per, credit=0, step=1: Signal(nc, ctx, f"{name}_{n}", per, credit, step)
        w_hi = sb("w_hi", [P, 1, KT, D], F32R)
        w_lo = sb("w_lo", [P, 1, KT, D], F32R)
        load_weights(nc, f"{name}_w", [weight], w_hi, w_lo, ident)
        a_in = sb("a_in", [P, 2, KT, CH])
        a_hi = sb("a_hi", [P, 2, KT, CH], F32R)
        a_lo = sb("a_lo", [P, 2, KT, CH], F32R)
        res = sb("res", [P, 2, TPC, D])
        row = sb("row", [P, D])
        y = sb("y", [P, 2, TPC, D])
        acc = [ctx.enter_context(nc.psum_tensor(f"{name}_acc{n}", [P, D], F32)) for n in range(4)]
        loaded = [sig(f"loaded{u}", 2, step=16) for u in range(2)]
        row_loaded = sig("row_loaded", 0)
        biased = sig("biased", 2)
        waited = sig("waited", 1)
        hi_ready = sig("a_hi_ready", 2)
        lo_ready = sig("a_lo_ready", 2, 2)
        acc_ready = sig("acc_ready", 8, 16)
        added = sig("added", 8, 16)
        stored = [sig(f"stored{u}", 1, 1, step=16) for u in range(2)]
        block = ctx.enter_context(nc.Block())

        def passes(eng, chunk):
            with eng.Fori(0, BATCH - 1) as it:
                for u in range(2):
                    chunk(it, u, True)
            for u in range(2):
                chunk(BATCH - 1, u, False)

        res_v = residual.rearrange("(c t p) d -> c p t d", p=P, t=TPC)
        out_v = out.rearrange("(c t p) d -> c p t d", p=P, t=TPC)

        @block.sync
        def _(sp):
            for u in range(2):
                stored[u].give_credit(sp)
            if bias is not None:
                sp.dma_start(row[:, :], bias.rearrange("(o d) -> o d", o=1).to_broadcast([P, D])).then_inc(row_loaded.sem, 16)
            attn_v = attn_t.rearrange("(b g) p t -> b p g t", g=HG)

            def load(it, u):
                b, half = (it, u) if u < 2 else (it + 1, u - 2)
                sp.wait_ge(lo_ready.sem, lo_ready.at(it, u - 1))
                sp.sem_inc(waited.sem, 1)
                sp.wait_ge(added.sem, added.at(it, 4 * (u - 1)))
                sp.dma_start(a_in[:, half], attn_v[b, :, :, half * CH:(half + 1) * CH]).then_inc(loaded[half].sem, 16)
                sp.dma_start(res[:, half], res_v[b * 2 + half]).then_inc(loaded[half].sem, 16)

            def chunk(it, u, more):
                if more or u == 0:
                    load(it, u + 1)
                sp.wait_ge(added.sem, added.at(it, 4 * (u + 1)))
                sp.dma_start(out_v[it * 2 + u], y[:, u]).then_inc(stored[u].sem, 16)

            load(0, 0)
            passes(sp, chunk)
            for u in range(2):
                sp.wait_ge(stored[u].sem, stored[u].at(BATCH, 0))

        @block.scalar
        def _(act):
            def split_hi(it, u):
                act.wait_ge(loaded[u % 2].sem, loaded[u % 2].at(it, 2 * (u // 2 + 1)))
                act.wait_ge(acc_ready.sem, acc_ready.at(it, 4 * (u - 1)))
                nc.scalar.activation(a_hi[:, u % 2], a_in[:, u % 2], ACT.Copy).then_inc(hi_ready.sem, 1)

            split_hi(0, 0)
            passes(act, lambda it, u, more: split_hi(it, u + 1) if more or u == 0 else None)

        @block.vector
        def _(dve):
            lo_ready.give_credit(dve)
            added.give_credit(dve)
            if bias is not None:
                dve.wait_ge(row_loaded.sem, 16)

            def split_lo(it, u):
                dve.wait_ge(hi_ready.sem, hi_ready.at(it, u + 1))
                nc.vector.tensor_tensor(a_lo[:, u % 2], a_in[:, u % 2], a_hi[:, u % 2].bitcast(F32),
                                        ALU.subtract).then_inc(lo_ready.sem, 1)

            def chunk(it, u, more):
                if bias is not None:
                    for t in range(TPC):
                        last = nc.vector.tensor_tensor(res[:, u, t], res[:, u, t], row[:, :], ALU.add)
                    last.then_inc(biased.sem, 1)
                if more or u == 0:
                    split_lo(it, u + 1)
                if bias is not None:
                    dve.wait_ge(biased.sem, biased.at(it, u + 1))
                dve.wait_ge(stored[u].sem, stored[u].at(it, 0))
                for t in range(TPC):
                    dve.wait_ge(acc_ready.sem, acc_ready.at(it, 4 * u + t + 1))
                    nc.vector.tensor_tensor(y[:, u, t], acc[t][:, :], res[:, u, t], ALU.add).then_inc(added.sem, 1)

            split_lo(0, 0)
            passes(dve, chunk)

        @block.tensor
        def _(pe):
            acc_ready.give_credit(pe)
            with pe.Fori(0, BATCH) as it:
                for u in range(2):
                    pe.wait_ge(lo_ready.sem, lo_ready.at(it, u + 1))
                    for t in range(TPC):
                        pe.wait_ge(added.sem, added.at(it, 4 * (u - 1) + t + 1))
                        i = 0
                        for a, w in ((a_hi, w_hi), (a_hi, w_lo), (a_lo, w_hi)):
                            for k in range(KT):
                                mm = nc.tensor.matmul(acc[t][:, :], a[:, u, k, t * P:(t + 1) * P], w[:, 0, k, :],
                                                      start=i == 0, stop=i == 11)
                                i += 1
                        mm.then_inc(acc_ready.sem, 1)


def route(nc, name, src, gate_w, gate_b, y_hi, y_lo, base, gates, ident, neg_half):
    with ExitStack() as ctx:
        sb = lambda n, shape, dt=F32: ctx.enter_context(nc.sbuf_tensor(f"{name}_{n}", shape, dt))
        sig = lambda n, per, credit=0, step=1: Signal(nc, ctx, f"{name}_{n}", per, credit, step)
        gw = sb("gw", [P, KT, EXPERTS])
        gw_hi = sb("gw_hi", [P, KT, EXPERTS], F32R)
        gw_lo = sb("gw_lo", [P, KT, EXPERTS], F32R)
        gb = sb("gb", [EXPERTS, 1])
        earlier = sb("earlier", [P, TPC, EXPERTS, EXPERTS])
        x_in = sb("x_in", [P, 2, TPC, D])
        x_n = sb("x_n", [P, 2, TPC, D])
        stats = sb("stats", [P, TPC, 6])
        mean_var = sb("mean_var", [P, TPC, 2])
        var_eps = sb("var_eps", [P, TPC])
        rstd = sb("rstd", [P, TPC])
        xt_hi = sb("xt_hi", [P, 2, KT, CH], F32R)
        xt_lo = sb("xt_lo", [P, 2, KT, CH], F32R)
        g_rows = sb("g_rows", [EXPERTS, CH])
        g = sb("g", [P, TPC, EXPERTS])
        above = sb("above", [P, TPC, EXPERTS, EXPERTS])
        ties = sb("ties", [P, TPC, EXPERTS, EXPERTS])
        rank = sb("rank", [P, TPC, EXPERTS])
        top = sb("top", [P, TPC])
        e_g = sb("e_g", [P, TPC, EXPERTS])
        turned = [ctx.enter_context(nc.psum_tensor(f"{name}_turned{n}", [P, KT, P], F32)) for n in range(2)]
        g_ps = ctx.enter_context(nc.psum_tensor(f"{name}_g_ps", [P, CH], F32))
        gt_ps = ctx.enter_context(nc.psum_tensor(f"{name}_gt_ps", [P, TPC, P], F32))
        small = nc.alloc_semaphore(f"{name}_small")
        earlier_made = nc.alloc_semaphore(f"{name}_earlier_made")
        gw_hi_ready = nc.alloc_semaphore(f"{name}_gw_hi_ready")
        gw_lo_ready = nc.alloc_semaphore(f"{name}_gw_lo_ready")
        loaded = [sig(f"loaded{u}", 1, step=16) for u in range(2)]
        step = sig("dve_step", 2 * 12)
        rooted = sig("rooted", 2)
        waited = sig("waited", 1)
        normed = sig("normed", 2, 1)
        based = sig("based", 2, 2)
        turned_ready = sig("turned_ready", 2 * TPC, 8)
        hi_ready = sig("hi_ready", 2 * TPC)
        lo_ready = sig("lo_ready", 2 * TPC, 2)
        scored = sig("scored", 2, 2)
        rows = sig("rows", 2, 1)
        g_turned = sig("g_turned", 2)
        g_read = sig("g_read", 2, 1)
        less_max = sig("less_max", 2)
        exped = sig("exped", 2)
        stored = [sig(f"stored{u}", 2, 2, step=16) for u in range(2)]
        block = ctx.enter_context(nc.Block())
        src_v = src.rearrange("(c t p) d -> c p t d", p=P, t=TPC)

        def passes(eng, chunk):
            with eng.Fori(0, BATCH - 1) as it:
                for u in range(2):
                    chunk(it, u, True)
            for u in range(2):
                chunk(BATCH - 1, u, False)

        @block.sync
        def _(sp):
            sp.dma_start(gw[:, :, :], gate_w.rearrange("(k p) e -> p k e", p=P)).then_inc(small, 16)
            sp.dma_start(gb[:, :], gate_b.rearrange("(e o) -> e o", o=1)).then_inc(small, 16)
            for u in range(2):
                stored[u].give_credit(sp)

            def load(it, u):
                sp.wait_ge(based.sem, based.at(it, u - 1))
                sp.dma_start(x_in[:, u % 2], src_v[it * 2 + u]).then_inc(loaded[u % 2].sem, 16)

            def chunk(it, u, more):
                if more or u == 0:
                    load(it, u + 1)
                sp.wait_ge(lo_ready.sem, lo_ready.at(it, TPC * (u + 1)))
                for part, dst in ((xt_hi, y_hi), (xt_lo, y_lo)):
                    sp.dma_start(dst.rearrange("k p (c t) -> c p k t", t=CH)[it * 2 + u], part[:, u].bitcast(F32)).then_inc(stored[u].sem, 16)

            load(0, 0)
            passes(sp, chunk)
            for u in range(2):
                sp.wait_ge(stored[u].sem, stored[u].at(BATCH, 0))

        @block.gpsimd
        def _(pool):
            based.give_credit(pool)
            pool.memset(earlier[:, :, :, :], 1.0).then_inc(earlier_made, 1)
            pool.wait_ge(earlier_made, 1)
            pool.affine_select(out=earlier[:, :, :, :], in_=earlier[:, :, :, :], compare_op=ALU.is_gt, fill=0.0, base=0,
                               pattern=[[0, TPC], [1, EXPERTS], [-1, EXPERTS]], channel_multiplier=0).then_inc(earlier_made, 1)

            def root(it, u):
                pool.wait_ge(step.sem, step.at(it, 12 * u + 3))
                pool.wait_ge(normed.sem, normed.at(it, u))
                nc.gpsimd.tensor_tensor(rstd[:, :], var_eps[:, :], neg_half[:, :], ALU.pow).then_inc(rooted.sem, 1)

            def chunk(it, u, more):
                pool.wait_ge(normed.sem, normed.at(it, u + 1))
                nc.gpsimd.tensor_tensor(base[:, bass.ds(it * (2 * TPC) + TPC * u, TPC), :], x_in[:, u], x_n[:, u],
                                        ALU.add).then_inc(based.sem, 1)
                if more or u == 0:
                    root(it, u + 1)

            root(0, 0)
            passes(pool, chunk)
            pool.wait_ge(based.sem, based.at(BATCH, 0))

        @block.scalar
        def _(act):
            act.wait_ge(small, 32)
            nc.scalar.activation(gw_hi[:, :, :], gw[:, :, :], ACT.Copy).then_inc(gw_hi_ready, 1)
            rows.give_credit(act)
            with act.Fori(0, BATCH) as it:
                for u in range(2):
                    for t in range(TPC):
                        act.wait_ge(turned_ready.sem, turned_ready.at(it, TPC * u + t + 1))
                        if t == 0:
                            act.wait_ge(scored.sem, scored.at(it, u - 1))
                            act.wait_ge(stored[u].sem, stored[u].at(it, 0))
                        nc.scalar.activation(xt_hi[:, u, :, t * P:(t + 1) * P], turned[t % 2][:, :, :],
                                             ACT.Copy).then_inc(hi_ready.sem, 1)
                    act.wait_ge(scored.sem, scored.at(it, u + 1))
                    act.wait_ge(g_read.sem, g_read.at(it, u))
                    nc.scalar.activation(g_rows[:, :], g_ps[0:EXPERTS, :], ACT.Identity,
                                         bias=gb[:, 0:1]).then_inc(rows.sem, 1)
                    act.wait_ge(less_max.sem, less_max.at(it, u + 1))
                    nc.scalar.activation(e_g[:, :, :], e_g[:, :, :], ACT.Exp).then_inc(exped.sem, 1)

        @block.vector
        def _(dve):
            normed.give_credit(dve)
            dve.wait_ge(small, 32)
            dve.wait_ge(gw_hi_ready, 1)
            dve.wait_ge(earlier_made, 2)
            nc.vector.tensor_tensor(gw_lo[:, :, :], gw[:, :, :], gw_hi[:, :, :].bitcast(F32), ALU.subtract).then_inc(gw_lo_ready, 1)
            lo_ready.give_credit(dve)
            g_read.give_credit(dve)

            def link(ins, it, n):
                ins.then_inc(step.sem, 1)
                dve.wait_ge(step.sem, step.at(it, n))

            def normalise(it, u):
                b = u % 2
                dve.wait_ge(loaded[b].sem, loaded[b].at(it, u // 2 + 1))
                for t in range(TPC):
                    last = nc.vector.bn_stats(stats[:, t, :], x_in[:, b, t, :])
                link(last, it, 12 * u + 1)
                dve.sem_inc(waited.sem, 1)
                for t in range(TPC):
                    last = nc.vector.bn_aggr(mean_var[:, t, :], stats[:, t, :])
                link(last, it, 12 * u + 2)
                link(nc.vector.tensor_scalar(var_eps[:, :], mean_var[:, :, 1], EPS, None, ALU.add), it, 12 * u + 3)
                dve.wait_ge(rooted.sem, rooted.at(it, u + 1))
                dve.wait_ge(turned_ready.sem, turned_ready.at(it, TPC * (u - 1)))
                dve.wait_ge(based.sem, based.at(it, u - 1))
                for t in range(TPC):
                    last = nc.vector.tensor_scalar(x_n[:, b, t, :], x_in[:, b, t, :], mean_var[:, t, 0:1],
                                                   rstd[:, t:t + 1], ALU.subtract, ALU.mult)
                last.then_inc(normed.sem, 1)

            four = [P, TPC, EXPERTS, EXPERTS]
            other = g[:, :, :].unsqueeze(2).to_broadcast(four)
            own = g[:, :, :].unsqueeze(3).to_broadcast(four)

            def chunk(it, u, more):
                for t in range(TPC):
                    dve.wait_ge(hi_ready.sem, hi_ready.at(it, TPC * u + t + 1))
                    nc.vector.tensor_tensor(xt_lo[:, u, :, t * P:(t + 1) * P], turned[t % 2][:, :, :],
                                            xt_hi[:, u, :, t * P:(t + 1) * P].bitcast(F32),
                                            ALU.subtract).then_inc(lo_ready.sem, 1)
                dve.wait_ge(g_turned.sem, g_turned.at(it, u + 1))
                nc.vector.tensor_copy(g[:, :, :], gt_ps[:, :, 0:EXPERTS]).then_inc(g_read.sem, 1)
                dve.wait_ge(g_read.sem, g_read.at(it, u + 1))
                nc.vector.tensor_tensor(above[:, :, :, :], other, own, ALU.is_gt)
                nc.vector.tensor_reduce(top[:, :], g[:, :, :], AX.X, ALU.max)
                n = 12 * u + 3
                link(nc.vector.tensor_tensor(ties[:, :, :, :], other, own, ALU.is_equal), it, n + 1)
                nc.vector.tensor_tensor(e_g[:, :, :], g[:, :, :], top[:, :].unsqueeze(2).to_broadcast([P, TPC, EXPERTS]),
                                        ALU.subtract).then_inc(less_max.sem, 1)
                link(nc.vector.tensor_tensor(ties[:, :, :, :], ties[:, :, :, :], earlier[:, :, :, :], ALU.mult), it, n + 2)
                link(nc.vector.tensor_tensor(above[:, :, :, :], above[:, :, :, :], ties[:, :, :, :], ALU.add), it, n + 3)
                link(nc.vector.tensor_reduce(rank[:, :, :], above[:, :, :, :], AX.X, ALU.add), it, n + 4)
                link(nc.vector.tensor_scalar(rank[:, :, :], rank[:, :, :], 2.0, None, ALU.is_lt), it, n + 5)
                dve.wait_ge(exped.sem, exped.at(it, u + 1))
                link(nc.vector.tensor_tensor(rank[:, :, :], rank[:, :, :], e_g[:, :, :], ALU.mult), it, n + 6)
                link(nc.vector.tensor_reduce(top[:, :], rank[:, :, :], AX.X, ALU.add), it, n + 7)
                link(nc.vector.reciprocal(top[:, :], top[:, :]), it, n + 8)
                link(nc.vector.tensor_tensor(gates[:, bass.ds(it * (2 * TPC) + TPC * u, TPC), :], rank[:, :, :],
                                             top[:, :].unsqueeze(2).to_broadcast([P, TPC, EXPERTS]), ALU.mult), it, n + 9)
                if more or u == 0:
                    normalise(it, u + 1)

            normalise(0, 0)
            passes(dve, chunk)

        @block.tensor
        def _(pe):
            pe.wait_ge(gw_lo_ready, 1)
            turned_ready.give_credit(pe)
            scored.give_credit(pe)
            with pe.Fori(0, BATCH) as it:
                for u in range(2):
                    pe.wait_ge(normed.sem, normed.at(it, u + 1))
                    for t in range(TPC):
                        pe.wait_ge(lo_ready.sem, lo_ready.at(it, TPC * u + t - 1))
                        for k in range(KT):
                            mm = nc.tensor.transpose(turned[t % 2][:, k, :], x_n[:, u, t, k * P:(k + 1) * P], ident[:, :])
                        mm.then_inc(turned_ready.sem, 1)
                    pe.wait_ge(lo_ready.sem, lo_ready.at(it, TPC * (u + 1)))
                    pe.wait_ge(rows.sem, rows.at(it, u))
                    i = 0
                    for x_part, w_part in ((xt_hi, gw_hi), (xt_hi, gw_lo), (xt_lo, gw_hi)):
                        for k in range(KT):
                            mm = nc.tensor.matmul(g_ps[0:EXPERTS, :], w_part[:, k, :], x_part[:, u, k, :],
                                                  start=i == 0, stop=i == 11)
                            i += 1
                    mm.then_inc(scored.sem, 1)
                    pe.wait_ge(gw_lo_ready, 1)
                    pe.wait_ge(rows.sem, rows.at(it, u + 1))
                    pe.wait_ge(g_read.sem, g_read.at(it, u))
                    for t in range(TPC):
                        mm = nc.tensor.transpose(gt_ps[:, t, 0:EXPERTS], g_rows[:, t * P:(t + 1) * P], ident[0:EXPERTS, 0:EXPERTS])
                    mm.then_inc(g_turned.sem, 1)


def split_experts(nc, w1, w2, w_hi, w_lo):
    with ExitStack() as ctx:
        raw = ctx.enter_context(nc.sbuf_tensor("split_raw", [P, 2, KT, D], F32))
        hi = ctx.enter_context(nc.sbuf_tensor("split_hi", [P, 2, KT, D], F32R))
        lo = ctx.enter_context(nc.sbuf_tensor("split_lo", [P, 2, KT, D], F32R))
        loaded = [nc.alloc_semaphore(f"split_loaded{u}") for u in range(2)]
        stored = [nc.alloc_semaphore(f"split_stored{u}") for u in range(2)]
        hi_ready = nc.alloc_semaphore("split_hi_ready")
        lo_ready = nc.alloc_semaphore("split_lo_ready")
        block = ctx.enter_context(nc.Block())
        mats = [(w, e) for e in range(EXPERTS) for w in range(2)]

        @block.sync
        def _(sp):
            for n, (w, e) in enumerate(mats):
                if n >= 2:
                    sp.wait_ge(lo_ready, n - 1)
                sp.dma_start(raw[:, n % 2], (w1, w2)[w][e].rearrange("(k p) n -> p k n", p=P)).then_inc(loaded[n % 2], 16)

        @block.gpsimd
        def _(pool):
            for n, (w, e) in enumerate(mats):
                pool.wait_ge(lo_ready, n + 1)
                for part, dst in ((hi, w_hi), (lo, w_lo)):
                    pool.dma_start(dst[e, w].rearrange("(k p) n -> p k n", p=P), part[:, n % 2].bitcast(F32)).then_inc(stored[n % 2], 16)
            for u in range(2):
                pool.wait_ge(stored[u], 16 * len(mats))

        @block.scalar
        def _(act):
            for n in range(len(mats)):
                act.wait_ge(loaded[n % 2], 16 * (n // 2 + 1))
                if n >= 2:
                    act.wait_ge(stored[n % 2], 32 * (n // 2))
                nc.scalar.activation(hi[:, n % 2], raw[:, n % 2], ACT.Copy).then_inc(hi_ready, 1)

        @block.vector
        def _(dve):
            for n in range(len(mats)):
                dve.wait_ge(hi_ready, n + 1)
                nc.vector.tensor_tensor(lo[:, n % 2], raw[:, n % 2], hi[:, n % 2].bitcast(F32), ALU.subtract).then_inc(lo_ready, 1)


def experts(nc, w_hi_d, w_lo_d, vectors, y_hi, y_lo, base, gates, out, ident):
    TOK, TT = 256, 2
    CHUNKS = BATCH * SEQ // TOK
    b1, g1, be1, b2, g2, be2 = vectors
    name = "experts"
    with ExitStack() as ctx:
        sb = lambda n, shape, dt=F32: ctx.enter_context(nc.sbuf_tensor(f"{name}_{n}", shape, dt))
        sig = lambda n, per, credit=0, step=1: Signal(nc, ctx, f"{name}_{n}", per, credit, step)
        w_hi = sb("w_hi", [P, 2, 2, KT, D], F32R)
        w_lo = sb("w_lo", [P, 2, 2, KT, D], F32R)
        rows = sb("rows", [P, 2, 4, D])
        cols = sb("cols", [P, 2, EXPERTS, KT])
        yt_hi = sb("yt_hi", [P, 2, KT, TOK], F32R)
        yt_lo = sb("yt_lo", [P, 2, KT, TOK], F32R)
        t1 = sb("t1", [P, TT, D])
        u1 = sb("u1", [P, TT, D])
        relu = sb("relu", [P, KT, TOK])
        ht_hi = sb("ht_hi", [P, KT, TOK], F32R)
        ht_lo = sb("ht_lo", [P, KT, TOK], F32R)
        t2 = sb("t2", [P, TT, D])
        u2 = sb("u2", [P, TT, D])
        v2 = sb("v2", [P, TT, D])
        stats = sb("stats", [P, 2, TT, 6])
        mean_var = sb("mean_var", [P, 2, TT, 2])
        rstd = sb("rstd", [P, 2, TT])
        neg_mean = sb("neg_mean", [P, 2, TT])
        root = sb("root", [P, 2, TT])
        eps = sb("eps", [P, 1])
        acc1 = [ctx.enter_context(nc.psum_tensor(f"{name}_acc1_{n}", [P, D], F32)) for n in range(TT)]
        acc2 = [ctx.enter_context(nc.psum_tensor(f"{name}_acc2_{n}", [P, D], F32)) for n in range(TT)]
        turned = [ctx.enter_context(nc.psum_tensor(f"{name}_turned{n}", [P, 2, TOK], F32)) for n in range(2)]

        weights_in = [nc.alloc_semaphore(f"{name}_weights_in{w}") for w in range(2)]
        cols_in = nc.alloc_semaphore(f"{name}_cols_in")
        y_in = [Signal(nc, ctx, f"{name}_y_in{u}", 2, 0, 16) for u in range(2)]
        m1 = sig("m1_done", TT, 2 * TT)
        b1_added = sig("b1_added", TT, TT)
        norm1 = sig("norm1_step", 4)
        u1_ready = sig("u1_ready", TT)
        turned_ready = sig("turned_ready", 2, 2)
        relu_ready = sig("relu_ready", 1)
        relu_banks = sig("relu_banks", 2, 2)
        hi_ready = sig("hi_ready", 1)
        lo_ready = sig("lo_ready", 1, 1)
        m2 = sig("m2_done", TT, 2 * TT)
        b2_added = sig("b2_added", TT, TT)
        norm2 = sig("norm2_step", 4)
        rooted = [sig(f"rooted{n}", 1) for n in range(2)]
        waited = sig("waited", 1)
        u2_ready = sig("u2_ready", TT, TT)
        g2_done = sig("g2_done", TT, TT)
        v2_ready = sig("v2_ready", TT)
        added = sig("added", TT, TT)
        stored = nc.alloc_semaphore(f"{name}_stored")
        block = ctx.enter_context(nc.Block())

        def chunks(eng, first, step, last_step):
            with eng.Fori(0, CHUNKS // 2 - 1) as i:
                for u in range(2):
                    step(i * 2 + (first + u), i * 2 + u, u, i + first // 2, True)
            i = CHUNKS // 2 - 1
            for u in range(2):
                step(first + 2 * i + u, 2 * i + u, u, i + first // 2, u == 0)

        @block.sync
        def _(sp):
            for n, vec in enumerate((g1, be1)):
                sp.dma_start(cols[:, n], vec.rearrange("e (k p) -> p e k", p=P),
                             allow_slow_non_contiguous=True).then_inc(cols_in, 16)

            def load_expert(e):
                w = e % 2
                if e >= 2:
                    sp.wait_ge(added.sem, added.at((e - 1) * CHUNKS, 0))
                for part, dst in ((w_hi_d, w_hi), (w_lo_d, w_lo)):
                    for m in range(2):
                        sp.dma_start(dst[:, w, m].bitcast(F32), part[e, m].rearrange("(k p) n -> p k n", p=P)).then_inc(weights_in[w], 16)
                for n, vec in enumerate((b1, b2, g2, be2)):
                    sp.dma_start(rows[:, w, n, :], vec[e:e + 1, :].to_broadcast([P, D])).then_inc(weights_in[w], 16)

            load_expert(0)
            for e in range(EXPERTS):
                if e == 0:
                    load_expert(1)

                def load_y(lin, c, u, pair, more):
                    sp.wait_ge(m1.sem, m1.at(lin, -TT))
                    for part, dst in ((y_hi, yt_hi), (y_lo, yt_lo)):
                        sp.dma_start(dst[:, u].bitcast(F32), part.rearrange("k p (c t) -> c p k t", t=TOK)[c]).then_inc(y_in[u].sem, 16)
                    if e == EXPERTS - 1:
                        return
                chunks(sp, e * CHUNKS, load_y, None)
                if 1 <= e < EXPERTS - 1:
                    load_expert(e + 1)

        @block.gpsimd
        def _(pool):
            g2_done.give_credit(pool)
            out_v = out.rearrange("(c t p) d -> c p t d", p=P, t=TT)
            for e in range(EXPERTS):
                w = e % 2

                def scale_shift(lin, c, u, pair, more):
                    for t in range(TT):
                        pool.wait_ge(u2_ready.sem, u2_ready.at(lin, t + 1))
                        pool.wait_ge(added.sem, added.at(lin, t + 1 - TT))
                        nc.gpsimd.tensor_tensor(v2[:, t], u2[:, t], rows[:, w, 2], ALU.mult).then_inc(g2_done.sem, 1)
                        pool.wait_ge(g2_done.sem, g2_done.at(lin, t + 1))
                        nc.gpsimd.tensor_tensor(v2[:, t], v2[:, t], rows[:, w, 3], ALU.add).then_inc(v2_ready.sem, 1)
                chunks(pool, e * CHUNKS, scale_shift, None)

        @block.tensor
        def _(pe):
            m1.give_credit(pe)
            m2.give_credit(pe)
            turned_ready.give_credit(pe)

            def product(acc, left_hi, left_lo, w, m, t):
                i = 0
                for left, right in ((left_hi, w_hi), (left_hi, w_lo), (left_lo, w_hi)):
                    for k in range(KT):
                        mm = nc.tensor.matmul(acc[:, :], left[:, k, t * P:(t + 1) * P], right[:, w, m, k, :],
                                              start=i == 0, stop=i == 11)
                        i += 1
                return mm

            for e in range(EXPERTS):
                w = e % 2
                pe.wait_ge(weights_in[w], 16 * 8 * (e // 2 + 1))

                def first_products(lin, u, pair):
                    pe.wait_ge(y_in[u].sem, y_in[u].at(pair, 2))
                    for t in range(TT):
                        pe.wait_ge(b1_added.sem, b1_added.at(lin, t + 1 - TT))
                        product(acc1[t], yt_hi[:, u], yt_lo[:, u], w, 0, t).then_inc(m1.sem, 1)

                def step(lin, c, u, pair, more):
                    for a in range(2):
                        pe.wait_ge(u1_ready.sem, u1_ready.at(lin, TT))
                        pe.wait_ge(relu_banks.sem, relu_banks.at(lin, a - 1))
                        for k in (2 * a, 2 * a + 1):
                            for t in range(TT):
                                mm = nc.tensor.transpose(turned[a][:, k % 2, t * P:(t + 1) * P],
                                                         u1[:, t, k * P:(k + 1) * P], ident[:, :])
                        mm.then_inc(turned_ready.sem, 1)
                    if more:
                        first_products(lin + 1, 1 - u, pair + (1 if u == 1 else 0))
                    pe.wait_ge(lo_ready.sem, lo_ready.at(lin, 1))
                    for t in range(TT):
                        pe.wait_ge(b2_added.sem, b2_added.at(lin, t + 1 - TT))
                        product(acc2[t], ht_hi, ht_lo, w, 1, t).then_inc(m2.sem, 1)

                first_products(e * CHUNKS, 0, e * CHUNKS // 2)
                chunks(pe, e * CHUNKS, step, None)

        @block.scalar
        def _(act):
            act.wait_ge(cols_in, 33)
            relu_banks.give_credit(act)
            u2_ready.give_credit(act)
            for e in range(EXPERTS):
                def normalise(lin, n, src, dst, norm, ready):
                    act.wait_ge(norm.sem, norm.at(lin, 2))
                    nc.scalar.activation(root[:, n, :], mean_var[:, n, :, 1], ACT.Sqrt, bias=eps[:, 0:1]).then_inc(rooted[n].sem, 1)
                    act.wait_ge(norm.sem, norm.at(lin, 4))
                    for t in range(TT):
                        nc.scalar.activation(dst[:, t], src[:, t], ACT.Identity, scale=rstd[:, n, t:t + 1],
                                             bias=neg_mean[:, n, t:t + 1]).then_inc(ready.sem, 1)

                def norm_first(lin):
                    act.wait_ge(turned_ready.sem, turned_ready.at(lin, 0))
                    normalise(lin, 0, t1, u1, norm1, u1_ready)

                def step(lin, c, u, pair, more):
                    act.wait_ge(lo_ready.sem, lo_ready.at(lin, 0))
                    for k in range(KT):
                        if k % 2 == 0:
                            act.wait_ge(turned_ready.sem, turned_ready.at(lin, k // 2 + 1))
                        ins = nc.scalar.activation(relu[:, k, :], turned[k // 2][:, k % 2, :], ACT.Relu,
                                                   scale=cols[:, 0, e, k:k + 1], bias=cols[:, 1, e, k:k + 1])
                        if k % 2:
                            ins.then_inc(relu_banks.sem, 1)
                    act.wait_ge(relu_banks.sem, relu_banks.at(lin, 2))
                    act.wait_ge(m2.sem, m2.at(lin, 0))
                    nc.scalar.activation(ht_hi[:, :, :], relu[:, :, :], ACT.Copy).then_inc(hi_ready.sem, 1)
                    if more:
                        norm_first(lin + 1)
                    act.wait_ge(g2_done.sem, g2_done.at(lin, 0))
                    normalise(lin, 1, t2, u2, norm2, u2_ready)

                norm_first(e * CHUNKS)
                chunks(act, e * CHUNKS, step, None)

        @block.vector
        def _(dve):
            nc.vector.memset(eps[:, :], EPS).then_inc(cols_in, 1)
            b1_added.give_credit(dve)
            b2_added.give_credit(dve)
            lo_ready.give_credit(dve)
            added.give_credit(dve)
            for e in range(EXPERTS):
                w = e % 2
                dve.wait_ge(weights_in[w], 16 * 8 * (e // 2 + 1))

                def statistics(lin, n, acc, row, t_sb, done, added_row, norm, ready):
                    for t in range(TT):
                        dve.wait_ge(done.sem, done.at(lin, t + 1))
                        nc.vector.tensor_tensor(t_sb[:, t], acc[t][:, :], rows[:, w, row], ALU.add).then_inc(added_row.sem, 1)
                    for t in range(TT):
                        dve.wait_ge(added_row.sem, added_row.at(lin, t + 1))
                        last = nc.vector.bn_stats(stats[:, n, t, :], t_sb[:, t])
                    last.then_inc(norm.sem, 1)
                    dve.wait_ge(norm.sem, norm.at(lin, 1))
                    dve.sem_inc(waited.sem, 1)
                    for t in range(TT):
                        last = nc.vector.bn_aggr(mean_var[:, n, t, :], stats[:, n, t, :])
                    last.then_inc(norm.sem, 1)
                    dve.wait_ge(norm.sem, norm.at(lin, 2))
                    dve.wait_ge(rooted[n].sem, rooted[n].at(lin, 1))
                    nc.vector.reciprocal(rstd[:, n, :], root[:, n, :]).then_inc(norm.sem, 1)
                    dve.wait_ge(norm.sem, norm.at(lin, 3))
                    nc.vector.scalar_tensor_tensor(neg_mean[:, n, :], mean_var[:, n, :, 0], -1.0, rstd[:, n, :],
                                                   ALU.mult, ALU.mult).then_inc(norm.sem, 1)

                def stats_first(lin):
                    dve.wait_ge(u1_ready.sem, u1_ready.at(lin, 0))
                    statistics(lin, 0, acc1, 0, t1, m1, b1_added, norm1, u1_ready)

                def step(lin, c, u, pair, more):
                    dve.wait_ge(hi_ready.sem, hi_ready.at(lin, 1))
                    nc.vector.tensor_tensor(ht_lo[:, :, :], relu[:, :, :], ht_hi[:, :, :].bitcast(F32),
                                            ALU.subtract).then_inc(lo_ready.sem, 1)
                    if more:
                        stats_first(lin + 1)
                    dve.wait_ge(u2_ready.sem, u2_ready.at(lin, 0))
                    statistics(lin, 1, acc2, 1, t2, m2, b2_added, norm2, u2_ready)
                    for t in range(TT):
                        dve.wait_ge(v2_ready.sem, v2_ready.at(lin, t + 1))
                        tile = base[:, bass.ds(c * TT + t, 1), :].rearrange("p o d -> p (o d)")
                        gate = gates[:, bass.ds(c * TT + t, 1), e:e + 1].rearrange("p o d -> p (o d)")
                        nc.vector.scalar_tensor_tensor(tile, v2[:, t], gate, tile, ALU.mult, ALU.add).then_inc(added.sem, 1)

                stats_first(e * CHUNKS)
                chunks(dve, e * CHUNKS, step, None)


def store_out(nc, base, out):
    with ExitStack() as ctx:
        stored = nc.alloc_semaphore("out_stored")
        block = ctx.enter_context(nc.Block())

        @block.sync
        def _(sp):
            v = out.rearrange("(n p) d -> p n d", p=P)
            for n in range(8):
                sp.dma_start(v[:, 4 * n:4 * n + 4], base[:, 4 * n:4 * n + 4]).then_inc(stored, 16)
            sp.wait_ge(stored, 128)


def in_phase(nc, phase, *args):
    with nc.cleanup_on_exit():
        phase(nc, *args)


def build_decoder(nc, a, out):
    tokens = BATCH * SEQ
    dram = lambda n, shape, dt=F32: nc.dram_tensor(n, shape, dt).ap()
    x = a["x"].rearrange("b s d -> (b s) d")
    ctx_in = a["ctx_1024"].rearrange("b s d -> (b s) d")
    out_rows = out.rearrange("b s d -> (b s) d")
    BG = BATCH * HG
    scale = DK ** -0.5
    with ExitStack() as ctx:
        ident = ctx.enter_context(nc.sbuf_tensor("ident", [P, P], F32))
        ident_b = ctx.enter_context(nc.sbuf_tensor("ident_b", [P, P], BF16))
        mask = ctx.enter_context(nc.sbuf_tensor("mask", [P, P], BF16))
        neg_half = ctx.enter_context(nc.sbuf_tensor("neg_half", [P, TPC], F32))
        in_phase(nc, build_constants, ident, ident_b, mask, neg_half)

        q1 = [dram(f"q1_{n}", (BG, P, SEQ)) for n in ("hi", "lo")]
        k1 = [dram(f"k1_{n}", (BG, P, SEQ)) for n in ("hi", "lo")]
        v1 = dram("v1", (BG, SEQ, P), F32)
        attn1 = dram("attn1", (BG, P, SEQ), F32)
        x1 = dram("x1", (tokens, D), F32)
        q2 = [dram(f"q2_{n}", (BG, P, SEQ)) for n in ("hi", "lo")]
        k2 = [dram(f"k2_{n}", (BG, P, CTX)) for n in ("hi", "lo")]
        v2 = dram("v2", (BG, CTX, P), F32)
        attn2 = dram("attn2", (BG, P, SEQ), F32)
        x2 = dram("x2", (tokens, D), F32)
        y = [dram(f"y_{n}", (KT, P, tokens)) for n in ("hi", "lo")]
        we = [dram(f"we_{n}", (EXPERTS, 2, D, D)) for n in ("hi", "lo")]

        in_phase(nc, project, "qkv1", x, 2, True,
                [(a["L0_attn_q_heads"], True), (a["L0_attn_k_heads"], True), (a["L0_attn_v_heads"], True)],
                [("T", q1[0], q1[1], scale), ("T", k1[0], k1[1], 1.0), ("N", v1)], ident, neg_half)
        in_phase(nc, attend, "self", q1, k1, v1, attn1, SEQ, True, ident, ident_b, mask)
        in_phase(nc, project_out, "out1", attn1, (a["L0_attn_output_proj"], True), None, x, x1, ident)
        in_phase(nc, project, "q2", x1, 2, True, [(a["L0_xattn_W_q"], False)], [("T", q2[0], q2[1], scale)], ident, neg_half)
        in_phase(nc, project, "kv2", ctx_in, 4, False, [(a["L0_xattn_W_k"], False), (a["L0_xattn_W_v"], False)],
                [("T", k2[0], k2[1], 1.0), ("N", v2)], ident, neg_half)
        in_phase(nc, attend, "cross", q2, k2, v2, attn2, CTX, False, ident, ident_b, mask)
        in_phase(nc, project_out, "out2", attn2, (a["L0_xattn_W_o"], False), a["L0_xattn_b_o"], x1, x2, ident)
        base = ctx.enter_context(nc.sbuf_tensor("base", [P, tokens // P, D], F32))
        gates = ctx.enter_context(nc.sbuf_tensor("gates", [P, tokens // P, EXPERTS], F32))
        in_phase(nc, route, "route", x2, a["L0_ffn_gate_W"], a["L0_ffn_gate_b"], y[0], y[1], base, gates, ident, neg_half)
        in_phase(nc, split_experts, a["L0_ffn_W1"], a["L0_ffn_W2"], we[0], we[1])
        in_phase(nc, experts, we[0], we[1], [a["L0_ffn_" + n] for n in ("b1", "g1", "be1", "b2", "g2", "be2")],
                y[0], y[1], base, gates, out_rows, ident)
        in_phase(nc, store_out, base, out_rows)


_INS = ["x", "ctx_1024", "L0_attn_q_heads", "L0_attn_k_heads", "L0_attn_v_heads", "L0_attn_output_proj",
        "L0_xattn_W_q", "L0_xattn_W_k", "L0_xattn_W_v", "L0_xattn_W_o", "L0_xattn_b_o",
        "L0_ffn_gate_W", "L0_ffn_gate_b", "L0_ffn_W1", "L0_ffn_b1", "L0_ffn_g1", "L0_ffn_be1",
        "L0_ffn_W2", "L0_ffn_b2", "L0_ffn_g2", "L0_ffn_be2"]


def kernel(**inputs):
    import concourse.bacc as bacc
    from concourse.bass_utils import run_bass_kernel_spmd

    nc = bacc.Bacc("TRN2", target_bir_lowering=False, num_devices=1)
    arrays, args = {}, {}
    for name in _INS:
        arr = np.ascontiguousarray(inputs[name])
        arrays[f"in_{name}"] = arr
        args[name] = nc.dram_tensor(f"in_{name}", arr.shape, mybir.dt.from_np(arr.dtype), kind="ExternalInput").ap()
    out = nc.dram_tensor("out", (BATCH, SEQ, D), F32, kind="ExternalOutput").ap()
    build_decoder(nc, args, out)
    return run_bass_kernel_spmd(nc, [arrays], core_ids=[0]).results[0]["out"]
```

```python
import numpy as np
import concourse.bass as bass
import concourse.mybir as mybir
from contextlib import ExitStack

F32, F32R, BF16 = mybir.dt.float32, mybir.dt.float32r, mybir.dt.bfloat16
ACT = mybir.ActivationFunctionType
ALU = mybir.AluOpType
AX = mybir.AxisListType

P = 128
BATCH, SEQ, CTX = 4, 1024, 2048
D, HEADS, DK = 512, 16, 32
KT = D // P
HG = HEADS // 4
EXPERTS = 4
CH = 512
TPC = CH // P
EPS = 1e-5
MASKED = -2.0 ** 127


class Signal:

    def __init__(self, nc, ctx, name, per, credit=0, step=1):
        self.sem = nc.alloc_semaphore(name)
        self.per, self.credit, self.step = per, credit, step

    def give_credit(self, eng):
        eng.sem_inc(self.sem, self.credit * self.step)

    def at(self, it, n):
        return it * (self.per * self.step) + (n + self.credit) * self.step


def build_constants(nc, ident, ident_b, mask, neg_half):
    with ExitStack() as ctx:
        made = nc.alloc_semaphore("constants_made")
        block = ctx.enter_context(nc.Block())

        @block.gpsimd
        def _(pool):
            pool.memset(ident[:, :], 0.0).then_inc(made, 1)
            pool.memset(mask[:, :], 0.0).then_inc(made, 1)
            pool.memset(neg_half[:, :], -0.5).then_inc(made, 1)
            pool.memset(ident_b[:, :], 0.0).then_inc(made, 1)
            pool.wait_ge(made, 4)
            pool.affine_select(out=ident_b[:, :], in_=ident_b[:, :], compare_op=ALU.not_equal, fill=1.0,
                               base=0, pattern=[[-1, P]], channel_multiplier=1).then_inc(made, 1)
            pool.affine_select(out=ident[:, :], in_=ident[:, :], compare_op=ALU.not_equal, fill=1.0,
                               base=0, pattern=[[-1, P]], channel_multiplier=1).then_inc(made, 1)
            pool.affine_select(out=mask[:, :], in_=mask[:, :], compare_op=ALU.is_ge, fill=MASKED,
                               base=0, pattern=[[-1, P]], channel_multiplier=1).then_inc(made, 1)
            pool.wait_ge(made, 7)


def load_weights(nc, name, weights, hi, lo, ident, first_loads):
    with ExitStack() as ctx:
        raw = ctx.enter_context(nc.sbuf_tensor(f"{name}_raw", [P, 2, KT, D], F32))
        turned = ctx.enter_context(nc.psum_tensor(f"{name}_turned", [P, KT, D], F32))
        loaded = [nc.alloc_semaphore(f"{name}_loaded{u}") for u in range(2)]
        turned_ready = nc.alloc_semaphore(f"{name}_turned")
        hi_ready = nc.alloc_semaphore(f"{name}_hi")
        lo_ready = nc.alloc_semaphore(f"{name}_lo")
        block = ctx.enter_context(nc.Block())

        @block.sync
        def _(sp):
            for n, (w, _) in enumerate(weights):
                if n >= 2:
                    sp.wait_ge(lo_ready, n - 1)
                sp.dma_start(raw[:, n % 2], w.rearrange("(k p) n -> p k n", p=P)).then_inc(loaded[n % 2], 16)
                if n == min(1, len(weights) - 1):
                    first_loads(sp)

        @block.tensor
        def _(pe):
            done = 0
            for n, (_, transposed) in enumerate(weights):
                if not transposed:
                    continue
                pe.wait_ge(loaded[n % 2], 16 * (n // 2 + 1))
                if n:
                    pe.wait_ge(lo_ready, n)
                for k in range(KT):
                    for m in range(KT):
                        mm = nc.tensor.transpose(turned[:, k, m * P:(m + 1) * P],
                                                 raw[:, n % 2, m, k * P:(k + 1) * P], ident[:, :])
                done += 1
                mm.then_inc(turned_ready, 1)

        def source(eng, n, seen):
            if weights[n][1]:
                eng.wait_ge(turned_ready, seen + 1)
                return turned[:, :, :], seen + 1
            eng.wait_ge(loaded[n % 2], 16 * (n // 2 + 1))
            return raw[:, n % 2], seen

        @block.scalar
        def _(act):
            seen = 0
            for n in range(len(weights)):
                src, seen = source(act, n, seen)
                nc.scalar.activation(hi[:, n], src, ACT.Copy).then_inc(hi_ready, 1)

        @block.vector
        def _(dve):
            seen = 0
            for n in range(len(weights)):
                src, seen = source(dve, n, seen)
                dve.wait_ge(hi_ready, n + 1)
                nc.vector.tensor_tensor(lo[:, n], src, hi[:, n].bitcast(F32),
                                        ALU.subtract).then_inc(lo_ready, 1)


def project(nc, name, src, chunks, norm, weights, outs, ident, neg_half):
    NOUT = 4 * len(weights)
    with ExitStack() as ctx:
        sb = lambda n, shape, dt=F32: ctx.enter_context(nc.sbuf_tensor(f"{name}_{n}", shape, dt))
        sig = lambda n, per, credit=0, step=1: Signal(nc, ctx, f"{name}_{n}", per, credit, step)
        w_hi = sb("w_hi", [P, len(weights), KT, D], F32R)
        w_lo = sb("w_lo", [P, len(weights), KT, D], F32R)
        x_in = sb("x_in", [P, 2, TPC, D])
        loaded = [sig(f"loaded{u}", chunks // 2, step=16) for u in range(2)]
        src_v = src.rearrange("(c t p) d -> c p t d", p=P, t=TPC)

        def load_chunk(sp, it, u):
            sp.dma_start(x_in[:, u % 2], src_v[it * chunks + u]).then_inc(loaded[u % 2].sem, 16)

        def first_loads(sp):
            for u in range(2):
                load_chunk(sp, 0, u)

        load_weights(nc, f"{name}_w", weights, w_hi, w_lo, ident, first_loads)
        x_n = sb("x_n", [P, 2, TPC, D]) if norm else x_in
        stats = sb("stats", [P, TPC, 6])
        mean_var = sb("mean_var", [P, TPC, 2])
        var_eps = sb("var_eps", [P, TPC])
        rstd = sb("rstd", [P, TPC])
        xt_hi = sb("xt_hi", [P, 2, KT, CH], F32R)
        xt_lo = sb("xt_lo", [P, 2, KT, CH], F32R)
        out_hi = sb("out_hi", [P, 4, D], F32R)
        out_lo = sb("out_lo", [P, 4, D], F32R)
        out_n = sb("out_n", [P, 4, D])
        turned = [ctx.enter_context(nc.psum_tensor(f"{name}_turned{n}", [P, KT, P], F32)) for n in range(2)]
        acc = [ctx.enter_context(nc.psum_tensor(f"{name}_acc{n}", [P, D], F32)) for n in range(4)]

        step = sig("dve_step", 3 * chunks)
        rooted = sig("rooted", chunks)
        waited = sig("waited", 1)
        normed = sig("normed", TPC * chunks, 2 * TPC)
        turned_ready = sig("turned_ready", TPC * chunks, 8)
        hi_ready = sig("xt_hi_ready", TPC * chunks)
        lo_ready = sig("xt_lo_ready", TPC * chunks, 2)
        acc_ready = sig("acc_ready", NOUT * chunks, 2 * NOUT)
        NSPLIT = 4 * sum(o[0] == "T" for o in outs)
        out_hi_ready = sig("out_hi_ready", NSPLIT * chunks)
        out_lo_ready = sig("out_lo_ready", NOUT * chunks, 4)
        dmas = lambda n: 2 if n < NSPLIT else 1
        stores = [sum(dmas(n) for n in range(s, NOUT, 4)) for s in range(4)]
        stored = [sig(f"stored{s}", stores[s] * chunks, 4, step=16) for s in range(4)]
        block = ctx.enter_context(nc.Block())
        TURN = {t * NOUT // TPC: t for t in range(TPC)}

        def passes(eng, chunk):
            with eng.Fori(0, BATCH - 1) as it:
                for u in range(chunks):
                    chunk(it, u, True)
            for u in range(chunks):
                chunk(BATCH - 1, u, False)

        def stores_before(s, u, n):
            return u * stores[s] + sum(dmas(m) for m in range(s, n, 4))

        @block.sync
        def _(sp):
            def load(it, u):
                if norm:
                    sp.wait_ge(normed.sem, normed.at(it, TPC * (u - 1)))
                else:
                    sp.wait_ge(turned_ready.sem, turned_ready.at(it, TPC * (u - 1)))
                load_chunk(sp, it, u)

            def chunk(it, u, more):
                for n in range(NOUT):
                    kind, g, s = outs[n // 4][0], n % 4, n % 4
                    if n == 0 and (more or u + 2 < chunks):
                        load(it, u + 2)
                    sp.wait_ge(out_lo_ready.sem, out_lo_ready.at(it, u * NOUT + n + 1))
                    if kind == "T":
                        tok = slice(u * CH, (u + 1) * CH)
                        sp.dma_start(outs[n // 4][1][it * HG + g, :, tok], out_hi[:, s].bitcast(F32)).then_inc(stored[s].sem, 16)
                        sp.dma_start(outs[n // 4][2][it * HG + g, :, tok], out_lo[:, s].bitcast(F32)).then_inc(stored[s].sem, 16)
                    else:
                        t0 = u * CH + g * P
                        rows = outs[n // 4][1].rearrange("(b h) t d -> b t h d", h=HG)[it, t0:t0 + P]
                        sp.dma_start(rows, out_n[:, s].rearrange("p (h d) -> p h d", h=HG)).then_inc(stored[s].sem, 16)

            for s in range(4):
                stored[s].give_credit(sp)
            passes(sp, chunk)
            for s in range(4):
                sp.wait_ge(stored[s].sem, stored[s].at(BATCH, 0))

        @block.gpsimd
        def _(pool):
            if not norm:
                return

            def root(it, u):
                pool.wait_ge(step.sem, step.at(it, 3 * u + 3))
                pool.wait_ge(normed.sem, normed.at(it, TPC * u))
                nc.gpsimd.tensor_tensor(rstd[:, :], var_eps[:, :], neg_half[:, :], ALU.pow).then_inc(rooted.sem, 1)

            root(0, 0)
            root(0, 1)
            passes(pool, lambda it, u, more: root(it, u + 2) if more or u + 2 < chunks else None)

        @block.vector
        def _(dve):
            normed.give_credit(dve)
            lo_ready.give_credit(dve)
            out_lo_ready.give_credit(dve)

            def variance(it, u):
                dve.wait_ge(loaded[u % 2].sem, loaded[u % 2].at(it, u // 2 + 1))
                for t in range(TPC):
                    last = nc.vector.bn_stats(stats[:, t, :], x_in[:, u % 2, t, :])
                last.then_inc(step.sem, 1)
                dve.wait_ge(step.sem, step.at(it, 3 * u + 1))
                dve.sem_inc(waited.sem, 1)
                for t in range(TPC):
                    last = nc.vector.bn_aggr(mean_var[:, t, :], stats[:, t, :])
                last.then_inc(step.sem, 1)
                dve.wait_ge(step.sem, step.at(it, 3 * u + 2))
                nc.vector.tensor_scalar(var_eps[:, :], mean_var[:, :, 1], EPS, None, ALU.add).then_inc(step.sem, 1)

            def normalise(it, u):
                dve.wait_ge(rooted.sem, rooted.at(it, u + 1))
                dve.wait_ge(turned_ready.sem, turned_ready.at(it, TPC * (u - 1)))
                for t in range(TPC):
                    nc.vector.tensor_scalar(x_n[:, u % 2, t, :], x_in[:, u % 2, t, :],
                                            mean_var[:, t, 0:1], rstd[:, t:t + 1],
                                            ALU.subtract, ALU.mult).then_inc(normed.sem, 1)

            def split_lo(it, u, t):
                dve.wait_ge(hi_ready.sem, hi_ready.at(it, TPC * u + t + 1))
                nc.vector.tensor_tensor(xt_lo[:, u % 2, :, t * P:(t + 1) * P], turned[t % 2][:, :, :],
                                        xt_hi[:, u % 2, :, t * P:(t + 1) * P].bitcast(F32),
                                        ALU.subtract).then_inc(lo_ready.sem, 1)

            def take_out(it, u, n):
                s = n % 4
                o = outs[n // 4]
                if o[0] == "T":
                    dve.wait_ge(out_hi_ready.sem, out_hi_ready.at(it, u * NSPLIT + n + 1))
                    dve.wait_ge(stored[s].sem, stored[s].at(it, stores_before(s, u, n)))
                    nc.vector.scalar_tensor_tensor(out_lo[:, s], acc[s][:, :], o[3], out_hi[:, s].bitcast(F32),
                                                   ALU.mult, ALU.subtract).then_inc(out_lo_ready.sem, 1)
                else:
                    dve.wait_ge(acc_ready.sem, acc_ready.at(it, u * NOUT + n + 1))
                    dve.wait_ge(stored[s].sem, stored[s].at(it, stores_before(s, u, n)))
                    nc.vector.tensor_copy(out_n[:, s], acc[s][:, :]).then_inc(out_lo_ready.sem, 1)

            def chunk(it, u, more):
                for n in range(NOUT):
                    if n in TURN and (more or u + 1 < chunks):
                        split_lo(it, u + 1, TURN[n])
                    if n == NOUT - 1 and norm and (more or u + 2 < chunks):
                        normalise(it, u + 2)
                    take_out(it, u, n)
                    if n == 1 and norm and (more or u + 2 < chunks):
                        variance(it, u + 2)

            if norm:
                variance(0, 0)
                normalise(0, 0)
            for t in range(TPC):
                split_lo(0, 0, t)
            if norm:
                variance(0, 1)
                normalise(0, 1)
            passes(dve, chunk)

        @block.scalar
        def _(act):
            def split_hi(it, u, t):
                act.wait_ge(turned_ready.sem, turned_ready.at(it, TPC * u + t + 1))
                if t == 0:
                    act.wait_ge(acc_ready.sem, acc_ready.at(it, (u - 1) * NOUT))
                nc.scalar.activation(xt_hi[:, u % 2, :, t * P:(t + 1) * P], turned[t % 2][:, :, :],
                                     ACT.Copy).then_inc(hi_ready.sem, 1)

            def chunk(it, u, more):
                for n in range(NOUT):
                    if n in TURN and (more or u + 1 < chunks):
                        split_hi(it, u + 1, TURN[n])
                    s = n % 4
                    o = outs[n // 4]
                    if o[0] == "T":
                        act.wait_ge(acc_ready.sem, acc_ready.at(it, u * NOUT + n + 1))
                        act.wait_ge(stored[s].sem, stored[s].at(it, stores_before(s, u, n)))
                        nc.scalar.activation(out_hi[:, s], acc[s][:, :], ACT.Copy,
                                             scale=o[3]).then_inc(out_hi_ready.sem, 1)

            for t in range(TPC):
                split_hi(0, 0, t)
            passes(act, chunk)

        @block.tensor
        def _(pe):
            turned_ready.give_credit(pe)
            acc_ready.give_credit(pe)

            def turn(it, u, t):
                if norm:
                    pe.wait_ge(normed.sem, normed.at(it, TPC * u + t + 1))
                elif t == 0:
                    pe.wait_ge(loaded[u % 2].sem, loaded[u % 2].at(it, u // 2 + 1))
                pe.wait_ge(lo_ready.sem, lo_ready.at(it, TPC * u + t - 1))
                for k in range(KT):
                    mm = nc.tensor.transpose(turned[t % 2][:, k, :], x_n[:, u % 2, t, k * P:(k + 1) * P], ident[:, :])
                mm.then_inc(turned_ready.sem, 1)

            def chunk(it, u, more):
                pe.wait_ge(lo_ready.sem, lo_ready.at(it, TPC * (u + 1)))
                for n in range(NOUT):
                    w, g, s = n // 4, n % 4, n % 4
                    if n in TURN and (more or u + 1 < chunks):
                        turn(it, u + 1, TURN[n])
                    pe.wait_ge(out_lo_ready.sem, out_lo_ready.at(it, u * NOUT + n - 3))
                    cols = slice(g * P, (g + 1) * P)
                    i = 0
                    for a, b in ((0, 0), (0, 1), (1, 0)):
                        for k in range(KT):
                            x_part = (xt_hi, xt_lo)[a][:, u % 2, k, :]
                            w_part = (w_hi, w_lo)[b][:, w, k, :]
                            if outs[w][0] == "T":
                                mm = nc.tensor.matmul(acc[s][:, :], w_part[:, cols], x_part,
                                                      start=i == 0, stop=i == 11)
                            else:
                                mm = nc.tensor.matmul(acc[s][:, :], x_part[:, cols], w_part,
                                                      start=i == 0, stop=i == 11)
                            i += 1
                    mm.then_inc(acc_ready.sem, 1)

            for t in range(TPC):
                turn(0, 0, t)
            passes(pe, chunk)


def attend(nc, name, q_parts, k_parts, v, out_t, keys, causal, ident, ident_b, mask):
    HALVES = keys // 1024
    QC = SEQ // 256
    steps = [(w, qc, half) for w in range(2) for qc in range(QC) for half in range(HALVES)]
    G = len(steps)
    NCH = 2 * QC
    SETS = keys // P
    PASSES = BATCH * HG // 2
    GROW, WEIGH, SPREAD, SPREAD_COPY = (1, 3, 4, 5) if HALVES == 2 else (0, 1, 2, 3)
    with ExitStack() as ctx:
        sb = lambda n, shape, dt=F32: ctx.enter_context(nc.sbuf_tensor(f"{name}_{n}", shape, dt))
        sig = lambda n, per, credit=0, step=1: Signal(nc, ctx, f"{name}_{n}", per, credit, step)
        q_st = sb("q_stack", [P, 2, 4, SEQ], F32R)
        k_st = sb("k_stack", [P, 2, 4, keys], F32R)
        v_sb = sb("v", [P, 2, SETS, P])
        probs = sb("probs", [P, 2, 8, 1024])
        probs_t = sb("probs_t", [P, 2, 4, 256])
        neg_max = sb("neg_max", [P, 2, HALVES, 8])
        sums = sb("sums", [P, 2, HALVES, 8])
        shift = sb("shift", [P, 2, 8])
        grow = sb("grow", [P, 2, 8])
        total = sb("total", [P, 2, 8])
        weight = sb("weight", [P, 2, HALVES, 8])
        w_sb = sb("w_sb", [P, HALVES * 256])
        part = sb("part", [P, 2, HALVES, 256])
        mixed = sb("mixed", [P, 2, 256]) if HALVES == 2 else part[:, :, 0, :]
        scores = [ctx.enter_context(nc.psum_tensor(f"{name}_scores{n}", [P, 1024], F32)) for n in range(2)]
        turned = [ctx.enter_context(nc.psum_tensor(f"{name}_turned{n}", [P, 2, 256], F32)) for n in range(2)]
        out_ps = [ctx.enter_context(nc.psum_tensor(f"{name}_out{n}", [P, 2, 256], F32)) for n in range(2)]

        def tiles(s):
            return 2 * steps[s % G][1] + 2 if causal else 8

        def tiles_before(s):
            return sum(tiles(m) for m in range(s))
        NT = tiles_before(G)

        def tile_at(s, j):
            return next((k for k in range(tiles(s)) if k * 8 // tiles(s) == j), None)

        def width(n):
            _, qc, _ = steps[n // 8 % G]
            return (2 * qc + n % 8 // 4 + 1) * P if causal else 1024

        def first_query(s, k):
            return P if causal and k == tiles(s) - 1 else 0

        loaded = [sig(f"loaded{w}", 8 + SETS // 8, step=16) for w in range(2)]
        scored = sig("scored", 8 * G)
        maxed = sig("maxed", 8 * G)
        exped = sig("exped", 8 * G, 2)
        turned_r = [sig(f"turned_ready{a}", NT, a) for a in range(2)]
        copied = [sig(f"copied{a}", NT, 1) for a in range(2)]
        pv_done = sig("pv_done", NT, 16)
        prep = sig("weights_prep", 5 * NCH)
        grown = sig("grown", NCH)
        waited = sig("waited", 1)
        totals = sig("totals", NCH)
        weighed = sig("weighed", NCH, 1)
        spread = sig("spread", NCH, 2)
        spread_sb = sig("spread_sb", NCH, 1)
        scaled = sig("scaled", NCH, 2)
        mixed_r = sig("mixed_ready", NCH, 2)
        stored = [sig(f"stored{c}", NCH // 2, 1, step=16) for c in range(2)]
        block = ctx.enter_context(nc.Block())

        def load_heads(sp, bh, w):
            for r in range(4):
                rows = slice(32 * r, 32 * r + 32)
                sp.dma_start(q_st[rows, w].bitcast(F32), q_parts[r // 2][bh].rearrange("(h p) t -> p h t", p=DK)).then_inc(loaded[w].sem, 16)
                sp.dma_start(k_st[rows, w].bitcast(F32), k_parts[r % 2][bh].rearrange("(h p) t -> p h t", p=DK)).then_inc(loaded[w].sem, 16)
            for k in range(0, SETS, 8):
                sp.dma_start(v_sb[:, w, k:k + 8], v[bh, k * P:(k + 8) * P].rearrange("(k p) d -> p k d", p=P)).then_inc(loaded[w].sem, 16)

        @block.sync
        def _(sp):
            for c in range(2):
                stored[c].give_credit(sp)
            load_heads(sp, 0, 0)

            def store(it, w):
                ready = mixed_r if HALVES == 2 else scaled
                for qc in range(QC):
                    c = w * QC + qc
                    sp.wait_ge(ready.sem, ready.at(it, c + 1))
                    sp.dma_start(out_t[it * 2 + w, :, qc * 256:(qc + 1) * 256], mixed[:, c % 2]).then_inc(stored[c % 2].sem, 16)

            def one_pass(it, more):
                sp.wait_ge(pv_done.sem, pv_done.at(it, 0))
                load_heads(sp, it * 2 + 1, 1)
                store(it, 0)
                if more:
                    sp.wait_ge(pv_done.sem, pv_done.at(it, tiles_before(G // 2)))
                    load_heads(sp, it * 2 + 2, 0)
                store(it, 1)
            with sp.Fori(0, PASSES - 1) as it:
                one_pass(it, True)
            one_pass(PASSES - 1, False)
            for c in range(2):
                sp.wait_ge(stored[c].sem, stored[c].at(PASSES, 0))

        @block.gpsimd
        def _(pool):
            if HALVES == 1:
                return
            mixed_r.give_credit(pool)
            with pool.Fori(0, PASSES) as it:
                def weights(c):
                    cp = c % 2
                    pool.wait_ge(exped.sem, exped.at(it, 16 * (c + 1)))
                    for a in range(2):
                        nc.gpsimd.tensor_tensor(shift[:, a, :], neg_max[:, cp, a, :], neg_max[:, cp, 1 - a, :],
                                                ALU.subtract).then_inc(prep.sem, 1)
                    pool.wait_ge(prep.sem, prep.at(it, 5 * c + 2))
                    pool.sem_inc(waited.sem, 1)
                    nc.gpsimd.tensor_scalar(shift[:, :, :], shift[:, :, :], 80.0, -200.0, ALU.min,
                                            ALU.max).then_inc(prep.sem, 1)
                    pool.wait_ge(grown.sem, grown.at(it, c + 1))
                    pool.wait_ge(weighed.sem, weighed.at(it, c))
                    for a in range(2):
                        nc.gpsimd.tensor_tensor(total[:, a, :], grow[:, a, :], sums[:, cp, 1 - a, :],
                                                ALU.mult).then_inc(prep.sem, 1)
                    pool.wait_ge(prep.sem, prep.at(it, 5 * c + 5))
                    nc.gpsimd.tensor_tensor(total[:, :, :], total[:, :, :], sums[:, cp, :, :],
                                            ALU.add).then_inc(totals.sem, 1)

                def finish(c):
                    cp = c % 2
                    pool.wait_ge(scaled.sem, scaled.at(it, c + 1))
                    pool.wait_ge(stored[cp].sem, stored[cp].at(it, c // 2))
                    nc.gpsimd.tensor_tensor(mixed[:, cp], part[:, cp, 0, :], part[:, cp, 1, :],
                                            ALU.add).then_inc(mixed_r.sem, 1)
                for c in range(NCH):
                    weights(c)
                    finish(c)

        def chunk_ends(s):
            return s // HALVES if s % HALVES == HALVES - 1 else None

        @block.tensor
        def _(pe):
            pv_done.give_credit(pe)
            spread.give_credit(pe)
            turned_r[1].give_credit(pe)

            def score(it, n):
                w, qc, half = steps[n // 8 % G]
                h, t = n % 4, n % 8 // 4
                if n % (4 * G) == 0:
                    pe.wait_ge(loaded[w].sem, loaded[w].at(it, (n // (8 * G) + 1) * loaded[w].per))
                pe.wait_ge(exped.sem, exped.at(it, n - 1))
                q0 = qc * 256 + t * P
                for k0 in range(0, width(n), 512):
                    kn = min(512, width(n) - k0)
                    mm = nc.tensor.matmul(scores[n % 2][:, k0:k0 + kn], q_st[:, w, h, q0:q0 + P],
                                          k_st[:, w, h, half * 1024 + k0:half * 1024 + k0 + kn],
                                          start=True, stop=not (causal and k0 + kn == width(n)))
                if causal:
                    mm = nc.tensor.matmul(scores[n % 2][:, width(n) - P:width(n)], ident_b[:, :], mask[:, :],
                                          start=False, stop=True)
                mm.then_inc(scored.sem, 1)

            def turn(it, s, k):
                n = tiles_before(s) + k
                if k == 0:
                    pe.wait_ge(exped.sem, exped.at(it, 8 * (s + 1)))
                for a in range(2):
                    pe.wait_ge(copied[a].sem, copied[a].at(it, n))
                    for h in (2 * a, 2 * a + 1):
                        for t in range(first_query(s, k) // P, 2):
                            mm = nc.tensor.transpose(turned[a][:, h % 2, t * P:(t + 1) * P],
                                                     probs[:, s % 2, 4 * t + h, k * P:(k + 1) * P], ident[:, :])
                    mm.then_inc(turned_r[a].sem, 1)

            def attend_tile(it, s, k):
                w, qc, half = steps[s]
                n = tiles_before(s) + k
                c = s // HALVES
                if k == 0 and half == 0:
                    pe.wait_ge(spread_sb.sem, spread_sb.at(it, c))
                    pe.wait_ge(scaled.sem, scaled.at(it, c - 1))
                for a in range(2):
                    pe.wait_ge(copied[a].sem, copied[a].at(it, n + 1))
                q0 = first_query(s, k)
                for h in range(4):
                    mm = nc.tensor.matmul(out_ps[c % 2][32 * h:32 * h + 32, half, q0:],
                                          v_sb[:, w, 8 * half + k, 32 * h:32 * h + 32],
                                          probs_t[:, n % 2, h, q0:], start=k == 0, stop=k == tiles(s) - 1,
                                          skip_group_check=True)
                mm.then_inc(pv_done.sem, 1)

            def spread_weights(it, c):
                pe.wait_ge(weighed.sem, weighed.at(it, c + 1))
                pe.wait_ge(scaled.sem, scaled.at(it, c))
                for a in range(HALVES):
                    for t in range(2):
                        for h in range(4):
                            wt = weight[:, c % 2, a, 4 * t + h:4 * t + h + 1].to_broadcast([P, DK])
                            mm = nc.tensor.matmul(out_ps[(c + 1) % 2][32 * h:32 * h + 32, a, t * P:(t + 1) * P], wt,
                                                  ident[:, :], start=True, stop=True, skip_group_check=True)
                mm.then_inc(spread.sem, 1)

            def one_pass(it, more):
                for s in range(G):
                    for j in range(8):
                        n = 8 * (s + 1) + j + 1
                        if n < 8 * G or more:
                            score(it, n)
                        if tile_at(s, j) is not None:
                            turn(it, s, tile_at(s, j))
                        if j == 0 and s > 0 and tiles(s - 1) == 8:
                            attend_tile(it, s - 1, 7)
                        if j > 0 and tile_at(s, j - 1) is not None:
                            attend_tile(it, s, tile_at(s, j - 1))
                        if j == SPREAD and chunk_ends(s) is not None:
                            spread_weights(it, chunk_ends(s))
                attend_tile(it, G - 1, tiles(G - 1) - 1)

            for n in range(9):
                score(0, n)
            with pe.Fori(0, PASSES - 1) as it:
                one_pass(it, True)
            one_pass(PASSES - 1, False)

        def copy_turned(eng, copy, it, s, k, a):
            n = tiles_before(s) + k
            eng.wait_ge(turned_r[a].sem, turned_r[a].at(it, n + 1))
            eng.wait_ge(pv_done.sem, pv_done.at(it, n - 1))
            q0 = first_query(s, k)
            copy(probs_t[:, n % 2, 2 * a:2 * a + 2, q0:], turned[a][:, :, q0:]).then_inc(copied[a].sem, 1)

        @block.scalar
        def _(act):
            exped.give_credit(act)
            copied[0].give_credit(act)
            spread_sb.give_credit(act)

            def exp_piece(it, n):
                s, j = n // 8, n % 8
                half, c = s % HALVES, s // HALVES
                act.wait_ge(maxed.sem, maxed.at(it, n + 1))
                if j == 0 and s > 0:
                    act.wait_ge(turned_r[1].sem, turned_r[1].at(it, tiles_before(s - 1)))
                nc.scalar.activation(probs[:, s % 2, j, 0:width(n)], scores[n % 2][:, 0:width(n)], ACT.Exp,
                                     bias=neg_max[:, c % 2, half, j:j + 1],
                                     accum_out=sums[:, c % 2, half, j:j + 1]).then_inc(exped.sem, 1)

            def one_pass(it, more):
                for s in range(G):
                    for j in range(8):
                        n = 8 * (s + 1) + j
                        if n < 8 * G or more:
                            exp_piece(it, n)
                        if tile_at(s, j) is not None:
                            copy_turned(act, lambda o, i: nc.scalar.activation(o, i, ACT.Copy), it, s, tile_at(s, j), 0)
                        c = chunk_ends(s)
                        if c is None:
                            continue
                        if HALVES == 2 and j == GROW:
                            act.wait_ge(prep.sem, prep.at(it, 5 * c + 3))
                            nc.scalar.activation(grow[:, :, :], shift[:, :, :], ACT.Exp).then_inc(grown.sem, 1)
                        if j == SPREAD_COPY:
                            act.wait_ge(spread.sem, spread.at(it, c + 1))
                            act.wait_ge(scaled.sem, scaled.at(it, c))
                            nc.scalar.activation(w_sb[:, :], out_ps[(c + 1) % 2][:, 0:HALVES, :],
                                                 ACT.Copy).then_inc(spread_sb.sem, 1)

            for n in range(8):
                exp_piece(0, n)
            with act.Fori(0, PASSES - 1) as it:
                one_pass(it, True)
            one_pass(PASSES - 1, False)

        @block.vector
        def _(dve):
            copied[1].give_credit(dve)
            scaled.give_credit(dve)
            weighed.give_credit(dve)

            def max_piece(it, n):
                s, j = n // 8, n % 8
                half, c = s % HALVES, s // HALVES
                sc = scores[n % 2]
                dve.wait_ge(scored.sem, scored.at(it, n + 1))
                if j == 0 and half == 0:
                    dve.wait_ge(spread.sem, spread.at(it, c - 1))
                nc.vector.tensor_reduce(neg_max[:, c % 2, half, j:j + 1], sc[:, 0:width(n)], AX.X, ALU.max,
                                        negate=True).then_inc(maxed.sem, 1)

            def scale_chunk(it, c):
                dve.wait_ge(spread_sb.sem, spread_sb.at(it, c + 1))
                dve.wait_ge(pv_done.sem, pv_done.at(it, tiles_before((c + 1) * HALVES)))
                if HALVES == 2:
                    dve.wait_ge(mixed_r.sem, mixed_r.at(it, c - 1))
                else:
                    dve.wait_ge(stored[c % 2].sem, stored[c % 2].at(it, c // 2))
                nc.vector.tensor_tensor(part[:, c % 2, :, :], out_ps[c % 2][:, 0:HALVES, :],
                                        w_sb[:, :].rearrange("p (a q) -> p a q", a=HALVES),
                                        ALU.mult).then_inc(scaled.sem, 1)

            def one_pass(it, more):
                for s in range(G):
                    for j in range(8):
                        n = 8 * (s + 1) + j + 1
                        if n < 8 * G or more:
                            max_piece(it, n)
                        if tile_at(s, j) is not None:
                            copy_turned(dve, lambda o, i: nc.vector.tensor_copy(o, i), it, s, tile_at(s, j), 1)
                        if j == 1 and s > 0 and chunk_ends(s - 1) is not None:
                            scale_chunk(it, chunk_ends(s - 1))
                        if j == WEIGH and chunk_ends(s) is not None:
                            c = chunk_ends(s)
                            if HALVES == 2:
                                dve.wait_ge(totals.sem, totals.at(it, c + 1))
                                nc.vector.reciprocal(weight[:, c % 2, :, :], total[:, :, :]).then_inc(weighed.sem, 1)
                            else:
                                dve.wait_ge(exped.sem, exped.at(it, 8 * (c + 1)))
                                nc.vector.reciprocal(weight[:, c % 2, :, :], sums[:, c % 2, :, :]).then_inc(weighed.sem, 1)
                scale_chunk(it, NCH - 1)

            for n in range(9):
                max_piece(0, n)
            with dve.Fori(0, PASSES - 1) as it:
                one_pass(it, True)
            one_pass(PASSES - 1, False)


def project_out(nc, name, attn_t, weight, bias, residual, out, ident):
    with ExitStack() as ctx:
        sb = lambda n, shape, dt=F32: ctx.enter_context(nc.sbuf_tensor(f"{name}_{n}", shape, dt))
        sig = lambda n, per, credit=0, step=1: Signal(nc, ctx, f"{name}_{n}", per, credit, step)
        w_hi = sb("w_hi", [P, 1, KT, D], F32R)
        w_lo = sb("w_lo", [P, 1, KT, D], F32R)
        a_in = sb("a_in", [P, 2, KT, CH])
        res = sb("res", [P, 2, TPC, D])
        a_loaded = [sig(f"a_loaded{u}", 1, step=16) for u in range(2)]
        res_loaded = [sig(f"res_loaded{u}", 1, step=16) for u in range(2)]
        attn_v = attn_t.rearrange("(b g) p t -> b p g t", g=HG)
        res_v = residual.rearrange("(c t p) d -> c p t d", p=P, t=TPC)

        def load_attention(sp, it, u):
            b, half = (it, u) if u < 2 else (it + 1, u - 2)
            sp.dma_start(a_in[:, half], attn_v[b, :, :, half * CH:(half + 1) * CH]).then_inc(a_loaded[half].sem, 16)

        def load_residual(sp, it, u):
            b, half = (it, u) if u < 2 else (it + 1, u - 2)
            sp.dma_start(res[:, half], res_v[b * 2 + half]).then_inc(res_loaded[half].sem, 16)

        def first_loads(sp):
            for u in range(2):
                load_attention(sp, 0, u)
                load_residual(sp, 0, u)

        load_weights(nc, f"{name}_w", [weight], w_hi, w_lo, ident, first_loads)
        a_hi = sb("a_hi", [P, 2, KT, CH], F32R)
        a_lo = sb("a_lo", [P, 2, KT, CH], F32R)
        row = sb("row", [P, D])
        y = sb("y", [P, 2, TPC, D])
        acc = [ctx.enter_context(nc.psum_tensor(f"{name}_acc{n}", [P, D], F32)) for n in range(4)]
        row_loaded = sig("row_loaded", 0)
        biased = sig("biased", 2)
        hi_ready = sig("a_hi_ready", 2)
        lo_ready = sig("a_lo_ready", 2, 2)
        acc_ready = sig("acc_ready", 8, 16)
        added = sig("added", 8, 16)
        stored = [sig(f"stored{u}", 1, 1, step=16) for u in range(2)]
        block = ctx.enter_context(nc.Block())

        def passes(eng, chunk):
            with eng.Fori(0, BATCH - 1) as it:
                for u in range(2):
                    chunk(it, u, True)
            for u in range(2):
                chunk(BATCH - 1, u, False)

        out_v = out.rearrange("(c t p) d -> c p t d", p=P, t=TPC)

        @block.sync
        def _(sp):
            for u in range(2):
                stored[u].give_credit(sp)
            if bias is not None:
                sp.dma_start(row[:, :], bias.rearrange("(o d) -> o d", o=1).to_broadcast([P, D])).then_inc(row_loaded.sem, 16)

            def chunk(it, u, more):
                if more:
                    sp.wait_ge(lo_ready.sem, lo_ready.at(it, u + 1))
                    load_attention(sp, it, u + 2)
                sp.wait_ge(added.sem, added.at(it, 4 * (u + 1)))
                sp.dma_start(out_v[it * 2 + u], y[:, u]).then_inc(stored[u].sem, 16)
                if more:
                    load_residual(sp, it, u + 2)

            passes(sp, chunk)
            for u in range(2):
                sp.wait_ge(stored[u].sem, stored[u].at(BATCH, 0))

        @block.scalar
        def _(act):
            def split_hi(it, u):
                act.wait_ge(a_loaded[u % 2].sem, a_loaded[u % 2].at(it, u // 2 + 1))
                act.wait_ge(acc_ready.sem, acc_ready.at(it, 4 * (u - 1)))
                nc.scalar.activation(a_hi[:, u % 2], a_in[:, u % 2], ACT.Copy).then_inc(hi_ready.sem, 1)

            split_hi(0, 0)
            passes(act, lambda it, u, more: split_hi(it, u + 1) if more or u == 0 else None)

        @block.vector
        def _(dve):
            lo_ready.give_credit(dve)
            added.give_credit(dve)
            if bias is not None:
                dve.wait_ge(row_loaded.sem, 16)

            def split_lo(it, u):
                dve.wait_ge(hi_ready.sem, hi_ready.at(it, u + 1))
                nc.vector.tensor_tensor(a_lo[:, u % 2], a_in[:, u % 2], a_hi[:, u % 2].bitcast(F32),
                                        ALU.subtract).then_inc(lo_ready.sem, 1)

            def chunk(it, u, more):
                dve.wait_ge(res_loaded[u].sem, res_loaded[u].at(it, 1))
                if bias is not None:
                    for t in range(TPC):
                        last = nc.vector.tensor_tensor(res[:, u, t], res[:, u, t], row[:, :], ALU.add)
                    last.then_inc(biased.sem, 1)
                if more or u == 0:
                    split_lo(it, u + 1)
                if bias is not None:
                    dve.wait_ge(biased.sem, biased.at(it, u + 1))
                dve.wait_ge(stored[u].sem, stored[u].at(it, 0))
                for t in range(TPC):
                    dve.wait_ge(acc_ready.sem, acc_ready.at(it, 4 * u + t + 1))
                    nc.vector.tensor_tensor(y[:, u, t], acc[t][:, :], res[:, u, t], ALU.add).then_inc(added.sem, 1)

            split_lo(0, 0)
            passes(dve, chunk)

        @block.tensor
        def _(pe):
            acc_ready.give_credit(pe)
            with pe.Fori(0, BATCH) as it:
                for u in range(2):
                    pe.wait_ge(lo_ready.sem, lo_ready.at(it, u + 1))
                    for t in range(TPC):
                        pe.wait_ge(added.sem, added.at(it, 4 * (u - 1) + t + 1))
                        i = 0
                        for a, w in ((a_hi, w_hi), (a_hi, w_lo), (a_lo, w_hi)):
                            for k in range(KT):
                                mm = nc.tensor.matmul(acc[t][:, :], a[:, u, k, t * P:(t + 1) * P], w[:, 0, k, :],
                                                      start=i == 0, stop=i == 11)
                                i += 1
                        mm.then_inc(acc_ready.sem, 1)


def route(nc, name, src, gate_w, gate_b, y_hi, y_lo, base, gates, ident, neg_half):
    with ExitStack() as ctx:
        sb = lambda n, shape, dt=F32: ctx.enter_context(nc.sbuf_tensor(f"{name}_{n}", shape, dt))
        sig = lambda n, per, credit=0, step=1: Signal(nc, ctx, f"{name}_{n}", per, credit, step)
        gw = sb("gw", [P, KT, EXPERTS])
        gw_hi = sb("gw_hi", [P, KT, EXPERTS], F32R)
        gw_lo = sb("gw_lo", [P, KT, EXPERTS], F32R)
        gb = sb("gb", [EXPERTS, 1])
        earlier = sb("earlier", [P, TPC, EXPERTS, EXPERTS])
        x_in = sb("x_in", [P, 2, TPC, D])
        x_n = sb("x_n", [P, 2, TPC, D])
        stats = sb("stats", [P, TPC, 6])
        mean_var = sb("mean_var", [P, TPC, 2])
        var_eps = sb("var_eps", [P, TPC])
        rstd = sb("rstd", [P, TPC])
        xt_hi = sb("xt_hi", [P, 2, KT, CH], F32R)
        xt_lo = sb("xt_lo", [P, 2, KT, CH], F32R)
        g_rows = sb("g_rows", [EXPERTS, CH])
        g = sb("g", [P, TPC, EXPERTS])
        above = sb("above", [P, TPC, EXPERTS, EXPERTS])
        ties = sb("ties", [P, TPC, EXPERTS, EXPERTS])
        rank = sb("rank", [P, TPC, EXPERTS])
        top = sb("top", [P, TPC])
        e_g = sb("e_g", [P, TPC, EXPERTS])
        turned = [ctx.enter_context(nc.psum_tensor(f"{name}_turned{n}", [P, KT, P], F32)) for n in range(2)]
        g_ps = ctx.enter_context(nc.psum_tensor(f"{name}_g_ps", [P, CH], F32))
        gt_ps = ctx.enter_context(nc.psum_tensor(f"{name}_gt_ps", [P, TPC, P], F32))
        small = nc.alloc_semaphore(f"{name}_small")
        earlier_made = nc.alloc_semaphore(f"{name}_earlier_made")
        gw_hi_ready = nc.alloc_semaphore(f"{name}_gw_hi_ready")
        gw_lo_ready = nc.alloc_semaphore(f"{name}_gw_lo_ready")
        loaded = [sig(f"loaded{u}", 1, step=16) for u in range(2)]
        step = sig("dve_step", 2 * 12, 9)
        rooted = sig("rooted", 2)
        waited = sig("waited", 1)
        normed = sig("normed", 2, 1)
        based = sig("based", 2, 2)
        turned_ready = sig("turned_ready", 2 * TPC, 8)
        hi_ready = sig("hi_ready", 2 * TPC)
        lo_ready = sig("lo_ready", 2 * TPC, 2)
        scored = sig("scored", 2, 2)
        rows = sig("rows", 2, 1)
        g_turned = sig("g_turned", 2)
        g_read = sig("g_read", 2, 1)
        less_max = sig("less_max", 2)
        exped = sig("exped", 2)
        stored = [sig(f"stored{u}", 2, 2, step=16) for u in range(2)]
        block = ctx.enter_context(nc.Block())
        src_v = src.rearrange("(c t p) d -> c p t d", p=P, t=TPC)

        def passes(eng, chunk):
            with eng.Fori(0, BATCH - 1) as it:
                for u in range(2):
                    chunk(it, u, True)
            for u in range(2):
                chunk(BATCH - 1, u, False)

        @block.sync
        def _(sp):
            sp.dma_start(gw[:, :, :], gate_w.rearrange("(k p) e -> p k e", p=P)).then_inc(small, 16)
            sp.dma_start(gb[:, :], gate_b.rearrange("(e o) -> e o", o=1)).then_inc(small, 16)
            for u in range(2):
                stored[u].give_credit(sp)

            def load(it, u):
                sp.wait_ge(based.sem, based.at(it, u - 1))
                sp.dma_start(x_in[:, u % 2], src_v[it * 2 + u]).then_inc(loaded[u % 2].sem, 16)

            def chunk(it, u, more):
                if more or u == 0:
                    load(it, u + 1)
                sp.wait_ge(lo_ready.sem, lo_ready.at(it, TPC * (u + 1)))
                for part, dst in ((xt_hi, y_hi), (xt_lo, y_lo)):
                    sp.dma_start(dst.rearrange("k p (c t) -> c p k t", t=CH)[it * 2 + u], part[:, u].bitcast(F32)).then_inc(stored[u].sem, 16)

            load(0, 0)
            passes(sp, chunk)
            for u in range(2):
                sp.wait_ge(stored[u].sem, stored[u].at(BATCH, 0))

        @block.gpsimd
        def _(pool):
            based.give_credit(pool)
            pool.memset(earlier[:, :, :, :], 1.0).then_inc(earlier_made, 1)
            pool.wait_ge(earlier_made, 1)
            pool.affine_select(out=earlier[:, :, :, :], in_=earlier[:, :, :, :], compare_op=ALU.is_gt, fill=0.0, base=0,
                               pattern=[[0, TPC], [1, EXPERTS], [-1, EXPERTS]], channel_multiplier=0).then_inc(earlier_made, 1)

            def root(it, u):
                pool.wait_ge(step.sem, step.at(it, 12 * u - 6))
                pool.wait_ge(normed.sem, normed.at(it, u))
                nc.gpsimd.tensor_tensor(rstd[:, :], var_eps[:, :], neg_half[:, :], ALU.pow).then_inc(rooted.sem, 1)

            def chunk(it, u, more):
                if more or u == 0:
                    root(it, u + 1)
                pool.wait_ge(normed.sem, normed.at(it, u + 1))
                nc.gpsimd.tensor_tensor(base[:, bass.ds(it * (2 * TPC) + TPC * u, TPC), :], x_in[:, u], x_n[:, u],
                                        ALU.add).then_inc(based.sem, 1)

            root(0, 0)
            passes(pool, chunk)
            pool.wait_ge(based.sem, based.at(BATCH, 0))

        @block.scalar
        def _(act):
            act.wait_ge(small, 32)
            nc.scalar.activation(gw_hi[:, :, :], gw[:, :, :], ACT.Copy).then_inc(gw_hi_ready, 1)
            rows.give_credit(act)
            with act.Fori(0, BATCH) as it:
                for u in range(2):
                    for t in range(TPC):
                        act.wait_ge(turned_ready.sem, turned_ready.at(it, TPC * u + t + 1))
                        if t == 0:
                            act.wait_ge(scored.sem, scored.at(it, u - 1))
                            act.wait_ge(stored[u].sem, stored[u].at(it, 0))
                        nc.scalar.activation(xt_hi[:, u, :, t * P:(t + 1) * P], turned[t % 2][:, :, :],
                                             ACT.Copy).then_inc(hi_ready.sem, 1)
                    act.wait_ge(scored.sem, scored.at(it, u + 1))
                    act.wait_ge(g_read.sem, g_read.at(it, u))
                    nc.scalar.activation(g_rows[:, :], g_ps[0:EXPERTS, :], ACT.Identity,
                                         bias=gb[:, 0:1]).then_inc(rows.sem, 1)
                    act.wait_ge(less_max.sem, less_max.at(it, u + 1))
                    nc.scalar.activation(e_g[:, :, :], e_g[:, :, :], ACT.Exp).then_inc(exped.sem, 1)

        @block.vector
        def _(dve):
            normed.give_credit(dve)
            dve.wait_ge(small, 32)
            dve.wait_ge(gw_hi_ready, 1)
            dve.wait_ge(earlier_made, 2)
            nc.vector.tensor_tensor(gw_lo[:, :, :], gw[:, :, :], gw_hi[:, :, :].bitcast(F32), ALU.subtract).then_inc(gw_lo_ready, 1)
            lo_ready.give_credit(dve)
            g_read.give_credit(dve)

            def link(ins, it, n):
                ins.then_inc(step.sem, 1)
                dve.wait_ge(step.sem, step.at(it, n))

            def variance(it, u):
                b = u % 2
                dve.wait_ge(loaded[b].sem, loaded[b].at(it, u // 2 + 1))
                for t in range(TPC):
                    last = nc.vector.bn_stats(stats[:, t, :], x_in[:, b, t, :])
                link(last, it, 12 * u - 8)
                dve.sem_inc(waited.sem, 1)
                for t in range(TPC):
                    last = nc.vector.bn_aggr(mean_var[:, t, :], stats[:, t, :])
                link(last, it, 12 * u - 7)
                link(nc.vector.tensor_scalar(var_eps[:, :], mean_var[:, :, 1], EPS, None, ALU.add), it, 12 * u - 6)

            def normalise(it, u):
                b = u % 2
                dve.wait_ge(rooted.sem, rooted.at(it, u + 1))
                dve.wait_ge(turned_ready.sem, turned_ready.at(it, TPC * (u - 1)))
                dve.wait_ge(based.sem, based.at(it, u - 1))
                for t in range(TPC):
                    last = nc.vector.tensor_scalar(x_n[:, b, t, :], x_in[:, b, t, :], mean_var[:, t, 0:1],
                                                   rstd[:, t:t + 1], ALU.subtract, ALU.mult)
                last.then_inc(normed.sem, 1)

            four = [P, TPC, EXPERTS, EXPERTS]
            other = g[:, :, :].unsqueeze(2).to_broadcast(four)
            own = g[:, :, :].unsqueeze(3).to_broadcast(four)

            def chunk(it, u, more):
                if more or u == 0:
                    variance(it, u + 1)
                for t in range(TPC):
                    dve.wait_ge(hi_ready.sem, hi_ready.at(it, TPC * u + t + 1))
                    nc.vector.tensor_tensor(xt_lo[:, u, :, t * P:(t + 1) * P], turned[t % 2][:, :, :],
                                            xt_hi[:, u, :, t * P:(t + 1) * P].bitcast(F32),
                                            ALU.subtract).then_inc(lo_ready.sem, 1)
                if more or u == 0:
                    normalise(it, u + 1)
                dve.wait_ge(g_turned.sem, g_turned.at(it, u + 1))
                nc.vector.tensor_copy(g[:, :, :], gt_ps[:, :, 0:EXPERTS]).then_inc(g_read.sem, 1)
                dve.wait_ge(g_read.sem, g_read.at(it, u + 1))
                nc.vector.tensor_tensor(above[:, :, :, :], other, own, ALU.is_gt)
                nc.vector.tensor_reduce(top[:, :], g[:, :, :], AX.X, ALU.max)
                n = 12 * u + (6 if more or u == 0 else 3)
                link(nc.vector.tensor_tensor(ties[:, :, :, :], other, own, ALU.is_equal), it, n + 1)
                nc.vector.tensor_tensor(e_g[:, :, :], g[:, :, :], top[:, :].unsqueeze(2).to_broadcast([P, TPC, EXPERTS]),
                                        ALU.subtract).then_inc(less_max.sem, 1)
                link(nc.vector.tensor_tensor(ties[:, :, :, :], ties[:, :, :, :], earlier[:, :, :, :], ALU.mult), it, n + 2)
                link(nc.vector.tensor_tensor(above[:, :, :, :], above[:, :, :, :], ties[:, :, :, :], ALU.add), it, n + 3)
                link(nc.vector.tensor_reduce(rank[:, :, :], above[:, :, :, :], AX.X, ALU.add), it, n + 4)
                link(nc.vector.tensor_scalar(rank[:, :, :], rank[:, :, :], 2.0, None, ALU.is_lt), it, n + 5)
                dve.wait_ge(exped.sem, exped.at(it, u + 1))
                link(nc.vector.tensor_tensor(rank[:, :, :], rank[:, :, :], e_g[:, :, :], ALU.mult), it, n + 6)
                link(nc.vector.tensor_reduce(top[:, :], rank[:, :, :], AX.X, ALU.add), it, n + 7)
                link(nc.vector.reciprocal(top[:, :], top[:, :]), it, n + 8)
                link(nc.vector.tensor_tensor(gates[:, bass.ds(it * (2 * TPC) + TPC * u, TPC), :], rank[:, :, :],
                                             top[:, :].unsqueeze(2).to_broadcast([P, TPC, EXPERTS]), ALU.mult), it, n + 9)

            variance(0, 0)
            step.give_credit(dve)
            normalise(0, 0)
            passes(dve, chunk)

        @block.tensor
        def _(pe):
            pe.wait_ge(gw_lo_ready, 1)
            turned_ready.give_credit(pe)
            scored.give_credit(pe)
            with pe.Fori(0, BATCH) as it:
                for u in range(2):
                    pe.wait_ge(normed.sem, normed.at(it, u + 1))
                    for t in range(TPC):
                        pe.wait_ge(lo_ready.sem, lo_ready.at(it, TPC * u + t - 1))
                        for k in range(KT):
                            mm = nc.tensor.transpose(turned[t % 2][:, k, :], x_n[:, u, t, k * P:(k + 1) * P], ident[:, :])
                        mm.then_inc(turned_ready.sem, 1)
                    pe.wait_ge(lo_ready.sem, lo_ready.at(it, TPC * (u + 1)))
                    pe.wait_ge(rows.sem, rows.at(it, u))
                    i = 0
                    for x_part, w_part in ((xt_hi, gw_hi), (xt_hi, gw_lo), (xt_lo, gw_hi)):
                        for k in range(KT):
                            mm = nc.tensor.matmul(g_ps[0:EXPERTS, :], w_part[:, k, :], x_part[:, u, k, :],
                                                  start=i == 0, stop=i == 11)
                            i += 1
                    mm.then_inc(scored.sem, 1)
                    pe.wait_ge(gw_lo_ready, 1)
                    pe.wait_ge(rows.sem, rows.at(it, u + 1))
                    pe.wait_ge(g_read.sem, g_read.at(it, u))
                    for t in range(TPC):
                        mm = nc.tensor.transpose(gt_ps[:, t, 0:EXPERTS], g_rows[:, t * P:(t + 1) * P], ident[0:EXPERTS, 0:EXPERTS])
                    mm.then_inc(g_turned.sem, 1)


def experts(nc, w1, w2, vectors, y_hi, y_lo, base, gates, out, ident):
    TOK, TT = 256, 2
    CHUNKS = BATCH * SEQ // TOK
    LOOPED = CHUNKS - 6
    SPLIT = CHUNKS - 6
    b1, g1, be1, b2, g2, be2 = vectors
    name = "experts"
    with ExitStack() as ctx:
        sb = lambda n, shape, dt=F32: ctx.enter_context(nc.sbuf_tensor(f"{name}_{n}", shape, dt))
        sig = lambda n, per, credit=0, step=1: Signal(nc, ctx, f"{name}_{n}", per, credit, step)
        w_hi = sb("w_hi", [P, 2, 2, KT, D], F32R)
        w_lo = sb("w_lo", [P, 2, 2, KT, D], F32R)
        raw = sb("raw", [P, KT // 2, D])
        rows = sb("rows", [P, 2, 4, D])
        cols = sb("cols", [P, 2, EXPERTS, KT])
        yt_hi = sb("yt_hi", [P, 2, KT, TOK], F32R)
        yt_lo = sb("yt_lo", [P, 2, KT, TOK], F32R)
        t1 = sb("t1", [P, TT, D])
        u1 = sb("u1", [P, TT, D])
        relu = sb("relu", [P, KT, TOK])
        ht_hi = sb("ht_hi", [P, 2, KT, TOK], F32R)
        ht_lo = sb("ht_lo", [P, 2, KT, TOK], F32R)
        t2 = sb("t2", [P, TT, D])
        u2 = sb("u2", [P, TT, D])
        v2 = sb("v2", [P, TT, D])
        stats = sb("stats", [P, 2, TT, 6])
        mean_var = sb("mean_var", [P, 2, TT, 2])
        rstd = sb("rstd", [P, 2, TT])
        neg_mean = sb("neg_mean", [P, 2, TT])
        root = sb("root", [P, 2, TT])
        eps = sb("eps", [P, 1])
        acc1 = [ctx.enter_context(nc.psum_tensor(f"{name}_acc1_{n}", [P, D], F32)) for n in range(TT)]
        acc2 = [ctx.enter_context(nc.psum_tensor(f"{name}_acc2_{n}", [P, D], F32)) for n in range(TT)]
        turned = [ctx.enter_context(nc.psum_tensor(f"{name}_turned{n}", [P, 2, TOK], F32)) for n in range(2)]

        first_raw = [raw, v2, u2, t2]
        first_in = [nc.alloc_semaphore(f"{name}_first_in{n}") for n in range(4)]
        half_in = nc.alloc_semaphore(f"{name}_half_in")
        half_hi = nc.alloc_semaphore(f"{name}_half_hi")
        half_lo = nc.alloc_semaphore(f"{name}_half_lo")
        rows_in = [nc.alloc_semaphore(f"{name}_rows_in{n}") for n in range(2)]
        cols_in = nc.alloc_semaphore(f"{name}_cols_in")
        eps_made = nc.alloc_semaphore(f"{name}_eps_made")
        stored = nc.alloc_semaphore(f"{name}_stored")
        y_in = [Signal(nc, ctx, f"{name}_y_in{u}", 2, 0, 16) for u in range(2)]
        m1 = sig("m1_done", TT, 2 * TT)
        b1_added = sig("b1_added", TT, TT)
        norm1 = sig("norm1_step", 4)
        u1_ready = sig("u1_ready", TT, TT)
        turned_ready = sig("turned_ready", 2, 2)
        relu_banks = sig("relu_banks", 2, 2)
        hi_ready = sig("hi_ready", 1)
        lo_ready = sig("lo_ready", 1, 1)
        m2 = sig("m2_done", TT, 2 * TT)
        b2_added = sig("b2_added", TT, TT)
        norm2 = sig("norm2_step", 4)
        rooted = [sig(f"rooted{n}", 1) for n in range(2)]
        waited = sig("waited", 1)
        u2_ready = sig("u2_ready", TT, TT)
        g2_done = sig("g2_done", TT, TT)
        v2_ready = sig("v2_ready", TT)
        added = sig("added", TT, TT)
        block = ctx.enter_context(nc.Block())

        def steps(eng, e, step):
            with eng.Fori(0, LOOPED // 2) as i:
                for u in range(2):
                    step(i * 2 + (e * CHUNKS + u), i * 2 + u, u, i + e * CHUNKS // 2)
            for c in range(LOOPED, CHUNKS):
                step(e * CHUNKS + c, c, c % 2, (e * CHUNKS + c) // 2)

        def expert_of(e, c, ahead):
            if isinstance(c, int) and c + ahead >= CHUNKS:
                return e + 1 if e + 1 < EXPERTS else None
            return e

        def begins(c, ahead):
            return isinstance(c, int) and c + ahead == CHUNKS

        def half_of(e, c):
            return c - SPLIT if isinstance(c, int) and e + 1 < EXPERTS and 0 <= c - SPLIT < 4 else None

        def half_rows(e, half):
            return (w1, w2)[half // 2][e, half % 2 * D // 2:(half % 2 + 1) * D // 2].rearrange("(k p) n -> p k n", p=P)

        def half_slot(w, e, half):
            k0 = half % 2 * KT // 2
            return w[:, e % 2, half // 2, k0:k0 + KT // 2]

        @block.sync
        def _(sp):
            def load_row(e, n):
                if e >= 2:
                    sp.wait_ge(added.sem, added.at((e - 1) * CHUNKS, 0))
                sp.dma_start(rows[:, e % 2, n, :], (b1, b2, g2, be2)[n][e:e + 1, :].to_broadcast([P, D])).then_inc(rows_in[e % 2], 16)

            def load_y(lin, c, u):
                sp.wait_ge(m1.sem, m1.at(lin, -TT))
                for part, dst in ((y_hi, yt_hi), (y_lo, yt_lo)):
                    sp.dma_start(dst[:, u].bitcast(F32), part.rearrange("k p (c t) -> c p k t", t=TOK)[c]).then_inc(y_in[u].sem, 16)

            for half in range(4):
                sp.dma_start(first_raw[half][:, :, :], half_rows(0, half)).then_inc(first_in[half], 16)
                if half == 1:
                    load_y(0, 0, 0)
            load_row(0, 0)
            for n, vec in enumerate((g1, be1)):
                sp.dma_start(cols[:, n], vec.rearrange("e (k p) -> p e k", p=P),
                             allow_slow_non_contiguous=True).then_inc(cols_in, 16)
            for n in range(1, 4):
                load_row(0, n)
            for e in range(EXPERTS):
                for c in range(6):
                    if (e, c) != (0, 0):
                        load_y(e * CHUNKS + c, c, c % 2)
                    if e + 1 < EXPERTS and c >= 2:
                        load_row(e + 1, c - 2)
                with sp.Fori(0, (CHUNKS - 6) // 2) as i:
                    for u in range(2):
                        load_y(i * 2 + (e * CHUNKS + 6 + u), i * 2 + (6 + u), u)

        @block.gpsimd
        def _(pool):
            g2_done.give_credit(pool)
            out_v = out.rearrange("(c t p) d -> c p t d", p=P, t=TT)
            for e in range(EXPERTS):
                pool.wait_ge(rows_in[e % 2], 64 * (e // 2 + 1))

                def step(lin, c, u, pair):
                    for t in range(TT):
                        pool.wait_ge(u2_ready.sem, u2_ready.at(lin, t + 1))
                        pool.wait_ge(added.sem, added.at(lin, t + 1 - TT))
                        nc.gpsimd.tensor_tensor(v2[:, t], u2[:, t], rows[:, e % 2, 2], ALU.mult).then_inc(g2_done.sem, 1)
                        pool.wait_ge(g2_done.sem, g2_done.at(lin, t + 1))
                        nc.gpsimd.tensor_tensor(v2[:, t], v2[:, t], rows[:, e % 2, 3], ALU.add).then_inc(v2_ready.sem, 1)
                    if e == EXPERTS - 1:
                        pool.wait_ge(added.sem, added.at(lin, TT))
                        pool.dma_start(out_v[c], base[:, bass.ds(c * TT, TT), :]).then_inc(stored, 16)
                steps(pool, e, step)
            pool.wait_ge(stored, 16 * CHUNKS)

        @block.tensor
        def _(pe):
            m1.give_credit(pe)
            m2.give_credit(pe)
            turned_ready.give_credit(pe)

            def product(acc, left_hi, left_lo, w, m, t):
                i = 0
                for left, right in ((left_hi, w_hi), (left_hi, w_lo), (left_lo, w_hi)):
                    for k in range(KT):
                        mm = nc.tensor.matmul(acc[:, :], left[:, k, t * P:(t + 1) * P], right[:, w, m, k, :],
                                              start=i == 0, stop=i == 11)
                        i += 1
                return mm

            def first_products(e, lin, u, pair):
                pe.wait_ge(y_in[u].sem, y_in[u].at(pair, 2))
                for t in range(TT):
                    pe.wait_ge(b1_added.sem, b1_added.at(lin, t + 1 - TT))
                    product(acc1[t], yt_hi[:, u], yt_lo[:, u], e % 2, 0, t).then_inc(m1.sem, 1)

            def second_products(e, lin, u):
                pe.wait_ge(lo_ready.sem, lo_ready.at(lin, 1))
                for t in range(TT):
                    pe.wait_ge(b2_added.sem, b2_added.at(lin, t + 1 - TT))
                    product(acc2[t], ht_hi[:, u], ht_lo[:, u], e % 2, 1, t).then_inc(m2.sem, 1)

            def turn(lin):
                for a in range(2):
                    pe.wait_ge(u1_ready.sem, u1_ready.at(lin, TT))
                    pe.wait_ge(relu_banks.sem, relu_banks.at(lin, a - 1))
                    for k in (2 * a, 2 * a + 1):
                        for t in range(TT):
                            mm = nc.tensor.transpose(turned[a][:, k % 2, t * P:(t + 1) * P],
                                                     u1[:, t, k * P:(k + 1) * P], ident[:, :])
                    mm.then_inc(turned_ready.sem, 1)

            pe.wait_ge(half_lo, 2)
            first_products(0, 0, 0, 0)
            turn(0)
            first_products(0, 1, 1, 0)
            for e in range(EXPERTS):
                pe.wait_ge(half_lo, 4 * e + 4)

                def step(lin, c, u, pair):
                    if expert_of(e, c, 1) is not None:
                        turn(lin + 1)
                    if begins(c, 2) and e + 1 < EXPERTS:
                        pe.wait_ge(half_lo, 4 * e + 6)
                    if expert_of(e, c, 2) is not None:
                        first_products(expert_of(e, c, 2), lin + 2, u, pair + 1)
                    second_products(e, lin, u)
                steps(pe, e, step)

        @block.scalar
        def _(act):
            act.wait_ge(cols_in, 32)
            act.wait_ge(eps_made, 1)
            relu_banks.give_credit(act)
            u1_ready.give_credit(act)
            u2_ready.give_credit(act)

            def half_high(e, half, src, loaded, value):
                act.wait_ge(loaded, value)
                if e >= 2:
                    act.wait_ge(m2.sem, m2.at((e - 1) * CHUNKS, 0))
                nc.scalar.activation(half_slot(w_hi, e, half), src[:, :, :], ACT.Copy).then_inc(half_hi, 1)

            def normalise(lin, n, src, dst, norm, ready):
                act.wait_ge(norm.sem, norm.at(lin, 2))
                nc.scalar.activation(root[:, n, :], mean_var[:, n, :, 1], ACT.Sqrt, bias=eps[:, 0:1]).then_inc(rooted[n].sem, 1)
                act.wait_ge(norm.sem, norm.at(lin, 4))
                for t in range(TT):
                    nc.scalar.activation(dst[:, t], src[:, t], ACT.Identity, scale=rstd[:, n, t:t + 1],
                                         bias=neg_mean[:, n, t:t + 1]).then_inc(ready.sem, 1)

            def normalise_first(lin):
                act.wait_ge(turned_ready.sem, turned_ready.at(lin, 0))
                normalise(lin, 0, t1, u1, norm1, u1_ready)

            def rectify(e, lin, u):
                act.wait_ge(lo_ready.sem, lo_ready.at(lin, 0))
                for k in range(KT):
                    if k % 2 == 0:
                        act.wait_ge(turned_ready.sem, turned_ready.at(lin, k // 2 + 1))
                    ins = nc.scalar.activation(relu[:, k, :], turned[k // 2][:, k % 2, :], ACT.Relu,
                                               scale=cols[:, 0, e, k:k + 1], bias=cols[:, 1, e, k:k + 1])
                    if k % 2:
                        ins.then_inc(relu_banks.sem, 1)
                act.wait_ge(relu_banks.sem, relu_banks.at(lin, 2))
                act.wait_ge(m2.sem, m2.at(lin, -TT))
                nc.scalar.activation(ht_hi[:, u], relu[:, :, :], ACT.Copy).then_inc(hi_ready.sem, 1)

            half_high(0, 0, first_raw[0], first_in[0], 16)
            half_high(0, 1, first_raw[1], first_in[1], 16)
            normalise_first(0)
            rectify(0, 0, 0)
            half_high(0, 2, first_raw[2], first_in[2], 16)
            half_high(0, 3, first_raw[3], first_in[3], 16)
            normalise_first(1)
            rectify(0, 1, 1)
            normalise_first(2)
            for e in range(EXPERTS):
                def step(lin, c, u, pair):
                    half = half_of(e, c)
                    if half is not None:
                        act.wait_ge(half_lo, 4 * (e + 1) + half)
                        act.dma_start(raw[:, :, :], half_rows(e + 1, half)).then_inc(half_in, 16)
                    if expert_of(e, c, 2) is not None:
                        rectify(expert_of(e, c, 2), lin + 2, u)
                    act.wait_ge(g2_done.sem, g2_done.at(lin, 0))
                    normalise(lin, 1, t2, u2, norm2, u2_ready)
                    if expert_of(e, c, 3) is not None:
                        normalise_first(lin + 3)
                    if half is not None:
                        half_high(e + 1, half, raw, half_in, 16 * (4 * e + half + 1))
                steps(act, e, step)

        @block.vector
        def _(dve):
            nc.vector.memset(eps[:, :], EPS).then_inc(eps_made, 1)
            b1_added.give_credit(dve)
            b2_added.give_credit(dve)
            lo_ready.give_credit(dve)
            added.give_credit(dve)

            def half_low(e, half, src):
                dve.wait_ge(half_hi, 4 * e + half + 1)
                nc.vector.tensor_tensor(half_slot(w_lo, e, half), src[:, :, :], half_slot(w_hi, e, half).bitcast(F32),
                                        ALU.subtract).then_inc(half_lo, 1)

            def moments(lin, n, acc, row, t_sb, done, added_row, norm):
                for t in range(TT):
                    dve.wait_ge(done.sem, done.at(lin, t + 1))
                    nc.vector.tensor_tensor(t_sb[:, t], acc[t][:, :], row, ALU.add).then_inc(added_row.sem, 1)
                for t in range(TT):
                    dve.wait_ge(added_row.sem, added_row.at(lin, t + 1))
                    last = nc.vector.bn_stats(stats[:, n, t, :], t_sb[:, t])
                last.then_inc(norm.sem, 1)
                dve.wait_ge(norm.sem, norm.at(lin, 1))
                dve.sem_inc(waited.sem, 1)
                for t in range(TT):
                    last = nc.vector.bn_aggr(mean_var[:, n, t, :], stats[:, n, t, :])
                last.then_inc(norm.sem, 1)
                dve.wait_ge(norm.sem, norm.at(lin, 2))

            def scales(lin, n, norm):
                dve.wait_ge(rooted[n].sem, rooted[n].at(lin, 1))
                nc.vector.reciprocal(rstd[:, n, :], root[:, n, :]).then_inc(norm.sem, 1)
                dve.wait_ge(norm.sem, norm.at(lin, 3))
                nc.vector.scalar_tensor_tensor(neg_mean[:, n, :], mean_var[:, n, :, 0], -1.0, rstd[:, n, :],
                                               ALU.mult, ALU.mult).then_inc(norm.sem, 1)

            def moments_first(e, lin):
                dve.wait_ge(u1_ready.sem, u1_ready.at(lin, 0))
                moments(lin, 0, acc1, rows[:, e % 2, 0], t1, m1, b1_added, norm1)

            def moments_second(e, lin):
                dve.wait_ge(u2_ready.sem, u2_ready.at(lin, 0))
                moments(lin, 1, acc2, rows[:, e % 2, 1], t2, m2, b2_added, norm2)

            def split_low(lin, u):
                dve.wait_ge(hi_ready.sem, hi_ready.at(lin, 1))
                nc.vector.tensor_tensor(ht_lo[:, u], relu[:, :, :], ht_hi[:, u].bitcast(F32),
                                        ALU.subtract).then_inc(lo_ready.sem, 1)

            half_low(0, 0, first_raw[0])
            half_low(0, 1, first_raw[1])
            dve.wait_ge(rows_in[0], 64)
            moments_first(0, 0)
            scales(0, 0, norm1)
            split_low(0, 0)
            half_low(0, 2, first_raw[2])
            half_low(0, 3, first_raw[3])
            moments_first(0, 1)
            scales(1, 0, norm1)
            split_low(1, 1)
            moments_first(0, 2)
            scales(2, 0, norm1)
            moments_second(0, 0)
            for e in range(EXPERTS):
                def step(lin, c, u, pair):
                    if expert_of(e, c, 2) is not None:
                        split_low(lin + 2, u)
                    scales(lin, 1, norm2)
                    if begins(c, 3) and e + 1 < EXPERTS:
                        dve.wait_ge(rows_in[(e + 1) % 2], 64 * ((e + 1) // 2 + 1))
                    if expert_of(e, c, 3) is not None:
                        moments_first(expert_of(e, c, 3), lin + 3)
                        scales(lin + 3, 0, norm1)
                    if expert_of(e, c, 1) is not None:
                        moments_second(expert_of(e, c, 1), lin + 1)
                    for t in range(TT):
                        dve.wait_ge(v2_ready.sem, v2_ready.at(lin, t + 1))
                        tile = base[:, bass.ds(c * TT + t, 1), :].rearrange("p o d -> p (o d)")
                        gate = gates[:, bass.ds(c * TT + t, 1), e:e + 1].rearrange("p o d -> p (o d)")
                        nc.vector.scalar_tensor_tensor(tile, v2[:, t], gate, tile, ALU.mult, ALU.add).then_inc(added.sem, 1)
                    if half_of(e, c) is not None:
                        half_low(e + 1, half_of(e, c), raw)
                steps(dve, e, step)


def in_phase(nc, phase, *args):
    with nc.cleanup_on_exit():
        phase(nc, *args)


def build_decoder(nc, a, out):
    tokens = BATCH * SEQ
    dram = lambda n, shape, dt=F32: nc.dram_tensor(n, shape, dt).ap()
    x = a["x"].rearrange("b s d -> (b s) d")
    ctx_in = a["ctx_1024"].rearrange("b s d -> (b s) d")
    out_rows = out.rearrange("b s d -> (b s) d")
    BG = BATCH * HG
    scale = DK ** -0.5
    with ExitStack() as ctx:
        ident = ctx.enter_context(nc.sbuf_tensor("ident", [P, P], F32))
        ident_b = ctx.enter_context(nc.sbuf_tensor("ident_b", [P, P], BF16))
        mask = ctx.enter_context(nc.sbuf_tensor("mask", [P, P], BF16))
        neg_half = ctx.enter_context(nc.sbuf_tensor("neg_half", [P, TPC], F32))
        in_phase(nc, build_constants, ident, ident_b, mask, neg_half)

        q1 = [dram(f"q1_{n}", (BG, P, SEQ)) for n in ("hi", "lo")]
        k1 = [dram(f"k1_{n}", (BG, P, SEQ)) for n in ("hi", "lo")]
        v1 = dram("v1", (BG, SEQ, P), F32)
        attn1 = dram("attn1", (BG, P, SEQ), F32)
        x1 = dram("x1", (tokens, D), F32)
        q2 = [dram(f"q2_{n}", (BG, P, SEQ)) for n in ("hi", "lo")]
        k2 = [dram(f"k2_{n}", (BG, P, CTX)) for n in ("hi", "lo")]
        v2 = dram("v2", (BG, CTX, P), F32)
        attn2 = dram("attn2", (BG, P, SEQ), F32)
        x2 = dram("x2", (tokens, D), F32)
        y = [dram(f"y_{n}", (KT, P, tokens)) for n in ("hi", "lo")]

        in_phase(nc, project, "qkv1", x, 2, True,
                [(a["L0_attn_q_heads"], True), (a["L0_attn_k_heads"], True), (a["L0_attn_v_heads"], True)],
                [("T", q1[0], q1[1], scale), ("T", k1[0], k1[1], 1.0), ("N", v1)], ident, neg_half)
        in_phase(nc, attend, "self", q1, k1, v1, attn1, SEQ, True, ident, ident_b, mask)
        in_phase(nc, project_out, "out1", attn1, (a["L0_attn_output_proj"], True), None, x, x1, ident)
        in_phase(nc, project, "q2", x1, 2, True, [(a["L0_xattn_W_q"], False)], [("T", q2[0], q2[1], scale)], ident, neg_half)
        in_phase(nc, project, "kv2", ctx_in, 4, False, [(a["L0_xattn_W_k"], False), (a["L0_xattn_W_v"], False)],
                [("T", k2[0], k2[1], 1.0), ("N", v2)], ident, neg_half)
        in_phase(nc, attend, "cross", q2, k2, v2, attn2, CTX, False, ident, ident_b, mask)
        in_phase(nc, project_out, "out2", attn2, (a["L0_xattn_W_o"], False), a["L0_xattn_b_o"], x1, x2, ident)
        base = ctx.enter_context(nc.sbuf_tensor("base", [P, tokens // P, D], F32))
        gates = ctx.enter_context(nc.sbuf_tensor("gates", [P, tokens // P, EXPERTS], F32))
        in_phase(nc, route, "route", x2, a["L0_ffn_gate_W"], a["L0_ffn_gate_b"], y[0], y[1], base, gates, ident, neg_half)
        in_phase(nc, experts, a["L0_ffn_W1"], a["L0_ffn_W2"], [a["L0_ffn_" + n] for n in ("b1", "g1", "be1", "b2", "g2", "be2")],
                y[0], y[1], base, gates, out_rows, ident)


_INS = ["x", "ctx_1024", "L0_attn_q_heads", "L0_attn_k_heads", "L0_attn_v_heads", "L0_attn_output_proj",
        "L0_xattn_W_q", "L0_xattn_W_k", "L0_xattn_W_v", "L0_xattn_W_o", "L0_xattn_b_o",
        "L0_ffn_gate_W", "L0_ffn_gate_b", "L0_ffn_W1", "L0_ffn_b1", "L0_ffn_g1", "L0_ffn_be1",
        "L0_ffn_W2", "L0_ffn_b2", "L0_ffn_g2", "L0_ffn_be2"]


def kernel(**inputs):
    import concourse.bacc as bacc
    from concourse.bass_utils import run_bass_kernel_spmd

    nc = bacc.Bacc("TRN2", target_bir_lowering=False, num_devices=1)
    arrays, args = {}, {}
    for name in _INS:
        arr = np.ascontiguousarray(inputs[name])
        arrays[f"in_{name}"] = arr
        args[name] = nc.dram_tensor(f"in_{name}", arr.shape, mybir.dt.from_np(arr.dtype), kind="ExternalInput").ap()
    out = nc.dram_tensor("out", (BATCH, SEQ, D), F32, kind="ExternalOutput").ap()
    build_decoder(nc, args, out)
    return run_bass_kernel_spmd(nc, [arrays], core_ids=[0]).results[0]["out"]
```
